# Optimizing a Trainium2 kernel written in Bass

```python
import numpy as np
import jax
import jax.numpy as jnp

def _softmax(x, axis=-1):
    return jax.nn.softmax(x, axis=axis)

def _gelu(x):
    return jax.nn.gelu(x, approximate=True)

def _silu(x):
    return jax.nn.silu(x)

def _sigmoid(x):
    return jax.nn.sigmoid(x)

def _layernorm(x, axis=-1, eps=1e-05):
    m = jnp.mean(x, axis=axis, keepdims=True)
    v = jnp.var(x, axis=axis, keepdims=True)
    return (x - m) / jnp.sqrt(v + eps)

def _scatter_add(tgt, idx, src, axis=0):
    return tgt.at[idx].add(src)

def _segment_sum(src, seg, n):
    return jax.ops.segment_sum(src, seg, n)
kernel_name = 'mk_macaron_d2_jaxref_r8_cb1164'

def setup_inputs(seed: int=0):
    np.random.seed(seed)
    _w = jnp.asarray

    def _L0_attn_setup():
        import jax, jax.numpy as jnp
        import numpy as np
        B, S, D = (2, 128, 512)
        H, KVH, HD = (32, 8, 128)
        GROUPS = H // KVH
        LAT, LH = (128, 32)
        THETA = 10000.0
        SCALE = 1.0 / float(np.sqrt(HD))

        def _rope_cos_sin(seq_len, head_dim, theta):
            inv_freq = 1.0 / theta ** (jnp.arange(0, head_dim, 2, dtype=jnp.float32) / head_dim)
            t = jnp.arange(seq_len, dtype=jnp.float32)
            freqs = jnp.outer(t, inv_freq)
            emb = jnp.concatenate([freqs, freqs], axis=-1)
            return (jnp.cos(emb), jnp.sin(emb))

        def _rotate_half(x):
            h = x.shape[-1] // 2
            return jnp.concatenate([-x[..., h:], x[..., :h]], axis=-1)

        def _apply_rope(x, cos, sin):
            return x * cos[None, None] + _rotate_half(x) * sin[None, None]

        def _causal_attn(q, k, v, scale):
            s = jnp.einsum('bhqd,bhkd->bhqk', q, k) * scale
            mask = jnp.tril(jnp.ones((q.shape[2], k.shape[2]), dtype=bool))
            s = jnp.where(mask[None, None], s, jnp.finfo(s.dtype).min)
            p = jax.nn.softmax(s, axis=-1)
            return jnp.einsum('bhqk,bhkd->bhqd', p, v)
        key = jax.random.key(seed)
        ks = jax.random.split(key, 9)
        sd = 0.02
        mk = lambda k, shape: jax.random.normal(k, shape, dtype=jnp.float32) * sd
        return {'hidden_states': jax.random.normal(ks[0], (B, S, D), dtype=jnp.float32), 'w_q': mk(ks[1], (D, H * HD)), 'w_k': mk(ks[2], (D, KVH * HD)), 'w_v': mk(ks[3], (D, KVH * HD)), 'w_o': mk(ks[4], (H * HD, D)), 'w_lq': mk(ks[5], (D, LAT)), 'w_lk': mk(ks[6], (LAT, LH * HD)), 'w_lv': mk(ks[7], (D, LH * HD)), 'w_lo': mk(ks[8], (LH * HD, D))}
    _L0_attn_in = _L0_attn_setup()

    def _L0_ffn_setup():
        import jax, jax.numpy as jnp
        import numpy as np
        M = 512
        K = 512

        def _make_2to4_mask(key, shape):
            scores = jax.random.normal(key, shape)
            g = scores.reshape(shape[0], shape[1] // 4, 4)
            rank = jnp.argsort(jnp.argsort(-jnp.abs(g), axis=-1), axis=-1)
            return (rank < 2).reshape(shape).astype(jnp.float32)
        key = jax.random.key(seed)
        k_x, k_w12, k_b12, k_w3, k_b3, k_m = jax.random.split(key, 6)
        x = jax.random.normal(k_x, (4, 256, K), dtype=jnp.float32)
        w12_dense = jax.random.normal(k_w12, (2 * M, K), dtype=jnp.float32) * (1.0 / np.sqrt(K))
        mask12 = _make_2to4_mask(k_m, (2 * M, K))
        w12 = w12_dense * mask12
        b12 = jax.random.normal(k_b12, (2 * M,), dtype=jnp.float32) * 0.01
        w3 = jax.random.normal(k_w3, (M, M), dtype=jnp.float32) * (1.0 / np.sqrt(M))
        b3 = jax.random.normal(k_b3, (M,), dtype=jnp.float32) * 0.01
        return {'x': x, 'w12': w12, 'b12': b12, 'w3': w3, 'b3': b3}
    _L0_ffn_in = _L0_ffn_setup()

    def _L1_attn_setup():
        import jax, jax.numpy as jnp
        import numpy as np
        B, S, E, H = (2, 256, 512, 32)
        D = E // H
        ROPE_BASE = 10000.0
        MASK_VAL = -66504.0

        def _rope(x, cos, sin):
            x1, x2 = jnp.split(x, 2, axis=-1)
            return jnp.concatenate([x1 * cos - x2 * sin, x2 * cos + x1 * sin], axis=-1)
        key = jax.random.key(seed)
        k1, k2, k3, k4, k5 = jax.random.split(key, 5)
        return {'hidden_states': jax.random.normal(k1, (B, S, E), dtype=jnp.float32), 'qkv_w': jax.random.normal(k2, (E, 3 * E), dtype=jnp.float32) * 0.02, 'qkv_b': jax.random.normal(k3, (3 * E,), dtype=jnp.float32) * 0.02, 'out_w': jax.random.normal(k4, (E, E), dtype=jnp.float32) * 0.02, 'out_b': jax.random.normal(k5, (E,), dtype=jnp.float32) * 0.02}
    _L1_attn_in = _L1_attn_setup()

    def _L1_ffn_setup():
        import jax, jax.numpy as jnp
        import numpy as np
        HIDDEN = 512
        INTER = 1376
        RANK = 128
        B, S = (2, 256)
        key = jax.random.key(seed)
        ks = jax.random.split(key, 7)
        sc = 0.02
        return {'x': jax.random.normal(ks[0], (B, S, HIDDEN), dtype=jnp.float32), 'U1': jax.random.normal(ks[1], (HIDDEN, RANK), dtype=jnp.float32) * sc, 'V1': jax.random.normal(ks[2], (RANK, 2 * INTER), dtype=jnp.float32) * sc, 'U2': jax.random.normal(ks[3], (INTER, RANK), dtype=jnp.float32) * sc, 'V2': jax.random.normal(ks[4], (RANK, HIDDEN), dtype=jnp.float32) * sc, 'b1': jax.random.normal(ks[5], (2 * INTER,), dtype=jnp.float32) * sc, 'b2': jax.random.normal(ks[6], (HIDDEN,), dtype=jnp.float32) * sc}
    _L1_ffn_in = _L1_ffn_setup()
    _d = {'L0_attn_hidden_states': _L0_attn_in['hidden_states'], 'L0_attn_w_q': _L0_attn_in['w_q'], 'L0_attn_w_k': _L0_attn_in['w_k'], 'L0_attn_w_v': _L0_attn_in['w_v'], 'L0_attn_w_o': _L0_attn_in['w_o'], 'L0_attn_w_lq': _L0_attn_in['w_lq'], 'L0_attn_w_lk': _L0_attn_in['w_lk'], 'L0_attn_w_lv': _L0_attn_in['w_lv'], 'L0_attn_w_lo': _L0_attn_in['w_lo'], 'L0_ffn_w12': _L0_ffn_in['w12'], 'L0_ffn_b12': _L0_ffn_in['b12'], 'L0_ffn_w3': _L0_ffn_in['w3'], 'L0_ffn_b3': _L0_ffn_in['b3'], 'L1_attn_qkv_w': _L1_attn_in['qkv_w'], 'L1_attn_qkv_b': _L1_attn_in['qkv_b'], 'L1_attn_out_w': _L1_attn_in['out_w'], 'L1_attn_out_b': _L1_attn_in['out_b'], 'L1_ffn_U1': _L1_ffn_in['U1'], 'L1_ffn_V1': _L1_ffn_in['V1'], 'L1_ffn_U2': _L1_ffn_in['U2'], 'L1_ffn_V2': _L1_ffn_in['V2'], 'L1_ffn_b1': _L1_ffn_in['b1'], 'L1_ffn_b2': _L1_ffn_in['b2']}
    _x0 = _d['L0_attn_hidden_states']
    _d['L0_attn_hidden_states'] = jax.random.normal(jax.random.fold_in(jax.random.key(seed), 1), (4, 256, 512), dtype=_x0.dtype)
    del _x0
    return _d

def reference(L0_attn_hidden_states, L0_attn_w_q, L0_attn_w_k, L0_attn_w_v, L0_attn_w_o, L0_attn_w_lq, L0_attn_w_lk, L0_attn_w_lv, L0_attn_w_lo, L0_ffn_w12, L0_ffn_b12, L0_ffn_w3, L0_ffn_b3, L1_attn_qkv_w, L1_attn_qkv_b, L1_attn_out_w, L1_attn_out_b, L1_ffn_U1, L1_ffn_V1, L1_ffn_U2, L1_ffn_V2, L1_ffn_b1, L1_ffn_b2):

    def _L0_attn_ref(hidden_states, w_q, w_k, w_v, w_o, w_lq, w_lk, w_lv, w_lo):
        import jax, jax.numpy as jnp
        import numpy as np
        B, S, D = (2, 128, 512)
        H, KVH, HD = (32, 8, 128)
        GROUPS = H // KVH
        LAT, LH = (128, 32)
        THETA = 10000.0
        SCALE = 1.0 / float(np.sqrt(HD))

        def _rope_cos_sin(seq_len, head_dim, theta):
            inv_freq = 1.0 / theta ** (jnp.arange(0, head_dim, 2, dtype=jnp.float32) / head_dim)
            t = jnp.arange(seq_len, dtype=jnp.float32)
            freqs = jnp.outer(t, inv_freq)
            emb = jnp.concatenate([freqs, freqs], axis=-1)
            return (jnp.cos(emb), jnp.sin(emb))

        def _rotate_half(x):
            h = x.shape[-1] // 2
            return jnp.concatenate([-x[..., h:], x[..., :h]], axis=-1)

        def _apply_rope(x, cos, sin):
            return x * cos[None, None] + _rotate_half(x) * sin[None, None]

        def _causal_attn(q, k, v, scale):
            s = jnp.einsum('bhqd,bhkd->bhqk', q, k) * scale
            mask = jnp.tril(jnp.ones((q.shape[2], k.shape[2]), dtype=bool))
            s = jnp.where(mask[None, None], s, jnp.finfo(s.dtype).min)
            p = jax.nn.softmax(s, axis=-1)
            return jnp.einsum('bhqk,bhkd->bhqd', p, v)
        x = hidden_states
        bsz, q_len, _ = x.shape
        q = (x @ w_q).reshape(bsz, q_len, H, HD).transpose(0, 2, 1, 3)
        k = (x @ w_k).reshape(bsz, q_len, KVH, HD).transpose(0, 2, 1, 3)
        v = (x @ w_v).reshape(bsz, q_len, KVH, HD).transpose(0, 2, 1, 3)
        lq = x @ w_lq
        lk = (lq @ w_lk).reshape(bsz, q_len, LH, HD).transpose(0, 2, 1, 3)
        lv = (x @ w_lv).reshape(bsz, q_len, LH, HD).transpose(0, 2, 1, 3)
        cos, sin = _rope_cos_sin(q_len, HD, THETA)
        q = _apply_rope(q, cos, sin)
        k = _apply_rope(k, cos, sin)
        lk = _apply_rope(lk, cos, sin)
        k = jnp.repeat(k, GROUPS, axis=1)
        v = jnp.repeat(v, GROUPS, axis=1)
        attn = _causal_attn(q, k, v, SCALE)
        lat = _causal_attn(q, lk, lv, SCALE)
        attn = attn.transpose(0, 2, 1, 3).reshape(bsz, q_len, H * HD)
        lat = lat.transpose(0, 2, 1, 3).reshape(bsz, q_len, LH * HD)
        return attn @ w_o + lat @ w_lo

    def _L0_ffn_ref(x, w12, b12, w3, b3):
        import jax, jax.numpy as jnp
        import numpy as np
        M = 512
        K = 512

        def _make_2to4_mask(key, shape):
            scores = jax.random.normal(key, shape)
            g = scores.reshape(shape[0], shape[1] // 4, 4)
            rank = jnp.argsort(jnp.argsort(-jnp.abs(g), axis=-1), axis=-1)
            return (rank < 2).reshape(shape).astype(jnp.float32)
        x12 = jnp.einsum('bsk,mk->bsm', x, w12) + b12
        x1, x2 = jnp.split(x12, 2, axis=-1)
        x4 = jax.nn.silu(x1) * x2
        return jnp.einsum('bsm,nm->bsn', x4, w3) + b3

    def _L1_attn_ref(hidden_states, qkv_w, qkv_b, out_w, out_b):
        import jax, jax.numpy as jnp
        import numpy as np
        B, S, E, H = (2, 256, 512, 32)
        D = E // H
        ROPE_BASE = 10000.0
        MASK_VAL = -66504.0

        def _rope(x, cos, sin):
            x1, x2 = jnp.split(x, 2, axis=-1)
            return jnp.concatenate([x1 * cos - x2 * sin, x2 * cos + x1 * sin], axis=-1)
        b, s, e = hidden_states.shape
        qkv = hidden_states @ qkv_w + qkv_b
        q, k, v = jnp.split(qkv, 3, axis=-1)
        q = q.reshape(b, s, H, D)
        k = k.reshape(b, s, H, D)
        v = v.reshape(b, s, H, D)
        half = D // 2
        inv_freq = 1.0 / ROPE_BASE ** (jnp.arange(0, half, dtype=jnp.float32) / half)
        ang = jnp.arange(s, dtype=jnp.float32)[:, None] * inv_freq[None, :]
        cos = jnp.cos(ang)[None, :, None, :]
        sin = jnp.sin(ang)[None, :, None, :]
        q = _rope(q, cos, sin)
        k = _rope(k, cos, sin)
        scale = 1.0 / jnp.sqrt(jnp.asarray(D, dtype=hidden_states.dtype))
        scores = jnp.einsum('bqhd,bkhd->bhqk', q, k) * scale
        causal = jnp.tril(jnp.ones((s, s), dtype=scores.dtype))
        scores = scores + (1.0 - causal) * MASK_VAL
        probs = jax.nn.softmax(scores, axis=-1)
        ctx = jnp.einsum('bhqk,bkhd->bqhd', probs, v).reshape(b, s, e)
        return ctx @ out_w + out_b

    def _L1_ffn_ref(x, U1, V1, U2, V2, b1, b2):
        import jax, jax.numpy as jnp
        import numpy as np
        HIDDEN = 512
        INTER = 1376
        RANK = 128
        B, S = (2, 256)
        P = jnp.einsum('bsh,hr->bsr', x, U1)
        H = jnp.einsum('bsr,rf->bsf', P, V1) + b1
        gate, up = (H[..., :INTER], H[..., INTER:])
        act = jax.nn.silu(gate) * up
        Z = jnp.einsum('bsi,ir->bsr', act, U2)
        out = jnp.einsum('bsr,rh->bsh', Z, V2) + b2
        return out
    x = L0_attn_hidden_states
    x = x + 0.5 * _L0_ffn_ref(_layernorm(x, axis=-1), L0_ffn_w12, L0_ffn_b12, L0_ffn_w3, L0_ffn_b3)
    x = x + _L0_attn_ref(_layernorm(x, axis=-1), L0_attn_w_q, L0_attn_w_k, L0_attn_w_v, L0_attn_w_o, L0_attn_w_lq, L0_attn_w_lk, L0_attn_w_lv, L0_attn_w_lo)
    x = x + 0.5 * _L0_ffn_ref(_layernorm(x, axis=-1), L0_ffn_w12, L0_ffn_b12, L0_ffn_w3, L0_ffn_b3)
    x = x + 0.5 * _L1_ffn_ref(_layernorm(x, axis=-1), L1_ffn_U1, L1_ffn_V1, L1_ffn_U2, L1_ffn_V2, L1_ffn_b1, L1_ffn_b2)
    x = x + _L1_attn_ref(_layernorm(x, axis=-1), L1_attn_qkv_w, L1_attn_qkv_b, L1_attn_out_w, L1_attn_out_b)
    x = x + 0.5 * _L1_ffn_ref(_layernorm(x, axis=-1), L1_ffn_U1, L1_ffn_V1, L1_ffn_U2, L1_ffn_V2, L1_ffn_b1, L1_ffn_b2)
    return x

_drawn_inputs = setup_inputs


def setup_inputs(seed=0):
    import zlib

    import numpy as np

    out = dict(_drawn_inputs(seed))
    spreads = {}
    factors = {'L0_attn_w_q': 3.59,
     'L0_attn_w_k': 3.68,
     'L0_attn_w_lq': 8.0,
     'L0_attn_w_lk': 8.0,
     'L0_ffn_b12': 8.0,
     'L0_ffn_b3': 5.642,
     'L1_attn_qkv_b': 54.528,
     'L1_attn_out_b': 200.0,
     'L1_ffn_U1': 8.0,
     'L1_ffn_V1': 8.0,
     'L1_ffn_U2': 8.0,
     'L1_ffn_V2': 8.0,
     'L1_ffn_b1': 8.0,
     'L1_ffn_b2': 190.4,
     'L1_attn_qkv_w': 8.0,
     'L1_attn_out_w': 8.0}
    for name, (base, spread) in spreads.items():
        noise = np.random.default_rng([zlib.crc32(name.encode()), seed]).standard_normal(out[name].shape)
        drawn = base * np.exp(spread * noise) if base else spread * noise
        out[name] = jnp.asarray(drawn.astype(out[name].dtype))
    for name, factor in factors.items():
        out[name] = (out[name] * factor).astype(out[name].dtype)
    return out
```

```python
from contextlib import ExitStack

import numpy as np

import concourse.bass as bass
from concourse import mybir

F32 = mybir.dt.float32
F32R = mybir.dt.float32r
ALU = mybir.AluOpType
ACT = mybir.ActivationFunctionType

P = 128
BATCH, SEQ, DIM = 4, 256, 512
TOKENS = BATCH * SEQ
TILES = TOKENS // P
KC = DIM // P
CH = 512
HI, LO = 0, 1
PASSES = ((HI, HI), (HI, LO), (LO, HI))
EPS = 1e-5

HEADS0, KVH, HD = 32, 8, 128
GH = HEADS0 // KVH
G_CHUNKS = 19
C_K, C_Q, C_LK, C_LVV, C_WO, C_WLO = 0, 1, 5, 6, 11, 15
EARLY = [0, 6, 7, 8, 9, 10, 1, 2, 3, 4, 5]
LATE = list(range(11, 19))
EARLY_AT = {0: EARLY[0:3], 1: EARLY[3:6], 2: EARLY[6:8], 3: EARLY[8:11]}
LATE_AT = {h: LATE[2 * h:2 * h + 2] for h in range(4)}
LVW = GH * HD + HD
HALF = LVW // 2

M0 = 4
INTER = 1376
M1 = -(-INTER // P)
F0_CHUNKS = (KC * 2 * M0 * P + M0 * DIM) // CH
F1_COLS = KC * P + 2 * M1 * P + M1 * P + DIM
F1_CHUNKS = -(-F1_COLS // CH)

HEADS1, D1 = 32, 16
GR1, HG1 = 4, 8
A1_CHUNKS = (KC * 3 * DIM + KC * DIM) // CH

W_F0A = 0
W_LQ = W_F0A + F0_CHUNKS
W_A0 = W_LQ + 1
W_F0B = W_A0 + KVH * G_CHUNKS
W_F1 = W_F0B + F0_CHUNKS
W_A1 = W_F1 + F1_CHUNKS
W_ALL = W_A1 + A1_CHUNKS

T_ID = 0
T_M0 = T_ID + P
T_M1 = T_M0 + 3 * P
T_COS = T_M1 + 3 * P
T_SIN = T_COS + 2 * SEQ
T_R1 = T_SIN + 2 * SEQ
T_EO = T_R1 + 4 * 2 * D1
T_MH = T_EO + 2
T_ALL = T_MH + 2

B_12 = 0
B_1 = B_12 + 2 * M0
B_ALL = B_1 + 2 * M1
RAW = 4


def constants():
    t = np.zeros((P, T_ALL), np.float32)
    t[:, T_ID:T_ID + P] = np.eye(P, dtype=np.float32)
    future = (np.arange(P)[None, :] > np.arange(P)[:, None]).astype(np.float32)
    for at, value in ((T_M0, 1e30), (T_M1, 66504.0)):
        t[:, at:at + P] = future * np.float32(value)
        t[:, at + 2 * P:at + 3 * P] = future * np.float32(value)
    inv = (1.0 / np.float32(10000.0) ** (np.arange(0, HD, 2, dtype=np.float32) / np.float32(HD))).astype(np.float32)
    ang = np.outer(np.arange(SEQ, dtype=np.float32), inv).astype(np.float32)
    cos = np.concatenate([np.cos(ang), np.cos(ang)], 1).T
    sin = np.concatenate([-np.sin(ang), np.sin(ang)], 1).T
    scale = np.float32(-1.0 / np.sqrt(HD))
    t[:, T_COS:T_COS + SEQ] = cos * scale
    t[:, T_COS + SEQ:T_COS + 2 * SEQ] = cos
    t[:, T_SIN:T_SIN + SEQ] = sin * scale
    t[:, T_SIN + SEQ:T_SIN + 2 * SEQ] = sin
    half = D1 // 2
    inv = (1.0 / np.float32(10000.0) ** (np.arange(0, half, dtype=np.float32) / np.float32(half))).astype(np.float32)
    ang = (np.arange(SEQ, dtype=np.float32)[:, None] * inv[None, :]).astype(np.float32)
    c1 = np.concatenate([np.cos(ang), np.cos(ang)], 1).reshape(2, P, D1).transpose(1, 0, 2)
    s1 = np.concatenate([-np.sin(ang), np.sin(ang)], 1).reshape(2, P, D1).transpose(1, 0, 2)
    t[:, T_R1:T_R1 + 8 * D1] = np.stack([c1 * np.float32(-0.25), s1 * np.float32(-0.25), c1, s1], 1).reshape(P, 8 * D1)
    t[:, T_EO] = (np.arange(P) % 32 < D1)
    t[:, T_EO + 1] = (np.arange(P) % 32 >= D1)
    t[:, T_MH:T_MH + 2] = -0.5
    return t


def program(nc, x_in, w_in, table_in, bias_in, rows_in, out):
    ctx = ExitStack()
    with ctx:
        def sem(name):
            return ctx.enter_context(nc.semaphore(name))

        def sb(scope, name, shape, dt=F32):
            return scope.enter_context(nc.sbuf_tensor(name, shape, dt))

        x = sb(ctx, "x", [P, TILES, DIM])
        table = sb(ctx, "table", [P, T_ALL])
        biases = sb(ctx, "biases", [P, B_ALL])
        row = sb(ctx, "row", [P, DIM])
        raw = sb(ctx, "raw", [P, RAW, CH])
        work = sb(ctx, "work", [P, 4, CH])
        stats = sb(ctx, "stats", [P, 2, 6])
        mean_var = sb(ctx, "mean_var", [P, 2, 2])
        var_eps = sb(ctx, "var_eps", [P, 2])
        rstd = sb(ctx, "rstd", [P, 2])
        neg_max = sb(ctx, "neg_max", [P, 2, 2])
        row_sum = sb(ctx, "row_sum", [P, 2, 2])
        inv_sum = sb(ctx, "inv_sum", [P, 2, 2])
        W = [sb(ctx, f"W{i}", [P, G_CHUNKS * CH], F32R) for i in (HI, LO)]
        with ExitStack() as a:
            xnT = [sb(a, f"xnT{i}", [P, KC, TOKENS], F32R) for i in (HI, LO)]
            with ExitStack() as s:
                WF0 = [sb(s, f"WF0_{i}", [P, F0_CHUNKS * CH], F32R) for i in (HI, LO)]
                h0 = [sb(s, f"h0_{i}", [P, 2, CH], F32R) for i in (HI, LO)]
            with ExitStack() as s:
                qlk = [sb(s, f"qlk{i}", [P, 2, 2 * SEQ], F32R) for i in (HI, LO)]
                kT = [sb(s, f"kT{i}", [P, SEQ], F32R) for i in (HI, LO)]
                lvv = [sb(s, f"lvv{i}", [P, 2, LVW], F32R) for i in (HI, LO)]
                pt0 = [sb(s, f"pt0_{i}", [P, 2, 4 * P], F32R) for i in (HI, LO)]
                oT0 = [sb(s, f"oT0_{i}", [P, 2 * GH, SEQ], F32R) for i in (HI, LO)]
                lqT = [sb(s, f"lqT{i}", [P, TOKENS], F32R) for i in (HI, LO)]
                s0 = sb(s, "s0", [P, 2, 3 * P])
            with ExitStack() as s:
                WF1 = [sb(s, f"WF1_{i}", [P, F1_CHUNKS * CH], F32R) for i in (HI, LO)]
                h1 = [sb(s, f"h1_{i}", [P, 2, CH], F32R) for i in (HI, LO)]
                pz = [sb(s, f"pz{i}", [P, CH], F32R) for i in (HI, LO)]
        with ExitStack() as a:
            xb = [sb(a, f"xb{i}", [P, KC, SEQ], F32R) for i in (HI, LO)]
            qE = [sb(a, f"qE{i}", [P, 2, 2, SEQ], F32R) for i in (HI, LO)]
            k1 = [sb(a, f"k1_{i}", [P, 2, SEQ], F32R) for i in (HI, LO)]
            vz = [sb(a, f"vz{i}", [P, 2, 2, HG1, P], F32R) for i in (HI, LO)]
            pt1 = [sb(a, f"pt1_{i}", [P, 2, 4 * P], F32R) for i in (HI, LO)]
            oT1 = [sb(a, f"oT1_{i}", [P, GR1, SEQ], F32R) for i in (HI, LO)]
            qkv = sb(a, "qkv", [P, 2, 3 * DIM])
            s1 = sb(a, "s1", [P, 2, 3 * P])
            bqkv = sb(a, "bqkv", [P, 3 * DIM])

        bank = [ctx.enter_context(nc.psum_tensor(f"bank{i}", [P, CH], F32)) for i in range(8)]
        ident = table[:, T_ID:T_ID + P]

        x_loaded = [sem(f"x_loaded{t}") for t in range(TILES)]
        table_loaded = sem("table_loaded")
        row_loaded = sem("row_loaded")
        bqkv_loaded = sem("bqkv_loaded")
        stored = sem("stored")
        x_written = sem("x_written")
        passed = sem("passed")

        raw_loaded = [sem(f"raw_loaded{i}") for i in range(RAW)]
        w_hi = sem("w_hi")
        w_split = sem("w_split")

        class Stream:

            used = [0] * RAW
            last = [None] * RAW
            done = 0

            def __init__(self, n, turns=1):
                self.n, self.turns, self.base, self.at = n, turns, Stream.done, []
                per = [len(range(s, n, RAW)) for s in range(RAW)]
                for j in range(n):
                    s = j % RAW
                    before = Stream.used[s] + j // RAW
                    if j >= RAW:
                        prev = Stream.done + j - RAW
                    elif turns > 1:
                        prev = Stream.done - n + max(range(s, n, RAW))
                        assert Stream.last[s] is not None and Stream.last[s] <= Stream.done
                        prev = max(prev, Stream.last[s])
                    else:
                        prev = Stream.last[s]
                    self.at.append((s, before, per[s], prev))
                for s in range(RAW):
                    if per[s]:
                        Stream.last[s] = Stream.done + n * (turns - 1) + max(range(s, n, RAW))
                    Stream.used[s] += per[s] * turns
                Stream.done += n * turns

            def load(self, sp, j, source, g=None):
                s, before, per, prev = self.at[j]
                turn = 0 if g is None else g
                if prev is not None:
                    sp.wait_ge(w_split, prev + 1 + turn * self.n)
                sp.dma_start(raw[:, s, :], source).then_inc(raw_loaded[s], 16)

            def split_hi(self, act, j, dst, g=None):
                s, before, per, _ = self.at[j]
                turn = 0 if g is None else g
                act.wait_ge(raw_loaded[s], 16 * (before + 1) + turn * (16 * per))
                nc.scalar.copy(dst[HI], raw[:, s, :]).then_inc(w_hi, 1)

            def split_lo(self, dve, j, dst, g=None):
                s = self.at[j][0]
                turn = 0 if g is None else g
                dve.wait_ge(w_hi, self.base + j + 1 + turn * self.n)
                nc.vector.tensor_tensor(dst[LO], raw[:, s, :], dst[HI].bitcast(F32),
                                        ALU.subtract).then_inc(w_split, 1)

            def ready(self, eng, j, g=None):
                turn = 0 if g is None else g
                eng.wait_ge(w_split, self.base + j + 1 + turn * self.n)

        def chunk(w, c):
            return [w[i][:, c * CH:(c + 1) * CH] for i in (HI, LO)]

        st_f0a = Stream(F0_CHUNKS)
        st_lq = Stream(1)
        st_a0 = Stream(len(EARLY))
        st_loop = Stream(G_CHUNKS, KVH)
        st_f0b = Stream(F0_CHUNKS - len(EARLY))
        st_f1a = Stream(F1_CHUNKS)
        st_a1 = Stream(A1_CHUNKS)
        st_f1b = Stream(F1_CHUNKS)

        ln_stat = sem("ln_stat")
        ln_var = sem("ln_var")
        ln_rstd = sem("ln_rstd")
        ln_xn = sem("ln_xn")
        ln_turned = sem("ln_turned")
        ln_hi = sem("ln_hi")
        ln_done = sem("ln_done")

        def at_least(eng, s, value):
            if not isinstance(value, int) or value > 0:
                eng.wait_ge(s, value)

        def ln_normalise(dve, n, slot, xt):
            nc.vector.bn_stats(stats[:, slot, :], xt).then_inc(ln_stat, 1)
            dve.wait_ge(ln_stat, n * 2 + 1)
            dve.sem_inc(passed, 1)
            nc.vector.bn_aggr(mean_var[:, slot, :], stats[:, slot, :]).then_inc(ln_stat, 1)
            dve.wait_ge(ln_stat, n * 2 + 2)
            nc.vector.tensor_scalar(var_eps[:, slot:slot + 1], mean_var[:, slot, 1:2], EPS, None,
                                    ALU.add).then_inc(ln_var, 1)
            dve.wait_ge(ln_rstd, n + 1)
            at_least(dve, ln_turned, n - 1)
            nc.vector.tensor_scalar(work[:, slot, :], xt, mean_var[:, slot, 0:1],
                                    rstd[:, slot:slot + 1], ALU.subtract, ALU.mult).then_inc(ln_xn, 1)

        def ln_power(pool, n, slot):
            pool.wait_ge(ln_var, n + 1)
            nc.gpsimd.tensor_tensor(rstd[:, slot:slot + 1], var_eps[:, slot:slot + 1],
                                    table[:, T_MH:T_MH + 1], ALU.pow).then_inc(ln_rstd, 1)

        def ln_turn(pe, n, slot, b):
            pe.wait_ge(ln_xn, n + 1)
            at_least(pe, ln_done, n)
            for c in range(KC):
                last = nc.tensor.transpose(bank[b][:, c * P:(c + 1) * P],
                                           work[:, slot, c * P:(c + 1) * P], ident)
            last.then_inc(ln_turned, 1)

        def turned(b):
            return bank[b][:, :].rearrange("p (c n) -> p c n", c=KC)

        def ln_hi_part(act, n, b, dst):
            act.wait_ge(ln_turned, n + 1)
            nc.scalar.copy(dst[HI], turned(b)).then_inc(ln_hi, 1)

        def ln_lo_part(dve, n, b, dst):
            dve.wait_ge(ln_hi, n + 1)
            nc.vector.tensor_tensor(dst[LO], turned(b), dst[HI].bitcast(F32),
                                    ALU.subtract).then_inc(ln_done, 1)

        def xnT_tile(t):
            return [xnT[i][:, :, t * P:(t + 1) * P] for i in (HI, LO)]

        def product(out_ap, lhs, rhs, start=True, stop=True):
            for k, (i, j) in enumerate(PASSES):
                last = nc.tensor.matmul(out_ap, lhs(i), rhs(j), start=start and k == 0,
                                        stop=stop and k == 2)
            return last

        f_ready = sem("f_ready")
        f_silu = sem("f_silu")
        f_mul = sem("f_mul")
        f_hi = sem("f_hi")
        f_lo = sem("f_lo")
        f_used = sem("f_used")
        f_out = sem("f_out")
        pz_ready = sem("pz_ready")
        pz_hi = sem("pz_hi")
        pz_lo = sem("pz_lo")
        RING, LNB, ZB = (0, 1, 2), 3, 4

        class FFN:

            m_all, o_all, u_all, z_all = 0, 0, 0, 0

            def __init__(self, layer, w, h, ln0, ln_next, x_before, row_n, first, own=(), beside=(),
                         needs=None):
                self.layer, self.w, self.h = layer, w, h
                self.M = M0 if layer == 0 else M1
                self.m0, self.o0, self.u0, self.z0 = FFN.m_all, FFN.o_all, FFN.u_all, FFN.z_all
                FFN.m_all += 2 * self.M
                FFN.o_all += TILES
                FFN.u_all += 2 * (self.M - 1)
                FFN.z_all += 4 if layer else 0
                self.out_banks = (4, 5, 6, 7) if layer == 0 else (5, 6, 7)
                self.ln0, self.ln_next, self.row_n, self.first = ln0, ln_next, row_n, first
                self.x_before = x_before
                self.needs = needs
                self.own = own
                self.beside = beside

            def gate_up(self, m, up, c):
                if self.layer == 0:
                    at = c * 2 * M0 * P + (up * M0 + m) * P
                else:
                    at = KC * P + (up * M1 + m) * P
                return lambda i: self.w[i][:, at:at + P]

            def down(self, m):
                if self.layer == 0:
                    at = KC * 2 * M0 * P + m * DIM
                    return lambda i: self.w[i][:, at:at + DIM]
                at = KC * P + 2 * M1 * P + m * P
                return lambda i: self.w[i][:, at:at + P]

            def bias(self, m, up):
                at = (B_12 + up * M0 + m) if self.layer == 0 else (B_1 + up * M1 + m)
                return biases[:, at:at + 1]

            def bank_of(self, o):
                return self.out_banks[(o - self.o0) % len(self.out_banks)]

            def ln_tiles(self, k, m):
                if m >= 4 or (k == 1 and self.ln_next is None):
                    return []
                return [(self.ln0 + 4 + m, 4 + m)] if k == 0 else [(self.ln_next + m, m)]

            def splits(self, k, m):
                at, per = k * self.M + m, -(-len(self.beside) // (2 * self.M))
                return self.beside[at * per:(at + 1) * per]

            def tensor(self, pe):
                M = self.M
                if self.first:
                    for t in range(4):
                        ln_turn(pe, self.ln0 + t, t % 2, LNB)
                at_least(pe, x_written, self.x_before)
                for k in range(2):
                    cols = slice(k * CH, k * CH + CH)
                    pe.wait_ge(ln_done, self.ln0 + 4 * k + 4)
                    if k == 0:
                        stream, j = self.needs or self.own[-1][:2]
                        stream.ready(pe, j)
                    z = self.z0 + 2 * k
                    if self.layer:
                        at_least(pe, pz_lo, z)
                        for c in range(KC):
                            last = product(bank[ZB][:, :], lambda i: self.w[i][:, c * P:(c + 1) * P],
                                           lambda i: xnT[i][:, c, cols], c == 0, c == KC - 1)
                        last.then_inc(pz_ready, 1)
                        pe.wait_ge(pz_lo, z + 1)
                    for m in range(M + 1):
                        if m < M:
                            self.tensor_gate_up(pe, k, m, cols)
                        if m > 0:
                            self.tensor_down(pe, k, m - 1)
                        if m < M:
                            for n, t in self.ln_tiles(k, m):
                                ln_turn(pe, n, t % 2, LNB)
                    if self.layer:
                        pe.wait_ge(pz_lo, z + 2)
                        for t in range(4):
                            o = 4 * k + t
                            if o >= 3:
                                pe.wait_ge(x_written, self.x_before + 2 * (o - 3) + 2)
                            at = F1_COLS - DIM
                            product(bank[self.bank_of(self.o0 + o)][:, :],
                                    lambda i: pz[i][:, t * P:(t + 1) * P],
                                    lambda i: self.w[i][:, at:at + DIM]).then_inc(f_out, 1)

            def tensor_gate_up(self, pe, k, m, cols):
                q = self.m0 + k * self.M + m
                for up in (0, 1):
                    f = 2 * q + up
                    prev = f - len(RING)
                    if prev >= 0 and prev % 2:
                        pe.wait_ge(f_mul, prev // 2 + 1)
                    elif prev >= 0:
                        pe.wait_ge(f_silu, prev // 2 + 1)
                    dst = bank[RING[f % len(RING)]][:, :]
                    if self.layer == 0:
                        for c in range(KC):
                            last = product(dst, self.gate_up(m, up, c), lambda i: xnT[i][:, c, cols],
                                           c == 0, c == KC - 1)
                    else:
                        last = product(dst, self.gate_up(m, up, 0), lambda i: pz[i][:, :])
                    last.then_inc(f_ready, 1)

            def tensor_down(self, pe, k, m):
                q = self.m0 + k * self.M + m
                pe.wait_ge(f_lo, q + 1)
                first, end = m == 0, m == self.M - 1
                if self.layer == 0:
                    for t in range(4):
                        if first and k == 1:
                            pe.wait_ge(x_written, self.x_before + 2 * t + 2)
                        last = product(bank[self.out_banks[t]][:, :],
                                       lambda i: self.h[i][:, q % 2, t * P:(t + 1) * P], self.down(m),
                                       first, end)
                        if end:
                            last.then_inc(f_out, 1)
                else:
                    last = product(bank[ZB][:, :], self.down(m), lambda i: self.h[i][:, q % 2, :],
                                   first, end)
                    if end:
                        last.then_inc(pz_ready, 1)
                if not end:
                    last.then_inc(f_used, 1)

            def scalar(self, act):
                M = self.M
                if self.first:
                    for t in range(4):
                        ln_hi_part(act, self.ln0 + t, LNB, xnT_tile(t))
                for st, j, dst in self.own:
                    st.split_hi(act, j, dst)
                for k in range(2):
                    if self.layer:
                        self.low_rank_hi(act, self.z0 + 2 * k)
                    for m in range(M + 1):
                        q = self.m0 + k * M + m
                        if m < M:
                            act.wait_ge(f_ready, 2 * q + 1)
                            at_least(act, f_lo, q - 1)
                            nc.scalar.activation(work[:, 2 + q % 2, :], bank[RING[(2 * q) % 3]][:, :],
                                                 ACT.Silu, bias=self.bias(m, 0)).then_inc(f_silu, 1)
                        if m > 0:
                            q -= 1
                            act.wait_ge(f_mul, q + 1)
                            if m > 2:
                                act.wait_ge(f_used, self.u0 + k * (M - 1) + m - 2)
                            nc.scalar.copy(self.h[HI][:, q % 2, :], work[:, 2 + q % 2, :]).then_inc(f_hi, 1)
                        if m < M:
                            for n, t in self.ln_tiles(k, m):
                                if k == 1:
                                    act.wait_ge(f_ready, 2 * (self.m0 + M))
                                ln_hi_part(act, n, LNB, xnT_tile(t))
                            for st, j, dst in self.splits(k, m):
                                st.split_hi(act, j, dst)
                    if self.layer:
                        self.low_rank_hi(act, self.z0 + 2 * k + 1)

            def low_rank_hi(self, act, z):
                act.wait_ge(pz_ready, z + 1)
                nc.scalar.copy(pz[HI][:, :], bank[ZB][:, :]).then_inc(pz_hi, 1)

            def vector(self, dve):
                M = self.M

                def normalise(k, n, t):
                    if self.x_before == 0 and n < TILES:
                        dve.wait_ge(x_loaded[t], 16)
                    elif n < self.ln0 + TILES:
                        dve.wait_ge(x_written, self.x_before)
                    else:
                        dve.wait_ge(x_written, self.x_before + 2 * (t + 1))
                    ln_normalise(dve, n, t % 2, x[:, t, :])

                if self.first:
                    for t in range(5):
                        if t < 4:
                            normalise(0, self.ln0 + t, t)
                        if t > 0:
                            ln_lo_part(dve, self.ln0 + t - 1, LNB, xnT_tile(t - 1))
                for st, j, dst in self.own:
                    st.split_lo(dve, j, dst)
                for k in range(2):
                    if self.layer:
                        self.low_rank_lo(dve, self.z0 + 2 * k)
                    for m in range(M + 1):
                        q = self.m0 + k * M + m
                        tiles = self.ln_tiles(k, m) if m < M else []
                        for n, t in tiles:
                            normalise(k, n, t)
                        if m < M:
                            dve.wait_ge(f_ready, 2 * q + 2)
                            dve.wait_ge(f_silu, q + 1)
                            w = work[:, 2 + q % 2, :]
                            nc.vector.scalar_tensor_tensor(w, bank[RING[(2 * q + 1) % 3]][:, :],
                                                           self.bias(m, 1), w, ALU.add,
                                                           ALU.mult).then_inc(f_mul, 1)
                        if m > 0:
                            q -= 1
                            dve.wait_ge(f_hi, q + 1)
                            nc.vector.tensor_tensor(self.h[LO][:, q % 2, :], work[:, 2 + q % 2, :],
                                                    self.h[HI][:, q % 2, :].bitcast(F32),
                                                    ALU.subtract).then_inc(f_lo, 1)
                        for n, t in tiles:
                            ln_lo_part(dve, n, LNB, xnT_tile(t))
                        if m < M:
                            for st, j, dst in self.splits(k, m):
                                st.split_lo(dve, j, dst)
                    if self.layer:
                        self.low_rank_lo(dve, self.z0 + 2 * k + 1)
                    for t in range(4 * k, 4 * k + 4):
                        xt = x[:, t, :]
                        before = self.x_before + 2 * t
                        dve.wait_ge(row_loaded, 16 * (self.row_n + 1))
                        dve.wait_ge(ln_xn, self.ln0 + t + 1)
                        nc.vector.scalar_tensor_tensor(xt, row[:, :], 0.5, xt, ALU.mult,
                                                       ALU.add).then_inc(x_written, 1)
                        dve.wait_ge(x_written, before + 1)
                        dve.wait_ge(f_out, self.o0 + t + 1)
                        nc.vector.scalar_tensor_tensor(xt, bank[self.bank_of(self.o0 + t)][:, :], 0.5, xt,
                                                       ALU.mult, ALU.add).then_inc(x_written, 1)

            def low_rank_lo(self, dve, z):
                dve.wait_ge(pz_hi, z + 1)
                nc.vector.tensor_tensor(pz[LO][:, :], bank[ZB][:, :], pz[HI][:, :].bitcast(F32),
                                        ALU.subtract).then_inc(pz_lo, 1)

            def gpsimd(self, pool):
                if self.first:
                    for t in range(4):
                        ln_power(pool, self.ln0 + t, t % 2)
                for k in range(2):
                    for m in range(self.M):
                        for n, t in self.ln_tiles(k, m):
                            ln_power(pool, n, t % 2)

        def lot(stream, w, columns):
            return [(stream, j, chunk(w, c)) for j, c in enumerate(columns)]

        X1 = 2 * TILES
        X2 = X1 + 1
        X3, X4 = X2 + 2 * TILES, X2 + 4 * TILES
        X5 = X4 + 1
        ffn0a = FFN(0, WF0, h0, 0, 8, 0, 0, True, lot(st_f0a, WF0, range(F0_CHUNKS)),
                    lot(st_lq, W, [C_WO]) + lot(st_a0, W, EARLY))
        ffn0b = FFN(0, W, h0, 16, 24, X2, 1, True, lot(st_f0b, W, [F0_CHUNKS - 1]),
                    lot(st_f1a, WF1, range(F1_CHUNKS)))
        ffn1a = FFN(1, WF1, h1, 24, None, X3, 2, False, (), lot(st_a1, W, range(A1_CHUNKS)),
                    (st_f1a, F1_CHUNKS - 1))
        ffn1b = FFN(1, WF1, h1, 40, None, X5, 4, True, lot(st_f1b, WF1, range(F1_CHUNKS)), ())

        a_proj = sem("a_proj")
        a_proj_free = sem("a_proj_free")
        a_lv_hi = sem("a_lv_hi")
        a_swapped = sem("a_swapped")
        a_sin = sem("a_sin")
        a_rope = sem("a_rope")
        a_rope_hi = sem("a_rope_hi")
        a_rope_lo = sem("a_rope_lo")
        a_scores = sem("a_scores")
        a_min = sem("a_min")
        a_exp = sem("a_exp")
        a_inv = sem("a_inv")
        a_norm = sem("a_norm")
        a_turned = sem("a_turned")
        a_pt_hi = sem("a_pt_hi")
        a_pt_lo = sem("a_pt_lo")
        a_pv = sem("a_pv")
        a_o_hi = sem("a_o_hi")
        a_o_lo = sem("a_o_lo")
        a_out = sem("a_out")
        a_added = sem("a_added")
        a_lq = sem("a_lq")
        a_lq_hi = sem("a_lq_hi")
        a_lq_lo = sem("a_lq_lo")
        pt_zero = sem("pt_zero")
        PT, OB, OUTB = 4, 5, (6, 7)
        FILLS, ROPES, INST = 9, 5, 2 * GH
        NB = BATCH

        class Place:

            def __init__(self, g, b):
                self.g, self.b = g, b

            def of(self, per_batch, local):
                return self.g * (per_batch * NB) + (self.b * per_batch + local)

            def fill(self, i):
                return self.of(FILLS, i), (self.b * FILLS + i) % 2

            def rope(self, i):
                return self.of(ROPES, i), (self.b * ROPES + i) % 2

            def inst(self, i):
                return self.of(INST, i), i % 2

        def fill_of_head(h):
            return 1 if h == 0 else 5 + h

        def a0_tensor(pe):
            for t in range(4, TILES):
                ln_turn(pe, 8 + t, t % 2, LNB)
            pe.wait_ge(ln_done, 16)
            st_lq.ready(pe, 0)
            for i in range(2):
                for c in range(KC):
                    at = C_WO * CH + c * P
                    last = product(bank[OUTB[i]][:, :], lambda p: W[p][:, at:at + P],
                                   lambda p: xnT[p][:, c, i * CH:(i + 1) * CH], c == 0, c == KC - 1)
                last.then_inc(a_lq, 1)
            pe.wait_ge(a_lq_lo, 2)
            pe.wait_ge(pt_zero, 2)
            with pe.Fori(0, KVH) as g:
                for b in range(NB):
                    a0_tensor_batch(pe, g, b)

        def a0_tensor_batch(pe, g, b):
            at = Place(g, b)

            def claim(at, i):
                n, s = at.fill(i)
                pe.wait_ge(a_proj_free, n + 1)
                return bank[s]

            def keys(at):
                if at.b == 0:
                    st_a0_or_loop_ready(pe, g)
                toks = slice(at.b * SEQ, (at.b + 1) * SEQ)
                dst = claim(at, 0)
                for c in range(KC):
                    last = product(dst[:, SEQ:2 * SEQ],
                                   lambda p: W[p][:, C_K * CH + c * P:C_K * CH + (c + 1) * P],
                                   lambda p: xnT[p][:, c, toks], c == 0, c == KC - 1)
                last.then_inc(a_proj, 1)

            def queries(at, h):
                toks = slice(at.b * SEQ, (at.b + 1) * SEQ)
                dst = claim(at, fill_of_head(h))
                for c in range(KC):
                    w = (C_Q + h) * CH + c * P
                    product(dst[:, 0:SEQ], lambda p: W[p][:, w:w + P],
                            lambda p: xnT[p][:, c, toks], c == 0, c == KC - 1)
                w = C_LK * CH + h * P
                product(dst[:, SEQ:2 * SEQ], lambda p: W[p][:, w:w + P],
                        lambda p: lqT[p][:, toks]).then_inc(a_proj, 1)

            def values():
                for i in range(4):
                    tt, half = divmod(i, 2)
                    dst = claim(at, 2 + i)
                    for c in range(KC):
                        w = C_LVV * CH + c * LVW + half * HALF
                        t = b * SEQ + tt * P
                        last = product(dst[:, 0:HALF], lambda p: xnT[p][:, c, t:t + P],
                                       lambda p: W[p][:, w:w + HALF], c == 0, c == KC - 1)
                    last.then_inc(a_proj, 1)

            def scores(i):
                n, s = at.inst(i)
                h, latent = divmod(i, 2)
                r, _ = at.rope(h + 1)
                if latent == 0:
                    pe.wait_ge(a_rope_lo, r + 3)
                pe.wait_ge(a_min, n + 1)
                for qt in range(2):
                    q = lambda p: qlk[p][:, h % 2, qt * P:(qt + 1) * P]
                    k = (lambda p: qlk[p][:, h % 2, SEQ:2 * SEQ]) if latent else (lambda p: kT[p][:, :])
                    last = product(bank[2 + s][:, qt * SEQ:(qt + 1) * SEQ], q, k)
                last.then_inc(a_scores, 1)

            def turn(i):
                n, s = at.inst(i)
                pe.wait_ge(a_norm, n + 1)
                pe.wait_ge(a_pt_lo, n + 1)
                for blk in range(3):
                    last = nc.tensor.transpose(bank[PT][:, blk * P:(blk + 1) * P],
                                               s0[:, s, blk * P:(blk + 1) * P], ident)
                last.then_inc(a_turned, 1)

            def weigh(i):
                n, s = at.inst(i)
                h, latent = divmod(i, 2)
                col = h * P if latent else GH * P
                if i == 0:
                    pe.wait_ge(a_proj_free, at.fill(5)[0] + 3)
                pe.wait_ge(a_pt_lo, n + 2)
                pe.wait_ge(a_o_lo, n + 1)
                for kt in range(2):
                    if kt == 0:
                        rhs = lambda p: pt0[p][:, s, P:3 * P]
                    else:
                        rhs = lambda p: pt0[p][:, s, :].rearrange("p (a n) -> p a n", n=P)[:, 0::3, :]
                    last = product(bank[OB][:, 0:SEQ], lambda p: lvv[p][:, kt, col:col + P], rhs,
                                   kt == 0, kt == 1)
                last.then_inc(a_pv, 1)

            def outputs(ids):
                for i in ids:
                    n, _ = at.inst(i)
                    h, latent = divmod(i, 2)
                    if i == 0:
                        pe.wait_ge(a_added, at.of(2, 1))
                        if b == 0:
                            st_loop.ready(pe, len(LATE) - 1, g)
                    pe.wait_ge(a_o_lo, n + 2)
                    w = ((C_WLO if latent else C_WO) + h) * CH
                    for tt in range(2):
                        last = product(bank[OUTB[tt]][:, :], lambda p: oT0[p][:, i, tt * P:(tt + 1) * P],
                                       lambda p: W[p][:, w:w + CH], i == 0, i == INST - 1)
                        if i == INST - 1:
                            last.then_inc(a_out, 1)

            if b == 0:
                keys(at)
                queries(at, 0)
            values()
            for h in range(GH):
                if h > 0:
                    turn(2 * h - 2)
                if h + 1 < GH:
                    queries(at, h + 1)
                if h > 0:
                    weigh(2 * h - 2)
                    turn(2 * h - 1)
                scores(2 * h)
                scores(2 * h + 1)
                if h > 0:
                    weigh(2 * h - 1)
            turn(INST - 2)
            outputs((0, 1, 2))
            weigh(INST - 2)
            turn(INST - 1)
            outputs((3, 4, 5))
            weigh(INST - 1)
            if b + 1 < NB:
                keys(Place(g, b + 1))
                queries(Place(g, b + 1), 0)
            outputs((6, 7))

        def st_a0_or_loop_ready(eng, g):
            eng.wait_ge(w_split, st_a0.base + len(EARLY) + g * G_CHUNKS)

        def dst_of(j):
            return chunk(W, LATE[j] if j < len(LATE) else EARLY[j - len(LATE)])

        def loop_splits(b, h):
            if b == 0:
                return [LATE.index(c) for c in LATE_AT[h]]
            if b == NB - 1:
                return [len(LATE) + EARLY.index(c) for c in EARLY_AT[h]]
            return []

        def a0_scalar(act):
            for t in range(4, TILES):
                ln_hi_part(act, 8 + t, LNB, xnT_tile(t))
            for i in range(2):
                act.wait_ge(a_lq, i + 1)
                nc.scalar.copy(lqT[HI][:, i * CH:(i + 1) * CH], bank[OUTB[i]][:, :]).then_inc(a_lq_hi, 1)
            with act.Fori(0, KVH) as g:
                for b in range(NB):
                    a0_scalar_batch(act, g, b)

        def a0_scalar_batch(act, g, b):
            def swap(at, i):
                n, s = at.rope(i)
                f, fs = at.fill(0 if i == 0 else fill_of_head(i - 1))
                act.wait_ge(a_proj, f + 1)
                act.wait_ge(a_rope_lo, n + 1)
                cols = slice(SEQ, 2 * SEQ) if i == 0 else slice(0, 2 * SEQ)
                half = P // 2
                nc.scalar.copy(work[0:half, s, cols], bank[fs][half:P, cols])
                nc.scalar.copy(work[half:P, s, cols], bank[fs][0:half, cols]).then_inc(a_swapped, 1)

            def rope_hi(at, i):
                n, s = at.rope(i)
                act.wait_ge(a_rope, n + 1)
                if i == 0:
                    nc.scalar.copy(kT[HI][:, :], work[:, 2 + s, SEQ:2 * SEQ]).then_inc(a_rope_hi, 1)
                else:
                    nc.scalar.copy(qlk[HI][:, (i - 1) % 2, :], work[:, 2 + s, :]).then_inc(a_rope_hi, 1)

            def values_hi(at):
                for i in range(4):
                    tt, half = divmod(i, 2)
                    f, fs = at.fill(2 + i)
                    act.wait_ge(a_proj, f + 1)
                    nc.scalar.copy(lvv[HI][:, tt, half * HALF:(half + 1) * HALF],
                                   bank[fs][:, 0:HALF]).then_inc(a_lv_hi, 1)

            def exponentials(i):
                n, s = at.inst(i)
                act.wait_ge(a_min, n + 3)
                for qt, cols in ((0, slice(0, P)), (1, slice(P, 3 * P))):
                    last = nc.scalar.activation(s0[:, s, cols], s0[:, s, cols], ACT.Exp,
                                                bias=neg_max[:, s, qt:qt + 1], scale=-1.0,
                                                accum_out=row_sum[:, s, qt:qt + 1])
                last.then_inc(a_exp, 1)

            def turned_hi(i):
                n, s = at.inst(i)
                act.wait_ge(a_turned, n + 1)
                nc.scalar.copy(pt0[HI][:, s, P:4 * P], bank[PT][:, 0:3 * P]).then_inc(a_pt_hi, 1)

            def result_hi(i):
                n, s = at.inst(i)
                act.wait_ge(a_pv, n + 1)
                nc.scalar.copy(oT0[HI][:, i, :], bank[OB][:, 0:SEQ]).then_inc(a_o_hi, 1)

            def splits(h):
                for j in loop_splits(b, h):
                    st_loop.split_hi(act, j, dst_of(j), g)

            at = Place(g, b)
            if b == 0:
                swap(at, 0)
                swap(at, 1)
                rope_hi(at, 0)
                rope_hi(at, 1)
            values_hi(at)
            for h in range(GH):
                if h > 0:
                    turned_hi(2 * h - 2)
                if h + 1 < GH:
                    swap(at, h + 2)
                if h > 0:
                    result_hi(2 * h - 2)
                    turned_hi(2 * h - 1)
                exponentials(2 * h)
                if h + 1 < GH:
                    rope_hi(at, h + 2)
                exponentials(2 * h + 1)
                if h > 0:
                    result_hi(2 * h - 1)
                splits(h)
            turned_hi(INST - 2)
            result_hi(INST - 2)
            turned_hi(INST - 1)
            result_hi(INST - 1)
            if b + 1 < NB:
                after = Place(g, b + 1)
                swap(after, 0)
                swap(after, 1)
                rope_hi(after, 0)
                rope_hi(after, 1)

        def a0_vector(dve):
            for s, n in ((a_proj_free, 2), (a_rope_lo, 2), (a_min, 2), (a_pt_lo, 1), (a_o_lo, 1),
                         (a_added, 1)):
                dve.sem_inc(s, n)
            dve.wait_ge(x_written, X1)
            for i in (HI, LO):
                nc.vector.memset(pt0[i][:, :, 0:P].bitcast(F32), 0.0).then_inc(pt_zero, 1)
            for t in range(4, TILES):
                ln_normalise(dve, 8 + t, t % 2, x[:, t, :])
                ln_lo_part(dve, 8 + t, LNB, xnT_tile(t))
            for i in range(2):
                dve.wait_ge(a_lq_hi, i + 1)
                cols = slice(i * CH, (i + 1) * CH)
                nc.vector.tensor_tensor(lqT[LO][:, cols], bank[OUTB[i]][:, :], lqT[HI][:, cols].bitcast(F32),
                                        ALU.subtract).then_inc(a_lq_lo, 1)
            with dve.Fori(0, KVH) as g:
                for b in range(NB):
                    a0_vector_batch(dve, g, b)

        def a0_vector_batch(dve, g, b):
            def cosine(at, i):
                n, s = at.rope(i)
                f, fs = at.fill(0 if i == 0 else fill_of_head(i - 1))
                dve.wait_ge(a_swapped, n + 1)
                dve.wait_ge(a_rope_lo, n + 1)
                cols = slice(SEQ, 2 * SEQ) if i == 0 else slice(0, 2 * SEQ)
                nc.vector.tensor_tensor(work[:, 2 + s, cols], bank[fs][:, cols],
                                        table[:, T_COS + cols.start:T_COS + cols.stop],
                                        ALU.mult).then_inc(a_proj_free, 1)

            def rotate(at, i):
                n, s = at.rope(i)
                f, _ = at.fill(0 if i == 0 else fill_of_head(i - 1))
                dve.wait_ge(a_sin, n + 1)
                dve.wait_ge(a_proj_free, f + 3)
                cols = slice(SEQ, 2 * SEQ) if i == 0 else slice(0, 2 * SEQ)
                nc.vector.tensor_tensor(work[:, 2 + s, cols], work[:, 2 + s, cols], work[:, s, cols],
                                        ALU.add).then_inc(a_rope, 1)

            def values_lo(at):
                for i in range(4):
                    tt, half = divmod(i, 2)
                    _, fs = at.fill(2 + i)
                    dve.wait_ge(a_lv_hi, at.of(4, i + 1))
                    cols = slice(half * HALF, (half + 1) * HALF)
                    nc.vector.tensor_tensor(lvv[LO][:, tt, cols], bank[fs][:, 0:HALF],
                                            lvv[HI][:, tt, cols].bitcast(F32),
                                            ALU.subtract).then_inc(a_proj_free, 1)

            def minima(i):
                n, s = at.inst(i)
                dve.wait_ge(a_scores, n + 1)
                dve.sem_inc(passed, 1)
                nc.vector.tensor_tensor_reduce(s0[:, s, 0:P], bank[2 + s][:, 0:P], table[:, T_M0:T_M0 + P],
                                               1.0, 3e38, ALU.add, ALU.min, neg_max[:, s, 0:1])
                nc.vector.tensor_tensor_reduce(s0[:, s, P:3 * P], bank[2 + s][:, 2 * P:4 * P],
                                               table[:, T_M0 + P:T_M0 + 3 * P],
                                               1.0, 3e38, ALU.add, ALU.min,
                                               neg_max[:, s, 1:2]).then_inc(a_min, 1)

            def inverses(i):
                n, s = at.inst(i)
                dve.wait_ge(a_exp, n + 1)
                nc.vector.reciprocal(inv_sum[:, s, :], row_sum[:, s, :]).then_inc(a_inv, 1)

            def turned_lo(i):
                n, s = at.inst(i)
                dve.wait_ge(a_pt_hi, n + 1)
                nc.vector.tensor_tensor(pt0[LO][:, s, P:4 * P], bank[PT][:, 0:3 * P],
                                        pt0[HI][:, s, P:4 * P].bitcast(F32),
                                        ALU.subtract).then_inc(a_pt_lo, 1)

            def result_lo(i):
                n, s = at.inst(i)
                dve.wait_ge(a_o_hi, n + 1)
                nc.vector.tensor_tensor(oT0[LO][:, i, :], bank[OB][:, 0:SEQ], oT0[HI][:, i, :].bitcast(F32),
                                        ALU.subtract).then_inc(a_o_lo, 1)

            def add_outputs(at):
                for tt in range(2):
                    xt = x[:, 2 * at.b + tt, :]
                    dve.wait_ge(a_out, at.of(2, tt + 1))
                    nc.vector.tensor_tensor(xt, xt, bank[OUTB[tt]][:, :], ALU.add).then_inc(a_added, 1)

            def splits(h):
                for j in loop_splits(b, h):
                    st_loop.split_lo(dve, j, dst_of(j), g)

            at = Place(g, b)
            if b == 0:
                cosine(at, 0)
                cosine(at, 1)
                rotate(at, 0)
                rotate(at, 1)
            values_lo(at)
            for h in range(GH):
                if h > 0:
                    turned_lo(2 * h - 2)
                if h + 1 < GH:
                    cosine(at, h + 2)
                if h > 0:
                    result_lo(2 * h - 2)
                    turned_lo(2 * h - 1)
                if h + 1 < GH:
                    rotate(at, h + 2)
                minima(2 * h)
                minima(2 * h + 1)
                inverses(2 * h)
                inverses(2 * h + 1)
                if h > 0:
                    result_lo(2 * h - 1)
                splits(h)
            turned_lo(INST - 2)
            result_lo(INST - 2)
            turned_lo(INST - 1)
            result_lo(INST - 1)
            if b + 1 < NB:
                after = Place(g, b + 1)
                cosine(after, 0)
                cosine(after, 1)
                rotate(after, 0)
                rotate(after, 1)
            add_outputs(at)

        def a0_gpsimd(pool):
            for t in range(4, TILES):
                ln_power(pool, 8 + t, t % 2)
            with pool.Fori(0, KVH) as g:
                for b in range(NB):
                    a0_gpsimd_batch(pool, g, b)

        def a0_gpsimd_batch(pool, g, b):
            def sine(at, i):
                n, s = at.rope(i)
                cols = slice(SEQ, 2 * SEQ) if i == 0 else slice(0, 2 * SEQ)
                pool.wait_ge(a_swapped, n + 1)
                nc.gpsimd.tensor_tensor(work[:, s, cols], work[:, s, cols],
                                        table[:, T_SIN + cols.start:T_SIN + cols.stop],
                                        ALU.mult).then_inc(a_sin, 1)

            def rope_lo(at, i):
                n, s = at.rope(i)
                pool.wait_ge(a_rope_hi, n + 1)
                if i == 0:
                    dst, hi, cols = kT[LO][:, :], kT[HI][:, :], slice(SEQ, 2 * SEQ)
                else:
                    dst, hi, cols = qlk[LO][:, (i - 1) % 2, :], qlk[HI][:, (i - 1) % 2, :], slice(0, 2 * SEQ)
                nc.gpsimd.tensor_tensor(dst, work[:, 2 + s, cols], hi.bitcast(F32),
                                        ALU.subtract).then_inc(a_rope_lo, 1)

            def normalise(i):
                n, s = at.inst(i)
                pool.wait_ge(a_inv, n + 1)
                nc.gpsimd.tensor_tensor(s0[:, s, 0:P], s0[:, s, 0:P],
                                        inv_sum[:, s, 0:1].to_broadcast([P, P]), ALU.mult)
                nc.gpsimd.tensor_tensor(s0[:, s, P:3 * P], s0[:, s, P:3 * P],
                                        inv_sum[:, s, 1:2].to_broadcast([P, 2 * P]),
                                        ALU.mult).then_inc(a_norm, 1)

            at = Place(g, b)
            if b == 0:
                for i in (0, 1):
                    sine(at, i)
                for i in (0, 1):
                    rope_lo(at, i)
            for h in range(GH):
                if h + 1 < GH:
                    sine(at, h + 2)
                    rope_lo(at, h + 2)
                normalise(2 * h)
                normalise(2 * h + 1)
            if b + 1 < NB:
                after = Place(g, b + 1)
                for i in (0, 1):
                    sine(after, i)
                for i in (0, 1):
                    rope_lo(after, i)

        b_proj = sem("b_proj")
        b_proj_free = sem("b_proj_free")
        b_sin = sem("b_sin")
        b_cos = sem("b_cos")
        b_rope = sem("b_rope")
        b_k_hi = sem("b_k_hi")
        b_v_hi = sem("b_v_hi")
        b_v_lo = sem("b_v_lo")
        b_scores = sem("b_scores")
        b_min = sem("b_min")
        b_exp = sem("b_exp")
        b_inv = sem("b_inv")
        b_norm = sem("b_norm")
        b_turned = sem("b_turned")
        b_pt_hi = sem("b_pt_hi")
        b_pt_lo = sem("b_pt_lo")
        b_pv = sem("b_pv")
        b_o_hi = sem("b_o_hi")
        b_o_lo = sem("b_o_lo")
        b_out = sem("b_out")
        b_added = sem("b_added")
        b_zero = sem("b_zero")
        LN1 = 32
        FILLS1, STEPS = 6 + GR1, HEADS1 + 3

        def prep_at(j):
            grp = j // HG1 + 1
            return grp if j % HG1 == 3 and grp < GR1 else None

        def ends_at(j):
            return (j - 3) // HG1 if j >= 3 and (j - 3) % HG1 == HG1 - 1 else None

        def b_tensor(pe):
            pe.wait_ge(b_zero, 2)
            st_a1.ready(pe, A1_CHUNKS - 1)
            with pe.Fori(0, BATCH) as b:
                b_tensor_batch(pe, b)

        def b_tensor_batch(pe, b):
            def claim(i):
                pe.wait_ge(b_proj_free, b * FILLS1 + i + 1)
                return bank[i % 2]

            def prepare(grp):
                dst = claim(6 + grp)
                if grp == 0:
                    pe.wait_ge(b_rope, b * 4 + 4)
                for j in range(2):
                    for tt in range(2):
                        c = j * DIM + grp * P
                        last = nc.tensor.transpose(dst[:, j * SEQ + tt * P:j * SEQ + (tt + 1) * P],
                                                   qkv[:, tt, c:c + P], ident)
                last.then_inc(b_proj, 1)

            def scores(i):
                grp, hh = divmod(i, HG1)
                rows, eo, s = slice(32 * (hh // 2), 32 * (hh // 2) + 32), hh % 2, grp % 2
                if hh == 0:
                    pe.wait_ge(b_proj_free, b * FILLS1 + 6 + grp + 3)
                pe.wait_ge(b_min, b * HEADS1 + i + 1)
                for qt in range(2):
                    last = product(bank[2 + i % 2][:, qt * SEQ:(qt + 1) * SEQ],
                                   lambda p: qE[p][rows, s, eo, qt * P:(qt + 1) * P],
                                   lambda p: k1[p][rows, s, :])
                last.then_inc(b_scores, 1)

            def turn(i):
                pe.wait_ge(b_norm, b * HEADS1 + i + 1)
                pe.wait_ge(b_pt_lo, b * HEADS1 + i + 1)
                for blk in range(3):
                    last = nc.tensor.transpose(bank[PT][:, blk * P:(blk + 1) * P],
                                               s1[:, i % 2, blk * P:(blk + 1) * P], ident)
                last.then_inc(b_turned, 1)

            def weigh(i):
                grp, hh = divmod(i, HG1)
                if hh == 0:
                    pe.wait_ge(b_v_lo, b * GR1 + grp + 1)
                    pe.wait_ge(b_o_lo, b * GR1 + grp + 1)
                pe.wait_ge(b_pt_lo, b * HEADS1 + i + 2)
                for kt in range(2):
                    if kt == 0:
                        rhs = lambda p: pt1[p][:, i % 2, P:3 * P]
                    else:
                        rhs = lambda p: pt1[p][:, i % 2, :].rearrange("p (a n) -> p a n", n=P)[:, 0::3, :]
                    last = product(bank[OB][:, 0:SEQ], lambda p: vz[p][:, grp % 2, kt, hh, :], rhs,
                                   hh == 0 and kt == 0, hh == HG1 - 1 and kt == 1)
                if hh == HG1 - 1:
                    last.then_inc(b_pv, 1)

            def outputs(grp):
                pe.wait_ge(b_o_lo, b * GR1 + grp + 2)
                w = (KC * 3 + grp) * CH
                for tt in range(2):
                    last = product(bank[OUTB[tt]][:, :], lambda p: oT1[p][:, grp, tt * P:(tt + 1) * P],
                                   lambda p: W[p][:, w:w + CH], grp == 0, grp == GR1 - 1)
                    if grp == GR1 - 1:
                        last.then_inc(b_out, 1)

            for tt in range(2):
                ln_turn(pe, b * 2 + (LN1 + tt), tt, OUTB[tt])
            for tt in range(2):
                pe.wait_ge(ln_done, b * 2 + (LN1 + tt + 1))
                for j in range(3):
                    dst = claim(3 * tt + j)
                    for c in range(KC):
                        w = c * 3 * DIM + j * DIM
                        last = product(dst[:, :], lambda p: xb[p][:, c, tt * P:(tt + 1) * P],
                                       lambda p: W[p][:, w:w + DIM], c == 0, c == KC - 1)
                    last.then_inc(b_proj, 1)
            prepare(0)
            for j in range(STEPS):
                if 2 <= j < HEADS1 + 2:
                    turn(j - 2)
                if j < HEADS1:
                    scores(j)
                if j >= 3:
                    weigh(j - 3)
                if prep_at(j):
                    prepare(prep_at(j))
                if j % HG1 == 5 and j > HG1:
                    outputs(j // HG1 - 1)
            outputs(GR1 - 1)

        def b_scalar(act):
            act.wait_ge(b_zero, 2)
            with act.Fori(0, BATCH) as b:
                b_scalar_batch(act, b)

        def diagonal(t, s, tt):
            flat = t[:, s, tt, :, :].rearrange("p h (a d) -> p (h a) d", d=D1)
            return flat[:, 0::HG1 + 1, :]

        def values_of(grp, tt):
            c = 2 * DIM + grp * P
            return qkv[:, tt, c:c + P].rearrange("p (h d) -> p h d", d=D1)

        def b_scalar_batch(act, b):
            def prepare_hi(grp):
                s = grp % 2
                src = bank[(6 + grp) % 2]
                act.wait_ge(b_proj, b * FILLS1 + 6 + grp + 1)
                nc.scalar.copy(k1[HI][:, s, :], src[:, SEQ:2 * SEQ])
                for eo in range(2):
                    last = nc.scalar.activation(qE[HI][:, s, eo, :], src[:, 0:SEQ], ACT.Copy,
                                                scale=table[:, T_EO + eo:T_EO + eo + 1])
                last.then_inc(b_k_hi, 1)
                for tt in range(2):
                    last = nc.scalar.copy(diagonal(vz[HI], s, tt), values_of(grp, tt))
                last.then_inc(b_v_hi, 1)

            def exponentials(i):
                s = i % 2
                act.wait_ge(b_min, b * HEADS1 + i + 3)
                for qt, cols in ((0, slice(0, P)), (1, slice(P, 3 * P))):
                    last = nc.scalar.activation(s1[:, s, cols], s1[:, s, cols], ACT.Exp,
                                                bias=neg_max[:, s, qt:qt + 1], scale=-1.0,
                                                accum_out=row_sum[:, s, qt:qt + 1])
                last.then_inc(b_exp, 1)

            def turned_hi(i):
                act.wait_ge(b_turned, b * HEADS1 + i + 1)
                nc.scalar.copy(pt1[HI][:, i % 2, P:4 * P], bank[PT][:, 0:3 * P]).then_inc(b_pt_hi, 1)

            def result_hi(grp):
                act.wait_ge(b_pv, b * GR1 + grp + 1)
                nc.scalar.copy(oT1[HI][:, grp, :], bank[OB][:, 0:SEQ]).then_inc(b_o_hi, 1)

            for tt in range(2):
                ln_hi_part(act, b * 2 + (LN1 + tt), OUTB[tt], xb_tile(tt))
            prepare_hi(0)
            for j in range(STEPS):
                if 2 <= j < HEADS1 + 2:
                    turned_hi(j - 2)
                if j < HEADS1:
                    exponentials(j)
                if ends_at(j) is not None:
                    result_hi(ends_at(j))
                if prep_at(j):
                    prepare_hi(prep_at(j))

        def xb_tile(tt):
            return [xb[i][:, :, tt * P:(tt + 1) * P] for i in (HI, LO)]

        def b_vector(dve):
            for s, n in ((b_proj_free, 2), (b_min, 2), (b_pt_lo, 1), (b_o_lo, 1)):
                dve.sem_inc(s, n)
            dve.wait_ge(b_zero, 2)
            dve.wait_ge(x_written, X4)
            dve.wait_ge(bqkv_loaded, 16)
            dve.wait_ge(row_loaded, 16 * 4)
            with dve.Fori(0, BATCH) as b:
                b_vector_batch(dve, b)
            dve.wait_ge(b_added, 2 * TILES)
            dve.sem_inc(x_written, 1)

        def per_head(ap):
            return ap.rearrange("p (h d) -> p h d", d=D1)

        def angles(kind, tt):
            c = T_R1 + (kind * 2 + tt) * D1
            return table[:, c:c + D1].unsqueeze(1).to_broadcast([P, HEADS1, D1])

        def b_vector_batch(dve, b):
            def biased(tt, j):
                i = 3 * tt + j
                dve.wait_ge(b_proj, b * FILLS1 + i + 1)
                cols = slice(j * DIM, (j + 1) * DIM)
                nc.vector.tensor_tensor(qkv[:, tt, cols], bank[i % 2][:, :], bqkv[:, cols],
                                        ALU.add).then_inc(b_proj_free, 1)

            def cosine(tt, j):
                r = 2 * tt + j
                cols = slice(j * DIM, (j + 1) * DIM)
                dve.wait_ge(b_proj_free, b * FILLS1 + 3 * tt + j + 3)
                nc.vector.tensor_tensor(per_head(work[:, 2 + r % 2, :]), per_head(qkv[:, tt, cols]),
                                        angles(2 * j, tt), ALU.mult).then_inc(b_cos, 1)

            def rotate(tt, j):
                r = 2 * tt + j
                cols = slice(j * DIM, (j + 1) * DIM)
                dve.wait_ge(b_sin, b * 4 + r + 1)
                dve.wait_ge(b_cos, b * 4 + r + 1)
                nc.vector.tensor_tensor(qkv[:, tt, cols], work[:, 2 + r % 2, :], work[:, r % 2, :],
                                        ALU.add).then_inc(b_rope, 1)

            def prepare_lo(grp):
                s = grp % 2
                src = bank[(6 + grp) % 2]
                dve.wait_ge(b_k_hi, b * GR1 + grp + 1)
                nc.vector.tensor_tensor(k1[LO][:, s, :], src[:, SEQ:2 * SEQ], k1[HI][:, s, :].bitcast(F32),
                                        ALU.subtract)
                for eo in range(2):
                    last = nc.vector.scalar_tensor_tensor(
                        qE[LO][:, s, eo, :], src[:, 0:SEQ], table[:, T_EO + eo:T_EO + eo + 1],
                        qE[HI][:, s, eo, :].bitcast(F32), ALU.mult, ALU.subtract)
                last.then_inc(b_proj_free, 1)

            def minima(i):
                s = i % 2
                dve.wait_ge(b_scores, b * HEADS1 + i + 1)
                dve.sem_inc(passed, 1)
                nc.vector.tensor_tensor_reduce(s1[:, s, 0:P], bank[2 + s][:, 0:P], table[:, T_M1:T_M1 + P],
                                               1.0, 3e38, ALU.add, ALU.min, neg_max[:, s, 0:1])
                nc.vector.tensor_tensor_reduce(s1[:, s, P:3 * P], bank[2 + s][:, 2 * P:4 * P],
                                               table[:, T_M1 + P:T_M1 + 3 * P],
                                               1.0, 3e38, ALU.add, ALU.min,
                                               neg_max[:, s, 1:2]).then_inc(b_min, 1)

            def inverses(i):
                dve.wait_ge(b_exp, b * HEADS1 + i + 1)
                nc.vector.reciprocal(inv_sum[:, i % 2, :], row_sum[:, i % 2, :]).then_inc(b_inv, 1)

            def turned_lo(i):
                dve.wait_ge(b_pt_hi, b * HEADS1 + i + 1)
                nc.vector.tensor_tensor(pt1[LO][:, i % 2, P:4 * P], bank[PT][:, 0:3 * P],
                                        pt1[HI][:, i % 2, P:4 * P].bitcast(F32),
                                        ALU.subtract).then_inc(b_pt_lo, 1)

            def result_lo(grp):
                dve.wait_ge(b_o_hi, b * GR1 + grp + 1)
                nc.vector.tensor_tensor(oT1[LO][:, grp, :], bank[OB][:, 0:SEQ],
                                        oT1[HI][:, grp, :].bitcast(F32),
                                        ALU.subtract).then_inc(b_o_lo, 1)

            def tile(tt):
                return x[:, bass.ds(b * 2 + tt, 1), :].rearrange("p a n -> p (a n)")

            for tt in range(2):
                ln_normalise(dve, b * 2 + (LN1 + tt), tt, tile(tt))
                ln_lo_part(dve, b * 2 + (LN1 + tt), OUTB[tt], xb_tile(tt))
            for tt in range(2):
                biased(tt, 0)
                cosine(tt, 0)
                biased(tt, 1)
                cosine(tt, 1)
                biased(tt, 2)
                rotate(tt, 0)
                rotate(tt, 1)
            prepare_lo(0)
            for j in range(STEPS):
                if 1 <= j < HEADS1 + 1:
                    inverses(j - 1)
                if 2 <= j < HEADS1 + 2:
                    turned_lo(j - 2)
                if j < HEADS1:
                    minima(j)
                if ends_at(j) is not None:
                    result_lo(ends_at(j))
                if prep_at(j):
                    prepare_lo(prep_at(j))
            for tt in range(2):
                nc.vector.tensor_tensor(tile(tt), tile(tt), row[:, :], ALU.add).then_inc(b_added, 1)
            for tt in range(2):
                dve.wait_ge(b_added, b * 4 + tt + 1)
                dve.wait_ge(b_out, b * 2 + tt + 1)
                nc.vector.tensor_tensor(tile(tt), tile(tt), bank[OUTB[tt]][:, :],
                                        ALU.add).then_inc(b_added, 1)

        def b_gpsimd(pool):
            pool.wait_ge(x_written, X4)
            for i in (HI, LO):
                nc.gpsimd.memset(vz[i][:, :, :, :, :].bitcast(F32), 0.0)
                nc.gpsimd.memset(pt1[i][:, :, 0:P].bitcast(F32), 0.0).then_inc(b_zero, 1)
            with pool.Fori(0, BATCH) as b:
                b_gpsimd_batch(pool, b)

        def b_gpsimd_batch(pool, b):
            def sine(tt, j):
                r = 2 * tt + j
                pool.wait_ge(b_proj_free, b * FILLS1 + 3 * tt + j + 3)
                if r >= 2:
                    pool.wait_ge(b_rope, b * 4 + r - 1)
                c = j * DIM
                halves = lambda ap: ap.rearrange("p (h a d) -> p h a d", a=2, d=D1 // 2)
                t = T_R1 + ((2 * j + 1) * 2 + tt) * D1
                src, dst = halves(qkv[:, tt, c:c + DIM]), halves(work[:, r % 2, :])
                for a in range(2):
                    sin = table[:, t + a * (D1 // 2):t + (a + 1) * (D1 // 2)]
                    last = nc.gpsimd.tensor_tensor(dst[:, :, a, :], src[:, :, 1 - a, :],
                                                   sin.unsqueeze(1).to_broadcast([P, HEADS1, D1 // 2]),
                                                   ALU.mult)
                last.then_inc(b_sin, 1)

            def values_lo(grp):
                pool.wait_ge(b_v_hi, b * GR1 + grp + 1)
                for tt in range(2):
                    last = nc.gpsimd.tensor_tensor(diagonal(vz[LO], grp % 2, tt), values_of(grp, tt),
                                                   diagonal(vz[HI], grp % 2, tt).bitcast(F32),
                                                   ALU.subtract)
                last.then_inc(b_v_lo, 1)

            def normalise(i):
                s = i % 2
                pool.wait_ge(b_inv, b * HEADS1 + i + 1)
                nc.gpsimd.tensor_tensor(s1[:, s, 0:P], s1[:, s, 0:P],
                                        inv_sum[:, s, 0:1].to_broadcast([P, P]), ALU.mult)
                nc.gpsimd.tensor_tensor(s1[:, s, P:3 * P], s1[:, s, P:3 * P],
                                        inv_sum[:, s, 1:2].to_broadcast([P, 2 * P]),
                                        ALU.mult).then_inc(b_norm, 1)

            for tt in range(2):
                ln_power(pool, b * 2 + (LN1 + tt), tt)
            for tt in range(2):
                for j in range(2):
                    sine(tt, j)
            values_lo(0)
            for j in range(STEPS):
                if 1 <= j < HEADS1 + 1:
                    normalise(j - 1)
                if prep_at(j):
                    values_lo(prep_at(j))

        block = ctx.enter_context(nc.Block())

        @block.sync
        def _(sp):
            def flat(n):
                return w_in[n, :, :]

            xr = x_in.rearrange("(t p) d -> t p d", p=P)
            sp.dma_start(x[:, 0, :], xr[0]).then_inc(x_loaded[0], 16)
            sp.dma_start(table[:, :], table_in).then_inc(table_loaded, 16)
            sp.dma_start(biases[:, :], bias_in).then_inc(table_loaded, 16)
            for t in range(1, 4):
                sp.dma_start(x[:, t, :], xr[t]).then_inc(x_loaded[t], 16)
            for j in range(F0_CHUNKS):
                st_f0a.load(sp, j, flat(W_F0A + j))
                if j == 3:
                    for t in range(4, TILES):
                        sp.dma_start(x[:, t, :], xr[t]).then_inc(x_loaded[t], 16)
                    sp.dma_start(row[:, :], rows_in[0]).then_inc(row_loaded, 16)
            st_lq.load(sp, 0, flat(W_LQ))
            for j in range(len(EARLY)):
                st_a0.load(sp, j, flat(W_A0 + j))
            with sp.Fori(0, KVH) as g:
                for j in range(G_CHUNKS):
                    src = w_in[bass.ds(g * G_CHUNKS + (W_A0 + len(EARLY) + j), 1), :, :]
                    st_loop.load(sp, j, src.rearrange("a p n -> (a p) n"), g)
            for j in range(F0_CHUNKS - len(EARLY)):
                st_f0b.load(sp, j, flat(W_F0B + len(EARLY) + j))
            sp.wait_ge(x_written, X1)
            sp.dma_start(row[:, :], rows_in[0]).then_inc(row_loaded, 16)
            for j in range(F1_CHUNKS):
                st_f1a.load(sp, j, flat(W_F1 + j))
            sp.wait_ge(x_written, X3)
            sp.dma_start(row[:, :], rows_in[1]).then_inc(row_loaded, 16)
            for j in range(A1_CHUNKS):
                st_a1.load(sp, j, flat(W_A1 + j))
            sp.wait_ge(x_written, X4)
            sp.dma_start(row[:, :], rows_in[2]).then_inc(row_loaded, 16)
            sp.dma_start(bqkv[:, :], rows_in[3:6].rearrange("a p n -> p a n")).then_inc(bqkv_loaded, 16)
            for j in range(F1_CHUNKS):
                st_f1b.load(sp, j, flat(W_F1 + j))
            sp.wait_ge(x_written, X5)
            sp.dma_start(row[:, :], rows_in[1]).then_inc(row_loaded, 16)
            outr = out.rearrange("(t p) d -> t p d", p=P)
            for t in range(TILES):
                sp.wait_ge(x_written, X5 + 2 * (t + 1))
                sp.dma_start(outr[t], x[:, t, :]).then_inc(stored, 16)
            sp.wait_ge(stored, 16 * TILES)

        @block.tensor
        def _(pe):
            pe.wait_ge(table_loaded, 32)
            ffn0a.tensor(pe)
            a0_tensor(pe)
            ffn0b.tensor(pe)
            ffn1a.tensor(pe)
            b_tensor(pe)
            ffn1b.tensor(pe)

        @block.scalar
        def _(act):
            act.wait_ge(table_loaded, 32)
            ffn0a.scalar(act)
            a0_scalar(act)
            ffn0b.scalar(act)
            ffn1a.scalar(act)
            b_scalar(act)
            ffn1b.scalar(act)

        @block.vector
        def _(dve):
            dve.wait_ge(table_loaded, 32)
            ffn0a.vector(dve)
            a0_vector(dve)
            dve.wait_ge(a_added, 1 + KVH * TILES)
            dve.sem_inc(x_written, 1)
            ffn0b.vector(dve)
            ffn1a.vector(dve)
            b_vector(dve)
            ffn1b.vector(dve)

        @block.gpsimd
        def _(pool):
            pool.wait_ge(table_loaded, 32)
            ffn0a.gpsimd(pool)
            a0_gpsimd(pool)
            ffn0b.gpsimd(pool)
            ffn1a.gpsimd(pool)
            b_gpsimd(pool)
            ffn1b.gpsimd(pool)


def chunks_of(a):
    n = -(-a.shape[1] // CH) * CH
    full = np.zeros((P, n), a.dtype)
    full[:, :a.shape[1]] = a
    return full.reshape(P, n // CH, CH).transpose(1, 0, 2)


def by_rows(w):
    k = w.shape[0] // P
    return w.reshape(k, P, w.shape[1]).transpose(1, 0, 2).reshape(P, k * w.shape[1])


def lay_out_weights(a):
    f0 = chunks_of(np.concatenate([by_rows(a["L0_ffn_w12"].T), by_rows(a["L0_ffn_w3"].T)], 1))
    wq, wk, wv = a["L0_attn_w_q"], a["L0_attn_w_k"], a["L0_attn_w_v"]
    wlk, wlv, wo, wlo = a["L0_attn_w_lk"], a["L0_attn_w_lv"], a["L0_attn_w_o"], a["L0_attn_w_lo"]
    groups = []
    for g in range(KVH):
        kv = slice(g * HD, (g + 1) * HD)
        hs = slice(g * GH * HD, (g + 1) * GH * HD)
        heads = [slice((g * GH + h) * HD, (g * GH + h + 1) * HD) for h in range(GH)]
        groups.append(chunks_of(np.concatenate(
            [by_rows(wk[:, kv])] + [by_rows(wq[:, h]) for h in heads] + [wlk[:, hs]]
            + [by_rows(np.concatenate([wlv[:, hs], wv[:, kv]], 1))]
            + [by_rows(wo[hs])] + [by_rows(wlo[hs])], 1)))
    groups.append(f0)
    a0 = [groups[0][EARLY]]
    for g in range(KVH):
        a0 += [groups[g][LATE], groups[g + 1][EARLY]]
    a0.append(f0[len(EARLY):])
    v1, u2 = a["L1_ffn_V1"], a["L1_ffn_U2"]
    halves = []
    for up in range(2):
        part = np.zeros((P, M1 * P), v1.dtype)
        part[:, :INTER] = v1[:, up * INTER:(up + 1) * INTER]
        halves.append(part)
    u2p = np.zeros((M1 * P, u2.shape[1]), u2.dtype)
    u2p[:INTER] = u2
    f1 = chunks_of(np.concatenate([by_rows(a["L1_ffn_U1"])] + halves + [by_rows(u2p), a["L1_ffn_V2"]], 1))
    a1 = chunks_of(np.concatenate([by_rows(a["L1_attn_qkv_w"]), by_rows(a["L1_attn_out_w"])], 1))
    lq = chunks_of(by_rows(a["L0_attn_w_lq"]))
    return np.ascontiguousarray(np.concatenate([f0, lq] + a0 + [f1, a1], 0))


def lay_out_biases(a):
    b = np.zeros((P, B_ALL), np.float32)
    b[:, B_12:B_12 + 2 * M0] = a["L0_ffn_b12"].reshape(2 * M0, P).T
    for up in range(2):
        part = np.zeros(M1 * P, np.float32)
        part[:INTER] = a["L1_ffn_b1"][up * INTER:(up + 1) * INTER]
        b[:, B_1 + up * M1:B_1 + (up + 1) * M1] = part.reshape(M1, P).T
    rows = np.concatenate([a["L0_ffn_b3"], a["L1_ffn_b2"], a["L1_attn_out_b"], a["L1_attn_qkv_b"]])
    rows = np.broadcast_to(rows.reshape(6, 1, DIM), (6, P, DIM))
    return b, np.ascontiguousarray(rows)


def kernel(**inputs):
    import concourse.bacc as bacc
    from concourse.bass_utils import run_bass_kernel_spmd

    a = {k: np.ascontiguousarray(v) for k, v in inputs.items()}
    weights = lay_out_weights(a)
    biases, rows = lay_out_biases(a)
    arrays = {"x": a["L0_attn_hidden_states"].reshape(TOKENS, DIM), "weights": weights,
              "constants": constants(), "bias_columns": biases, "bias_rows": rows}
    nc = bacc.Bacc("TRN2", target_bir_lowering=False, num_devices=1)
    args = [nc.dram_tensor(f"in_{n}", v.shape, F32, kind="ExternalInput").ap() for n, v in arrays.items()]
    args.append(nc.dram_tensor("out", (TOKENS, DIM), F32, kind="ExternalOutput").ap())
    program(nc, *args)
    r = run_bass_kernel_spmd(nc, [{f"in_{n}": v for n, v in arrays.items()}], core_ids=[0])
    return r.results[0]["out"].reshape(BATCH, SEQ, DIM)
```

```python
from contextlib import ExitStack

import numpy as np

import concourse.bass as bass
from concourse import mybir

F32 = mybir.dt.float32
F32R = mybir.dt.float32r
ALU = mybir.AluOpType
ACT = mybir.ActivationFunctionType

P = 128
BATCH, SEQ, DIM = 4, 256, 512
TOKENS = BATCH * SEQ
TILES = TOKENS // P
KC = DIM // P
CH = 512
HI, LO = 0, 1
PASSES = ((HI, HI), (HI, LO), (LO, HI))
EPS = 1e-5

HEADS0, KVH, HD = 32, 8, 128
GH = HEADS0 // KVH
G_CHUNKS = 19
C_K, C_Q, C_LK, C_LVV, C_WO, C_WLO = 0, 1, 5, 6, 11, 15
SPLIT_AT = {2: [17, 14], 3: [18], 11: [1], 12: [0, 2], 13: [3, 6], 14: [4, 7], 15: [8, 9],
            16: [10, 11, 15, 12], 17: [16, 13]}
SPLIT_LATE = {13: [5]}
SPLIT_FROM = 11
TURN = [c for s in sorted(SPLIT_AT) for c in SPLIT_AT[s] + SPLIT_LATE.get(s, [])]
OWN = sum(len(c) for s, c in SPLIT_AT.items() if s < SPLIT_FROM)
BEFORE = TURN[OWN:]
WEIGHTS_FOR = {2 + h: [C_WO + h, C_WLO + h] for h in range(GH)}
WEIGHTS_FOR.update({14: [C_K, C_Q, C_LK], 15: [C_Q + 1], 16: [C_Q + 2], 17: [C_Q + 3]})
LVW = GH * HD + HD
HALF = LVW // 2

M0 = 4
INTER = 1376
M1 = -(-INTER // P)
F0_CHUNKS = (KC * 2 * M0 * P + M0 * DIM) // CH
F1_COLS = KC * P + 2 * M1 * P + M1 * P + DIM
F1_CHUNKS = -(-F1_COLS // CH)

HEADS1, D1 = 32, 16
GR1, HG1 = 4, 8
A1_CHUNKS = (KC * 3 * DIM + KC * DIM) // CH

W_F0A = 0
W_LQ = W_F0A + F0_CHUNKS
W_A0 = W_LQ + 1
W_F0B = W_A0 + KVH * G_CHUNKS
W_F1 = W_F0B + F0_CHUNKS
W_A1 = W_F1 + F1_CHUNKS
W_ALL = W_A1 + A1_CHUNKS
TAIL = TURN[:OWN] + [c for c in TURN[OWN:] if c < F0_CHUNKS]

T_ID = 0
T_M0 = T_ID + P
T_M1 = T_M0 + 3 * P
T_COS = T_M1 + 3 * P
T_SIN = T_COS + 2 * SEQ
T_R1 = T_SIN + 2 * SEQ
T_EO = T_R1 + 4 * 2 * D1
T_MH = T_EO + 2
T_ALL = T_MH + 2

B_12 = 0
B_1 = B_12 + 2 * M0
B_ALL = B_1 + 2 * M1
RAW = 4


def constants():
    t = np.zeros((P, T_ALL), np.float32)
    t[:, T_ID:T_ID + P] = np.eye(P, dtype=np.float32)
    future = (np.arange(P)[None, :] > np.arange(P)[:, None]).astype(np.float32)
    for at, value in ((T_M0, 1e30), (T_M1, 66504.0)):
        t[:, at:at + P] = future * np.float32(value)
        t[:, at + 2 * P:at + 3 * P] = future * np.float32(value)
    inv = (1.0 / np.float32(10000.0) ** (np.arange(0, HD, 2, dtype=np.float32) / np.float32(HD))).astype(np.float32)
    ang = np.outer(np.arange(SEQ, dtype=np.float32), inv).astype(np.float32)
    cos = np.concatenate([np.cos(ang), np.cos(ang)], 1).T
    sin = np.concatenate([-np.sin(ang), np.sin(ang)], 1).T
    scale = np.float32(-1.0 / np.sqrt(HD))
    t[:, T_COS:T_COS + SEQ] = cos * scale
    t[:, T_COS + SEQ:T_COS + 2 * SEQ] = cos
    t[:, T_SIN:T_SIN + SEQ] = sin * scale
    t[:, T_SIN + SEQ:T_SIN + 2 * SEQ] = sin
    half = D1 // 2
    inv = (1.0 / np.float32(10000.0) ** (np.arange(0, half, dtype=np.float32) / np.float32(half))).astype(np.float32)
    ang = (np.arange(SEQ, dtype=np.float32)[:, None] * inv[None, :]).astype(np.float32)
    c1 = np.concatenate([np.cos(ang), np.cos(ang)], 1).reshape(2, P, D1).transpose(1, 0, 2)
    s1 = np.concatenate([-np.sin(ang), np.sin(ang)], 1).reshape(2, P, D1).transpose(1, 0, 2)
    t[:, T_R1:T_R1 + 8 * D1] = np.stack([c1 * np.float32(-0.25), s1 * np.float32(-0.25), c1, s1], 1).reshape(P, 8 * D1)
    t[:, T_EO] = (np.arange(P) % 32 < D1)
    t[:, T_EO + 1] = (np.arange(P) % 32 >= D1)
    t[:, T_MH:T_MH + 2] = -0.5
    return t


def program(nc, x_in, w_in, table_in, bias_in, rows_in, out):
    ctx = ExitStack()
    with ctx:
        def sem(name):
            return ctx.enter_context(nc.semaphore(name))

        def sb(scope, name, shape, dt=F32):
            return scope.enter_context(nc.sbuf_tensor(name, shape, dt))

        x = sb(ctx, "x", [P, TILES, DIM])
        table = sb(ctx, "table", [P, T_ALL])
        biases = sb(ctx, "biases", [P, B_ALL])
        row = sb(ctx, "row", [P, DIM])
        raw = sb(ctx, "raw", [P, RAW, CH])
        work = sb(ctx, "work", [P, 4, CH])
        stats = sb(ctx, "stats", [P, 2, 6])
        mean_var = sb(ctx, "mean_var", [P, 2, 2])
        var_eps = sb(ctx, "var_eps", [P, 2])
        rstd = sb(ctx, "rstd", [P, 2])
        neg_max = sb(ctx, "neg_max", [P, 4, 2])
        row_sum = sb(ctx, "row_sum", [P, 4, 2])
        inv_sum = sb(ctx, "inv_sum", [P, 4, 2])
        W = [sb(ctx, f"W{i}", [P, G_CHUNKS * CH], F32R) for i in (HI, LO)]
        with ExitStack() as a:
            xnT = [sb(a, f"xnT{i}", [P, KC, TOKENS], F32R) for i in (HI, LO)]
            with ExitStack() as s:
                WF0 = [sb(s, f"WF0_{i}", [P, F0_CHUNKS * CH], F32R) for i in (HI, LO)]
                h0 = [sb(s, f"h0_{i}", [P, 2, CH], F32R) for i in (HI, LO)]
            with ExitStack() as s:
                qk = [sb(s, f"qk{i}", [P, 6, SEQ], F32R) for i in (HI, LO)]
                lvv = sb(s, "lvv", [P, 2, LVW])
                pt0 = sb(s, "pt0", [P, 2, 3 * P])
                oT0 = [sb(s, f"oT0_{i}", [P, 4, SEQ], F32R) for i in (HI, LO)]
                lqT = [sb(s, f"lqT{i}", [P, TOKENS], F32R) for i in (HI, LO)]
                s0 = sb(s, "s0", [P, 4, 3 * P])
            with ExitStack() as s:
                WF1 = [sb(s, f"WF1_{i}", [P, F1_CHUNKS * CH], F32R) for i in (HI, LO)]
                h1 = [sb(s, f"h1_{i}", [P, 2, CH], F32R) for i in (HI, LO)]
                pz = [sb(s, f"pz{i}", [P, CH], F32R) for i in (HI, LO)]
        with ExitStack() as a:
            xb = [sb(a, f"xb{i}", [P, KC, SEQ], F32R) for i in (HI, LO)]
            qE = [sb(a, f"qE{i}", [P, 2, 2, SEQ], F32R) for i in (HI, LO)]
            k1 = [sb(a, f"k1_{i}", [P, 2, SEQ], F32R) for i in (HI, LO)]
            vz = [sb(a, f"vz{i}", [P, 2, 2, HG1, P], F32R) for i in (HI, LO)]
            pt1 = [sb(a, f"pt1_{i}", [P, 2, 4 * P], F32R) for i in (HI, LO)]
            oT1 = [sb(a, f"oT1_{i}", [P, GR1, SEQ], F32R) for i in (HI, LO)]
            qkv = sb(a, "qkv", [P, 2, 3 * DIM])
            s1 = sb(a, "s1", [P, 2, 3 * P])
            bqkv = sb(a, "bqkv", [P, 3 * DIM])

        bank = [ctx.enter_context(nc.psum_tensor(f"bank{i}", [P, CH], F32)) for i in range(8)]
        ident = table[:, T_ID:T_ID + P]

        x_loaded = [sem(f"x_loaded{t}") for t in range(TILES)]
        table_loaded = sem("table_loaded")
        row_loaded = sem("row_loaded")
        bqkv_loaded = sem("bqkv_loaded")
        stored = sem("stored")
        x_written = sem("x_written")
        passed = sem("passed")

        raw_loaded = [sem(f"raw_loaded{i}") for i in range(RAW)]
        w_hi = sem("w_hi")
        w_split = sem("w_split")

        class Stream:

            used = [0] * RAW
            last = [None] * RAW
            done = 0

            def __init__(self, n, turns=1):
                self.n, self.turns, self.base, self.at = n, turns, Stream.done, []
                per = [len(range(s, n, RAW)) for s in range(RAW)]
                for j in range(n):
                    s = j % RAW
                    before = Stream.used[s] + j // RAW
                    if j >= RAW:
                        prev = Stream.done + j - RAW
                    elif turns > 1:
                        prev = Stream.done - n + max(range(s, n, RAW))
                        assert Stream.last[s] is not None and Stream.last[s] <= Stream.done
                        prev = max(prev, Stream.last[s])
                    else:
                        prev = Stream.last[s]
                    self.at.append((s, before, per[s], prev))
                for s in range(RAW):
                    if per[s]:
                        Stream.last[s] = Stream.done + n * (turns - 1) + max(range(s, n, RAW))
                    Stream.used[s] += per[s] * turns
                Stream.done += n * turns

            def load(self, sp, j, source, g=None):
                s, before, per, prev = self.at[j]
                turn = 0 if g is None else g
                if prev is not None:
                    sp.wait_ge(w_split, prev + 1 + turn * self.n)
                sp.dma_start(raw[:, s, :], source).then_inc(raw_loaded[s], 16)

            def split_hi(self, act, j, dst, g=None):
                s, before, per, _ = self.at[j]
                turn = 0 if g is None else g
                act.wait_ge(raw_loaded[s], 16 * (before + 1) + turn * (16 * per))
                nc.scalar.copy(dst[HI], raw[:, s, :]).then_inc(w_hi, 1)

            def split_lo(self, dve, j, dst, g=None):
                s = self.at[j][0]
                turn = 0 if g is None else g
                dve.wait_ge(w_hi, self.base + j + 1 + turn * self.n)
                nc.vector.tensor_tensor(dst[LO], raw[:, s, :], dst[HI].bitcast(F32),
                                        ALU.subtract).then_inc(w_split, 1)

            def ready(self, eng, j, g=None):
                turn = 0 if g is None else g
                eng.wait_ge(w_split, self.base + j + 1 + turn * self.n)

        def chunk(w, c):
            return [w[i][:, c * CH:(c + 1) * CH] for i in (HI, LO)]

        st_f0a = Stream(F0_CHUNKS)
        st_lq = Stream(1)
        st_a0 = Stream(len(BEFORE))
        st_loop = Stream(G_CHUNKS, KVH - 1)
        st_tail = Stream(len(TAIL))
        st_f1a = Stream(F1_CHUNKS)
        st_a1 = Stream(A1_CHUNKS)
        st_f1b = Stream(F1_CHUNKS)

        ln_stat = sem("ln_stat")
        ln_var = sem("ln_var")
        ln_rstd = sem("ln_rstd")
        ln_xn = sem("ln_xn")
        ln_turned = sem("ln_turned")
        ln_hi = sem("ln_hi")
        ln_done = sem("ln_done")

        def at_least(eng, s, value):
            if not isinstance(value, int) or value > 0:
                eng.wait_ge(s, value)

        def ln_normalise(dve, n, slot, xt):
            nc.vector.bn_stats(stats[:, slot, :], xt).then_inc(ln_stat, 1)
            dve.wait_ge(ln_stat, n * 2 + 1)
            dve.sem_inc(passed, 1)
            nc.vector.bn_aggr(mean_var[:, slot, :], stats[:, slot, :]).then_inc(ln_stat, 1)
            dve.wait_ge(ln_stat, n * 2 + 2)
            nc.vector.tensor_scalar(var_eps[:, slot:slot + 1], mean_var[:, slot, 1:2], EPS, None,
                                    ALU.add).then_inc(ln_var, 1)
            dve.wait_ge(ln_rstd, n + 1)
            at_least(dve, ln_turned, n - 1)
            nc.vector.tensor_scalar(work[:, slot, :], xt, mean_var[:, slot, 0:1],
                                    rstd[:, slot:slot + 1], ALU.subtract, ALU.mult).then_inc(ln_xn, 1)

        def ln_power(pool, n, slot):
            pool.wait_ge(ln_var, n + 1)
            nc.gpsimd.tensor_tensor(rstd[:, slot:slot + 1], var_eps[:, slot:slot + 1],
                                    table[:, T_MH:T_MH + 1], ALU.pow).then_inc(ln_rstd, 1)

        def ln_turn(pe, n, slot, b):
            pe.wait_ge(ln_xn, n + 1)
            at_least(pe, ln_done, n)
            for c in range(KC):
                last = nc.tensor.transpose(bank[b][:, c * P:(c + 1) * P],
                                           work[:, slot, c * P:(c + 1) * P], ident)
            last.then_inc(ln_turned, 1)

        def turned(b):
            return bank[b][:, :].rearrange("p (c n) -> p c n", c=KC)

        def ln_hi_part(act, n, b, dst):
            act.wait_ge(ln_turned, n + 1)
            nc.scalar.copy(dst[HI], turned(b)).then_inc(ln_hi, 1)

        def ln_lo_part(dve, n, b, dst):
            dve.wait_ge(ln_hi, n + 1)
            nc.vector.tensor_tensor(dst[LO], turned(b), dst[HI].bitcast(F32),
                                    ALU.subtract).then_inc(ln_done, 1)

        def xnT_tile(t):
            return [xnT[i][:, :, t * P:(t + 1) * P] for i in (HI, LO)]

        def product(out_ap, lhs, rhs, start=True, stop=True):
            for k, (i, j) in enumerate(PASSES):
                last = nc.tensor.matmul(out_ap, lhs(i), rhs(j), start=start and k == 0,
                                        stop=stop and k == 2)
            return last

        f_ready = sem("f_ready")
        f_silu = sem("f_silu")
        f_mul = sem("f_mul")
        f_hi = sem("f_hi")
        f_lo = sem("f_lo")
        f_used = sem("f_used")
        f_out = sem("f_out")
        pz_ready = sem("pz_ready")
        pz_hi = sem("pz_hi")
        pz_lo = sem("pz_lo")
        RING, LNB, ZB = (0, 1, 2), 3, 4

        class FFN:

            m_all, o_all, u_all, z_all = 0, 0, 0, 0

            def __init__(self, layer, w, h, ln0, ln_next, x_before, row_n, first, own=(), beside=(),
                         needs=None):
                self.layer, self.w, self.h = layer, w, h
                self.M = M0 if layer == 0 else M1
                self.m0, self.o0, self.u0, self.z0 = FFN.m_all, FFN.o_all, FFN.u_all, FFN.z_all
                FFN.m_all += 2 * self.M
                FFN.o_all += TILES
                FFN.u_all += 2 * (self.M - 1)
                FFN.z_all += 4 if layer else 0
                self.out_banks = (4, 5, 6, 7) if layer == 0 else (5, 6, 7)
                self.ln0, self.ln_next, self.row_n, self.first = ln0, ln_next, row_n, first
                self.x_before = x_before
                self.needs = needs
                self.own = own
                self.beside = beside

            def gate_up(self, m, up, c):
                if self.layer == 0:
                    at = c * 2 * M0 * P + (up * M0 + m) * P
                else:
                    at = KC * P + (up * M1 + m) * P
                return lambda i: self.w[i][:, at:at + P]

            def down(self, m):
                if self.layer == 0:
                    at = KC * 2 * M0 * P + m * DIM
                    return lambda i: self.w[i][:, at:at + DIM]
                at = KC * P + 2 * M1 * P + m * P
                return lambda i: self.w[i][:, at:at + P]

            def bias(self, m, up):
                at = (B_12 + up * M0 + m) if self.layer == 0 else (B_1 + up * M1 + m)
                return biases[:, at:at + 1]

            def bank_of(self, o):
                return self.out_banks[(o - self.o0) % len(self.out_banks)]

            def ln_tiles(self, k, m):
                if m >= 4 or (k == 1 and self.ln_next is None):
                    return []
                return [(self.ln0 + 4 + m, 4 + m)] if k == 0 else [(self.ln_next + m, m)]

            def splits(self, k, m):
                at, per = k * self.M + m, -(-len(self.beside) // (2 * self.M))
                return self.beside[at * per:(at + 1) * per]

            def tensor(self, pe):
                M = self.M
                if self.first:
                    for t in range(4):
                        ln_turn(pe, self.ln0 + t, t % 2, LNB)
                at_least(pe, x_written, self.x_before)
                for k in range(2):
                    cols = slice(k * CH, k * CH + CH)
                    pe.wait_ge(ln_done, self.ln0 + 4 * k + 4)
                    if k == 0:
                        stream, j = self.needs or self.own[-1][:2]
                        stream.ready(pe, j)
                    z = self.z0 + 2 * k
                    if self.layer:
                        at_least(pe, pz_lo, z)
                        for c in range(KC):
                            last = product(bank[ZB][:, :], lambda i: self.w[i][:, c * P:(c + 1) * P],
                                           lambda i: xnT[i][:, c, cols], c == 0, c == KC - 1)
                        last.then_inc(pz_ready, 1)
                        pe.wait_ge(pz_lo, z + 1)
                    for m in range(M + 1):
                        if m < M:
                            self.tensor_gate_up(pe, k, m, cols)
                        if m > 0:
                            self.tensor_down(pe, k, m - 1)
                        if m < M:
                            for n, t in self.ln_tiles(k, m):
                                ln_turn(pe, n, t % 2, LNB)
                    if self.layer:
                        pe.wait_ge(pz_lo, z + 2)
                        for t in range(4):
                            o = 4 * k + t
                            if o >= 3:
                                pe.wait_ge(x_written, self.x_before + 2 * (o - 3) + 2)
                            at = F1_COLS - DIM
                            product(bank[self.bank_of(self.o0 + o)][:, :],
                                    lambda i: pz[i][:, t * P:(t + 1) * P],
                                    lambda i: self.w[i][:, at:at + DIM]).then_inc(f_out, 1)

            def tensor_gate_up(self, pe, k, m, cols):
                q = self.m0 + k * self.M + m
                for up in (0, 1):
                    f = 2 * q + up
                    prev = f - len(RING)
                    if prev >= 0 and prev % 2:
                        pe.wait_ge(f_mul, prev // 2 + 1)
                    elif prev >= 0:
                        pe.wait_ge(f_silu, prev // 2 + 1)
                    dst = bank[RING[f % len(RING)]][:, :]
                    if self.layer == 0:
                        for c in range(KC):
                            last = product(dst, self.gate_up(m, up, c), lambda i: xnT[i][:, c, cols],
                                           c == 0, c == KC - 1)
                    else:
                        last = product(dst, self.gate_up(m, up, 0), lambda i: pz[i][:, :])
                    last.then_inc(f_ready, 1)

            def tensor_down(self, pe, k, m):
                q = self.m0 + k * self.M + m
                pe.wait_ge(f_lo, q + 1)
                first, end = m == 0, m == self.M - 1
                if self.layer == 0:
                    for t in range(4):
                        if first and k == 1:
                            pe.wait_ge(x_written, self.x_before + 2 * t + 2)
                        last = product(bank[self.out_banks[t]][:, :],
                                       lambda i: self.h[i][:, q % 2, t * P:(t + 1) * P], self.down(m),
                                       first, end)
                        if end:
                            last.then_inc(f_out, 1)
                else:
                    last = product(bank[ZB][:, :], self.down(m), lambda i: self.h[i][:, q % 2, :],
                                   first, end)
                    if end:
                        last.then_inc(pz_ready, 1)
                if not end:
                    last.then_inc(f_used, 1)

            def scalar(self, act):
                M = self.M
                if self.first:
                    for t in range(4):
                        ln_hi_part(act, self.ln0 + t, LNB, xnT_tile(t))
                for st, j, dst in self.own:
                    st.split_hi(act, j, dst)
                for k in range(2):
                    if self.layer:
                        self.low_rank_hi(act, self.z0 + 2 * k)
                    for m in range(M + 1):
                        q = self.m0 + k * M + m
                        if m < M:
                            act.wait_ge(f_ready, 2 * q + 1)
                            at_least(act, f_lo, q - 1)
                            nc.scalar.activation(work[:, 2 + q % 2, :], bank[RING[(2 * q) % 3]][:, :],
                                                 ACT.Silu, bias=self.bias(m, 0)).then_inc(f_silu, 1)
                        if m > 0:
                            q -= 1
                            act.wait_ge(f_mul, q + 1)
                            if m > 2:
                                act.wait_ge(f_used, self.u0 + k * (M - 1) + m - 2)
                            nc.scalar.copy(self.h[HI][:, q % 2, :], work[:, 2 + q % 2, :]).then_inc(f_hi, 1)
                        if m < M:
                            for n, t in self.ln_tiles(k, m):
                                if k == 1:
                                    act.wait_ge(f_ready, 2 * (self.m0 + M))
                                ln_hi_part(act, n, LNB, xnT_tile(t))
                            for st, j, dst in self.splits(k, m):
                                st.split_hi(act, j, dst)
                    if self.layer:
                        self.low_rank_hi(act, self.z0 + 2 * k + 1)

            def low_rank_hi(self, act, z):
                act.wait_ge(pz_ready, z + 1)
                nc.scalar.copy(pz[HI][:, :], bank[ZB][:, :]).then_inc(pz_hi, 1)

            def vector(self, dve):
                M = self.M

                def normalise(k, n, t):
                    if self.x_before == 0 and n < TILES:
                        dve.wait_ge(x_loaded[t], 16)
                    elif n < self.ln0 + TILES:
                        dve.wait_ge(x_written, self.x_before)
                    else:
                        dve.wait_ge(x_written, self.x_before + 2 * (t + 1))
                    ln_normalise(dve, n, t % 2, x[:, t, :])

                if self.first:
                    for t in range(5):
                        if t < 4:
                            normalise(0, self.ln0 + t, t)
                        if t > 0:
                            ln_lo_part(dve, self.ln0 + t - 1, LNB, xnT_tile(t - 1))
                for st, j, dst in self.own:
                    st.split_lo(dve, j, dst)
                for k in range(2):
                    if self.layer:
                        self.low_rank_lo(dve, self.z0 + 2 * k)
                    for m in range(M + 1):
                        q = self.m0 + k * M + m
                        tiles = self.ln_tiles(k, m) if m < M else []
                        for n, t in tiles:
                            normalise(k, n, t)
                        if m < M:
                            dve.wait_ge(f_ready, 2 * q + 2)
                            dve.wait_ge(f_silu, q + 1)
                            w = work[:, 2 + q % 2, :]
                            nc.vector.scalar_tensor_tensor(w, bank[RING[(2 * q + 1) % 3]][:, :],
                                                           self.bias(m, 1), w, ALU.add,
                                                           ALU.mult).then_inc(f_mul, 1)
                        if m > 0:
                            q -= 1
                            dve.wait_ge(f_hi, q + 1)
                            nc.vector.tensor_tensor(self.h[LO][:, q % 2, :], work[:, 2 + q % 2, :],
                                                    self.h[HI][:, q % 2, :].bitcast(F32),
                                                    ALU.subtract).then_inc(f_lo, 1)
                        for n, t in tiles:
                            ln_lo_part(dve, n, LNB, xnT_tile(t))
                        if m < M:
                            for st, j, dst in self.splits(k, m):
                                st.split_lo(dve, j, dst)
                    if self.layer:
                        self.low_rank_lo(dve, self.z0 + 2 * k + 1)
                    for t in range(4 * k, 4 * k + 4):
                        xt = x[:, t, :]
                        before = self.x_before + 2 * t
                        dve.wait_ge(row_loaded, 16 * (self.row_n + 1))
                        dve.wait_ge(ln_xn, self.ln0 + t + 1)
                        nc.vector.scalar_tensor_tensor(xt, row[:, :], 0.5, xt, ALU.mult,
                                                       ALU.add).then_inc(x_written, 1)
                        dve.wait_ge(x_written, before + 1)
                        dve.wait_ge(f_out, self.o0 + t + 1)
                        nc.vector.scalar_tensor_tensor(xt, bank[self.bank_of(self.o0 + t)][:, :], 0.5, xt,
                                                       ALU.mult, ALU.add).then_inc(x_written, 1)

            def low_rank_lo(self, dve, z):
                dve.wait_ge(pz_hi, z + 1)
                nc.vector.tensor_tensor(pz[LO][:, :], bank[ZB][:, :], pz[HI][:, :].bitcast(F32),
                                        ALU.subtract).then_inc(pz_lo, 1)

            def gpsimd(self, pool):
                if self.first:
                    for t in range(4):
                        ln_power(pool, self.ln0 + t, t % 2)
                for k in range(2):
                    for m in range(self.M):
                        for n, t in self.ln_tiles(k, m):
                            ln_power(pool, n, t % 2)

        def lot(stream, w, columns):
            return [(stream, j, chunk(w, c)) for j, c in enumerate(columns)]

        X1 = 2 * TILES
        X2 = X1 + 1
        X3, X4 = X2 + 2 * TILES, X2 + 4 * TILES
        X5 = X4 + 1
        ffn0a = FFN(0, WF0, h0, 0, 8, 0, 0, True, lot(st_f0a, WF0, range(F0_CHUNKS)),
                    lot(st_lq, W, [C_WO + 3]) + lot(st_a0, W, BEFORE))
        ffn0b = FFN(0, W, h0, 16, 24, X2, 1, True, (), lot(st_f1a, WF1, range(F1_CHUNKS)),
                    (st_tail, len(TAIL) - 1))
        ffn1a = FFN(1, WF1, h1, 24, None, X3, 2, False, (), lot(st_a1, W, range(A1_CHUNKS)),
                    (st_f1a, F1_CHUNKS - 1))
        ffn1b = FFN(1, WF1, h1, 40, None, X5, 4, True, lot(st_f1b, WF1, range(F1_CHUNKS)), ())

        a_proj = sem("a_proj")
        a_proj_free = sem("a_proj_free")
        a_swapped = sem("a_swapped")
        a_sin = sem("a_sin")
        a_rope = sem("a_rope")
        a_rope_hi = sem("a_rope_hi")
        a_rope_lo = sem("a_rope_lo")
        a_scores = sem("a_scores")
        a_min = sem("a_min")
        a_exp = sem("a_exp")
        a_inv = sem("a_inv")
        a_norm = sem("a_norm")
        a_turned = sem("a_turned")
        a_pt = sem("a_pt")
        a_pv = sem("a_pv")
        a_o_hi = sem("a_o_hi")
        a_o_lo = sem("a_o_lo")
        a_out = sem("a_out")
        a_added = sem("a_added")
        a_lq = sem("a_lq")
        a_lq_hi = sem("a_lq_hi")
        a_lq_lo = sem("a_lq_lo")
        PT, OB, OUTB = 4, 5, (6, 7)
        STEPS0 = BATCH * GH
        FILLS, ROPES = 9, 5
        AHEAD = 3

        class Step:

            def __init__(self, g, s):
                self.g, self.s = g, s
                self.batch, self.h = divmod(s, GH)
                self.first = isinstance(g, int) and g == 0 and s < 1
                self.second = isinstance(g, int) and g == 0 and s < 2
                self.last_group = isinstance(g, int) and g == KVH - 1
                self.heads = not (self.last_group and s >= STEPS0)
                self.queries = not (self.last_group and s >= STEPS0 - 2)
                self.key = self.queries and self.h == GH - 2
                self.tokens = slice(self.batch % BATCH * SEQ, (self.batch % BATCH + 1) * SEQ)
                self.added = 1 + 2 * self.batch + g * (2 * BATCH)

            def near(self, d):
                return Step(self.g, self.s + d)

            def number(self):
                return self.g * STEPS0 + self.s

            def inst(self, k):
                return self.g * (2 * STEPS0) + (2 * self.s + k), (2 * self.s + k) % 4

            def fill(self, what):
                i = 6 if what == "k" else (0, 5, 7, 8)[self.h] if what == "q" else 1 + what
                n = FILLS * self.batch + i + AHEAD
                return self.g * (BATCH * FILLS) + n, n % 2

            def rope(self, what):
                i = 2 if what == "k" else (0, 1, 3, 4)[self.h]
                n = ROPES * self.batch + i + AHEAD
                return self.g * (BATCH * ROPES) + n, n % 2

            def columns(self, what):
                return slice(SEQ, 2 * SEQ) if what == "k" else slice(0, 2 * SEQ)

            def target(self, what):
                if what == "k":
                    at = 4 + self.near(2).batch % 2
                    return [qk[i][:, at, :] for i in (HI, LO)]
                at = 2 * (self.h % 2)
                return [qk[i][:, at:at + 2, :].rearrange("p a n -> p (a n)") for i in (HI, LO)]

        def a0_run(eng, step):
            step(Step(0, 0))
            step(Step(0, 1))
            with eng.Fori(0, KVH - 1) as g:
                for s in range(2, STEPS0 + 2):
                    step(Step(g, s))
            for s in range(2, STEPS0 + 2):
                step(Step(KVH - 1, s))

        def step_splits(st, late):
            s = st.s
            if s < 2:
                return []
            stream, turn = (st_tail, TAIL) if st.last_group else (st_loop, TURN)
            chunks = (SPLIT_LATE if late else SPLIT_AT).get(s, [])
            return [(stream, turn.index(c), chunk(W, c)) for c in chunks if c in turn]

        def weights(pe, st, chunks):
            if st.s < 2 or not chunks or (st.last_group and st.s >= SPLIT_FROM):
                return
            at = max(TURN.index(c) + 1 - (G_CHUNKS if st.s < SPLIT_FROM and c in TURN[OWN:] else 0)
                     for c in chunks)
            stream = st_tail if st.last_group else st_loop
            pe.wait_ge(w_split, stream.base + at + (0 if st.last_group else st.g * G_CHUNKS))

        def a0_tensor(pe):
            for t in range(4, TILES):
                ln_turn(pe, 8 + t, t % 2, LNB)
            pe.wait_ge(ln_done, 16)
            st_lq.ready(pe, 0)
            for i in range(2):
                for c in range(KC):
                    at = (C_WO + 3) * CH + c * P
                    last = product(bank[OUTB[i]][:, :], lambda p: W[p][:, at:at + P],
                                   lambda p: xnT[p][:, c, i * CH:(i + 1) * CH], c == 0, c == KC - 1)
                last.then_inc(a_lq, 1)
            pe.wait_ge(a_lq_lo, 2)
            st_a0.ready(pe, len(BEFORE) - 1)
            a0_keys(pe, Step(0, -2))
            a0_queries(pe, Step(0, -2))
            a0_queries(pe, Step(0, -1))
            a0_run(pe, lambda st: a0_tensor_step(pe, st))

        def a0_claim(pe, st, what):
            n, s = st.fill(what)
            pe.wait_ge(a_proj_free, n + 1)
            return bank[s]

        def a0_keys(pe, st):
            dst, to = a0_claim(pe, st, "k"), st.near(2)
            for c in range(KC):
                w = C_K * CH + c * P
                last = product(dst[:, SEQ:2 * SEQ], lambda p: W[p][:, w:w + P],
                               lambda p: xnT[p][:, c, to.tokens], c == 0, c == KC - 1)
            last.then_inc(a_proj, 1)

        def a0_queries(pe, st):
            dst, to = a0_claim(pe, st, "q"), st.near(2)
            for c in range(KC):
                w = (C_Q + to.h) * CH + c * P
                product(dst[:, 0:SEQ], lambda p: W[p][:, w:w + P],
                        lambda p: xnT[p][:, c, to.tokens], c == 0, c == KC - 1)
            w = C_LK * CH + to.h * P
            product(dst[:, SEQ:2 * SEQ], lambda p: W[p][:, w:w + P],
                    lambda p: lqT[p][:, to.tokens]).then_inc(a_proj, 1)

        def a0_values(pe, st):
            for i in range(4):
                tt, half = divmod(i, 2)
                dst = a0_claim(pe, st, i)
                t = st.tokens.start + tt * P
                for c in range(KC):
                    w = C_LVV * CH + c * LVW + half * HALF
                    last = product(dst[:, 0:HALF], lambda p: xnT[p][:, c, t:t + P],
                                   lambda p: W[p][:, w:w + HALF], c == 0, c == KC - 1)
                last.then_inc(a_proj, 1)

        def score_columns(k, qt):
            n = (qt + 1) * P
            return bank[2 + qt][:, (1 - k) * n:(2 - k) * n]

        def a0_tensor_step(pe, st):
            def scores():
                pe.wait_ge(a_rope_lo, st.near(-2).rope("q")[0] + 3)
                pe.wait_ge(a_min, st.inst(1)[0] + 1)
                q, k = 2 * (st.h % 2), 4 + st.batch % 2
                pair = slice(q + 1, k + 1, k - q - 1)
                for qt in range(2):
                    n = (qt + 1) * P
                    dst = bank[2 + qt][:, 0:2 * n].rearrange("p (a n) -> p a n", a=2)
                    last = product(dst, lambda p: qk[p][:, q, qt * P:(qt + 1) * P],
                                   lambda p: qk[p][:, pair, 0:n])
                last.then_inc(a_scores, 1)

            def turn(k):
                n, s = st.near(-1).inst(k)
                pe.wait_ge(a_norm, n + 1)
                pe.wait_ge(a_pt, n + 1)
                for blk in range(3):
                    last = nc.tensor.transpose(bank[PT][:, blk * P:(blk + 1) * P],
                                               s0[:, s, blk * P:(blk + 1) * P], ident)
                last.then_inc(a_turned, 1)

            def weigh(k):
                before = st.near(-1)
                n, _ = before.inst(k)
                col = before.h * P if k else GH * P
                if before.h == 0 and k == 0:
                    pe.wait_ge(a_proj_free, before.fill(3)[0] + 3)
                pe.wait_ge(a_pt, n + 2)
                pe.wait_ge(a_o_lo, n + 1)
                nc.tensor.matmul(bank[OB][:, 0:SEQ], lvv[:, 0, col:col + P], pt0[:, k, 0:2 * P],
                                 start=True, stop=False)
                nc.tensor.matmul(bank[OB][:, P:SEQ], lvv[:, 1, col:col + P], pt0[:, k, 2 * P:3 * P],
                                 start=False, stop=True).then_inc(a_pv, 1)

            def output(k):
                done = st.near(-2)
                n, s = done.inst(k)
                first, end = done.h == 0 and k == 0, done.h == GH - 1 and k == 1
                if first:
                    pe.wait_ge(a_added, done.added)
                pe.wait_ge(a_o_lo, n + 2)
                w = ((C_WLO if k else C_WO) + done.h) * CH
                for tt in range(2):
                    last = product(bank[OUTB[tt]][:, :], lambda p: oT0[p][:, s, tt * P:(tt + 1) * P],
                                   lambda p: W[p][:, w:w + CH], first, end)
                    if end:
                        last.then_inc(a_out, 1)

            lag1, lag2 = lagging(st), not st.second
            if lag1:
                turn(0)
            if st.heads:
                scores()
            if st.s in WEIGHTS_FOR:
                weights(pe, st, WEIGHTS_FOR[st.s])
            if st.key:
                a0_keys(pe, st)
            if lag1:
                weigh(0)
                turn(1)
            if st.queries:
                a0_queries(pe, st)
            if lag2:
                output(0)
            if lag1:
                weigh(1)
            if lag2:
                output(1)
            if st.h == 0 and st.heads:
                if st.s == STEPS0:
                    weights(pe, st, range(C_LVV, C_WO))
                a0_values(pe, st)

        def lagging(st):
            return not st.first and not (st.last_group and st.s == STEPS0 + 1)

        def a0_scalar(act):
            for t in range(4, TILES):
                ln_hi_part(act, 8 + t, LNB, xnT_tile(t))
            for i in range(2):
                act.wait_ge(a_lq, i + 1)
                nc.scalar.copy(lqT[HI][:, i * CH:(i + 1) * CH], bank[OUTB[i]][:, :]).then_inc(a_lq_hi, 1)
            a0_swap(act, Step(0, -2), "k")
            a0_swap(act, Step(0, -2), "q")
            a0_rope_hi(act, Step(0, -2), "k")
            a0_rope_hi(act, Step(0, -2), "q")
            a0_swap(act, Step(0, -1), "q")
            a0_run(act, lambda st: a0_scalar_step(act, st))

        def a0_swap(act, st, what):
            n, s = st.rope(what)
            f, fs = st.fill(what)
            cols, half = st.columns(what), P // 2
            act.wait_ge(a_proj, f + 1)
            act.wait_ge(a_rope_lo, n + 1)
            nc.scalar.copy(work[0:half, s, cols], bank[fs][half:P, cols])
            nc.scalar.copy(work[half:P, s, cols], bank[fs][0:half, cols]).then_inc(a_swapped, 1)

        def a0_rope_hi(act, st, what):
            n, s = st.rope(what)
            act.wait_ge(a_rope, n + 1)
            nc.scalar.copy(st.target(what)[HI], work[:, 2 + s, st.columns(what)]).then_inc(a_rope_hi, 1)

        def a0_scalar_step(act, st):
            before = st.near(-1)

            def exponentials(k):
                n, s = st.inst(k)
                act.wait_ge(a_min, n + 3)
                for qt, cols in ((0, slice(0, P)), (1, slice(P, 3 * P))):
                    last = nc.scalar.activation(s0[:, s, cols], s0[:, s, cols], ACT.Exp,
                                                bias=neg_max[:, s, qt:qt + 1], scale=-1.0,
                                                accum_out=row_sum[:, s, qt:qt + 1])
                last.then_inc(a_exp, 1)

            def turned_out(k):
                act.wait_ge(a_turned, before.inst(k)[0] + 1)
                nc.scalar.copy(pt0[:, k, :], bank[PT][:, 0:3 * P]).then_inc(a_pt, 1)

            def result_hi(k):
                n, s = before.inst(k)
                act.wait_ge(a_pv, n + 1)
                nc.scalar.copy(oT0[HI][:, s, :], bank[OB][:, 0:SEQ]).then_inc(a_o_hi, 1)

            turn_of = None if st.last_group else st.g
            if lagging(st):
                turned_out(0)
            if before.queries:
                a0_rope_hi(act, before, "q")
            if st.heads:
                exponentials(0)
            if st.key:
                a0_swap(act, st, "k")
            if st.heads:
                exponentials(1)
            if lagging(st):
                result_hi(0)
                turned_out(1)
            for stream, j, dst in step_splits(st, False):
                stream.split_hi(act, j, dst, turn_of)
            if st.key:
                a0_rope_hi(act, st, "k")
            if st.queries:
                a0_swap(act, st, "q")
            if lagging(st):
                result_hi(1)
            for stream, j, dst in step_splits(st, True):
                stream.split_hi(act, j, dst, turn_of)

        def a0_vector(dve):
            for s, n in ((a_proj_free, 2), (a_rope_lo, 2), (a_min, 2), (a_pt, 1), (a_o_lo, 1),
                         (a_added, 1)):
                dve.sem_inc(s, n)
            dve.wait_ge(x_written, X1)
            for t in range(4, TILES):
                ln_normalise(dve, 8 + t, t % 2, x[:, t, :])
                if t > 4:
                    ln_lo_part(dve, 7 + t, LNB, xnT_tile(t - 1))
            ln_lo_part(dve, 7 + TILES, LNB, xnT_tile(TILES - 1))
            for i in range(2):
                dve.wait_ge(a_lq_hi, i + 1)
                cols = slice(i * CH, (i + 1) * CH)
                nc.vector.tensor_tensor(lqT[LO][:, cols], bank[OUTB[i]][:, :], lqT[HI][:, cols].bitcast(F32),
                                        ALU.subtract).then_inc(a_lq_lo, 1)
            a0_cosine(dve, Step(0, -2), "k")
            a0_cosine(dve, Step(0, -2), "q")
            a0_rotate(dve, Step(0, -2), "k")
            a0_rotate(dve, Step(0, -2), "q")
            a0_cosine(dve, Step(0, -1), "q")
            a0_run(dve, lambda st: a0_vector_step(dve, st))
            dve.wait_ge(a_added, 1 + KVH * TILES)
            dve.sem_inc(x_written, 1)

        def a0_cosine(dve, st, what):
            n, s = st.rope(what)
            _, fs = st.fill(what)
            cols = st.columns(what)
            dve.wait_ge(a_swapped, n + 1)
            dve.wait_ge(a_rope_lo, n + 1)
            nc.vector.tensor_tensor(work[:, 2 + s, cols], bank[fs][:, cols],
                                    table[:, T_COS + cols.start:T_COS + cols.stop],
                                    ALU.mult).then_inc(a_proj_free, 1)

        def a0_rotate(dve, st, what):
            n, s = st.rope(what)
            cols = st.columns(what)
            dve.wait_ge(a_sin, n + 1)
            dve.wait_ge(a_proj_free, st.fill(what)[0] + 3)
            nc.vector.tensor_tensor(work[:, 2 + s, cols], work[:, 2 + s, cols], work[:, s, cols],
                                    ALU.add).then_inc(a_rope, 1)

        def a0_vector_step(dve, st):
            before = st.near(-1)

            def minima(k):
                _, s = st.inst(k)
                if k == 0:
                    dve.wait_ge(a_scores, st.number() + 1)
                    dve.sem_inc(passed, 1)
                nc.vector.tensor_tensor_reduce(s0[:, s, 0:P], score_columns(k, 0), table[:, T_M0:T_M0 + P],
                                               1.0, 3e38, ALU.add, ALU.min, neg_max[:, s, 0:1])
                nc.vector.tensor_tensor_reduce(s0[:, s, P:3 * P], score_columns(k, 1),
                                               table[:, T_M0 + P:T_M0 + 3 * P],
                                               1.0, 3e38, ALU.add, ALU.min,
                                               neg_max[:, s, 1:2]).then_inc(a_min, 1)

            def inverses(k):
                n, s = st.inst(k)
                dve.wait_ge(a_exp, n + 1)
                nc.vector.reciprocal(inv_sum[:, s, :], row_sum[:, s, :]).then_inc(a_inv, 1)

            def result_lo(k):
                n, s = before.inst(k)
                dve.wait_ge(a_o_hi, n + 1)
                nc.vector.tensor_tensor(oT0[LO][:, s, :], bank[OB][:, 0:SEQ], oT0[HI][:, s, :].bitcast(F32),
                                        ALU.subtract).then_inc(a_o_lo, 1)

            turn_of = None if st.last_group else st.g
            if before.queries:
                a0_rotate(dve, before, "q")
            if st.heads:
                minima(0)
                minima(1)
            if st.key:
                a0_cosine(dve, st, "k")
            if st.heads:
                inverses(0)
                inverses(1)
            if st.key:
                a0_rotate(dve, st, "k")
            if lagging(st):
                result_lo(0)
            for stream, j, dst in step_splits(st, False):
                stream.split_lo(dve, j, dst, turn_of)
            if st.queries:
                a0_cosine(dve, st, "q")
            if lagging(st):
                result_lo(1)
            if st.h == 1 and not st.second:
                done = st.near(-2)
                for tt in range(2):
                    xt = x[:, 2 * (done.batch % BATCH) + tt, :]
                    dve.wait_ge(a_out, done.added + tt)
                    nc.vector.tensor_tensor(xt, xt, bank[OUTB[tt]][:, :], ALU.add).then_inc(a_added, 1)
            if st.h == 0 and st.heads:
                for i in range(4):
                    tt, half = divmod(i, 2)
                    f, fs = st.fill(i)
                    dve.wait_ge(a_proj, f + 1)
                    nc.vector.tensor_copy(lvv[:, tt, half * HALF:(half + 1) * HALF],
                                          bank[fs][:, 0:HALF]).then_inc(a_proj_free, 1)
            for stream, j, dst in step_splits(st, True):
                stream.split_lo(dve, j, dst, turn_of)

        def a0_gpsimd(pool):
            for t in range(4, TILES):
                ln_power(pool, 8 + t, t % 2)
            a0_sine(pool, Step(0, -2), "k")
            a0_sine(pool, Step(0, -2), "q")
            a0_rope_lo(pool, Step(0, -2), "k")
            a0_rope_lo(pool, Step(0, -2), "q")
            a0_sine(pool, Step(0, -1), "q")
            a0_run(pool, lambda st: a0_gpsimd_step(pool, st))

        def a0_sine(pool, st, what):
            n, s = st.rope(what)
            cols = st.columns(what)
            pool.wait_ge(a_swapped, n + 1)
            nc.gpsimd.tensor_tensor(work[:, s, cols], work[:, s, cols],
                                    table[:, T_SIN + cols.start:T_SIN + cols.stop],
                                    ALU.mult).then_inc(a_sin, 1)

        def a0_rope_lo(pool, st, what):
            n, s = st.rope(what)
            pool.wait_ge(a_rope_hi, n + 1)
            hi, lo = st.target(what)
            nc.gpsimd.tensor_tensor(lo, work[:, 2 + s, st.columns(what)], hi.bitcast(F32),
                                    ALU.subtract).then_inc(a_rope_lo, 1)

        def a0_gpsimd_step(pool, st):
            if st.near(-1).queries:
                a0_rope_lo(pool, st.near(-1), "q")
            if st.key:
                a0_sine(pool, st, "k")
            for k in range(2 if st.heads else 0):
                n, s = st.inst(k)
                pool.wait_ge(a_inv, n + 1)
                nc.gpsimd.tensor_tensor(s0[:, s, 0:P], s0[:, s, 0:P],
                                        inv_sum[:, s, 0:1].to_broadcast([P, P]), ALU.mult)
                nc.gpsimd.tensor_tensor(s0[:, s, P:3 * P], s0[:, s, P:3 * P],
                                        inv_sum[:, s, 1:2].to_broadcast([P, 2 * P]),
                                        ALU.mult).then_inc(a_norm, 1)
            if st.key:
                a0_rope_lo(pool, st, "k")
            if st.queries:
                a0_sine(pool, st, "q")

        b_proj = sem("b_proj")
        b_proj_free = sem("b_proj_free")
        b_sin = sem("b_sin")
        b_cos = sem("b_cos")
        b_rope = sem("b_rope")
        b_k_hi = sem("b_k_hi")
        b_v_hi = sem("b_v_hi")
        b_v_lo = sem("b_v_lo")
        b_scores = sem("b_scores")
        b_min = sem("b_min")
        b_exp = sem("b_exp")
        b_inv = sem("b_inv")
        b_norm = sem("b_norm")
        b_turned = sem("b_turned")
        b_pt_hi = sem("b_pt_hi")
        b_pt_lo = sem("b_pt_lo")
        b_pv = sem("b_pv")
        b_o_hi = sem("b_o_hi")
        b_o_lo = sem("b_o_lo")
        b_out = sem("b_out")
        b_added = sem("b_added")
        b_zero = sem("b_zero")
        LN1 = 32
        FILLS1, STEPS = 6 + GR1, HEADS1 + 3

        def prep_at(j):
            grp = j // HG1 + 1
            return grp if j % HG1 == 3 and grp < GR1 else None

        def ends_at(j):
            return (j - 3) // HG1 if j >= 3 and (j - 3) % HG1 == HG1 - 1 else None

        def b_tensor(pe):
            pe.wait_ge(b_zero, 2)
            st_a1.ready(pe, A1_CHUNKS - 1)
            with pe.Fori(0, BATCH) as b:
                b_tensor_batch(pe, b)

        def b_tensor_batch(pe, b):
            def claim(i):
                pe.wait_ge(b_proj_free, b * FILLS1 + i + 1)
                return bank[i % 2]

            def prepare(grp):
                dst = claim(6 + grp)
                if grp == 0:
                    pe.wait_ge(b_rope, b * 4 + 4)
                for j in range(2):
                    for tt in range(2):
                        c = j * DIM + grp * P
                        last = nc.tensor.transpose(dst[:, j * SEQ + tt * P:j * SEQ + (tt + 1) * P],
                                                   qkv[:, tt, c:c + P], ident)
                last.then_inc(b_proj, 1)

            def scores(i):
                grp, hh = divmod(i, HG1)
                rows, eo, s = slice(32 * (hh // 2), 32 * (hh // 2) + 32), hh % 2, grp % 2
                if hh == 0:
                    pe.wait_ge(b_proj_free, b * FILLS1 + 6 + grp + 3)
                pe.wait_ge(b_min, b * HEADS1 + i + 1)
                for qt in range(2):
                    last = product(bank[2 + i % 2][:, qt * SEQ:(qt + 1) * SEQ],
                                   lambda p: qE[p][rows, s, eo, qt * P:(qt + 1) * P],
                                   lambda p: k1[p][rows, s, :])
                last.then_inc(b_scores, 1)

            def turn(i):
                pe.wait_ge(b_norm, b * HEADS1 + i + 1)
                pe.wait_ge(b_pt_lo, b * HEADS1 + i + 1)
                for blk in range(3):
                    last = nc.tensor.transpose(bank[PT][:, blk * P:(blk + 1) * P],
                                               s1[:, i % 2, blk * P:(blk + 1) * P], ident)
                last.then_inc(b_turned, 1)

            def weigh(i):
                grp, hh = divmod(i, HG1)
                if hh == 0:
                    pe.wait_ge(b_v_lo, b * GR1 + grp + 1)
                    pe.wait_ge(b_o_lo, b * GR1 + grp + 1)
                pe.wait_ge(b_pt_lo, b * HEADS1 + i + 2)
                for kt in range(2):
                    if kt == 0:
                        rhs = lambda p: pt1[p][:, i % 2, P:3 * P]
                    else:
                        rhs = lambda p: pt1[p][:, i % 2, :].rearrange("p (a n) -> p a n", n=P)[:, 0::3, :]
                    last = product(bank[OB][:, 0:SEQ], lambda p: vz[p][:, grp % 2, kt, hh, :], rhs,
                                   hh == 0 and kt == 0, hh == HG1 - 1 and kt == 1)
                if hh == HG1 - 1:
                    last.then_inc(b_pv, 1)

            def outputs(grp):
                pe.wait_ge(b_o_lo, b * GR1 + grp + 2)
                w = (KC * 3 + grp) * CH
                for tt in range(2):
                    last = product(bank[OUTB[tt]][:, :], lambda p: oT1[p][:, grp, tt * P:(tt + 1) * P],
                                   lambda p: W[p][:, w:w + CH], grp == 0, grp == GR1 - 1)
                    if grp == GR1 - 1:
                        last.then_inc(b_out, 1)

            for tt in range(2):
                ln_turn(pe, b * 2 + (LN1 + tt), tt, OUTB[tt])
            for tt in range(2):
                pe.wait_ge(ln_done, b * 2 + (LN1 + tt + 1))
                for j in range(3):
                    dst = claim(3 * tt + j)
                    for c in range(KC):
                        w = c * 3 * DIM + j * DIM
                        last = product(dst[:, :], lambda p: xb[p][:, c, tt * P:(tt + 1) * P],
                                       lambda p: W[p][:, w:w + DIM], c == 0, c == KC - 1)
                    last.then_inc(b_proj, 1)
            prepare(0)
            for j in range(STEPS):
                if 2 <= j < HEADS1 + 2:
                    turn(j - 2)
                if j < HEADS1:
                    scores(j)
                if j >= 3:
                    weigh(j - 3)
                if prep_at(j):
                    prepare(prep_at(j))
                if j % HG1 == 5 and j > HG1:
                    outputs(j // HG1 - 1)
            outputs(GR1 - 1)

        def b_scalar(act):
            act.wait_ge(b_zero, 2)
            with act.Fori(0, BATCH) as b:
                b_scalar_batch(act, b)

        def diagonal(t, s, tt):
            flat = t[:, s, tt, :, :].rearrange("p h (a d) -> p (h a) d", d=D1)
            return flat[:, 0::HG1 + 1, :]

        def values_of(grp, tt):
            c = 2 * DIM + grp * P
            return qkv[:, tt, c:c + P].rearrange("p (h d) -> p h d", d=D1)

        def b_scalar_batch(act, b):
            def prepare_hi(grp):
                s = grp % 2
                src = bank[(6 + grp) % 2]
                act.wait_ge(b_proj, b * FILLS1 + 6 + grp + 1)
                nc.scalar.copy(k1[HI][:, s, :], src[:, SEQ:2 * SEQ])
                for eo in range(2):
                    last = nc.scalar.activation(qE[HI][:, s, eo, :], src[:, 0:SEQ], ACT.Copy,
                                                scale=table[:, T_EO + eo:T_EO + eo + 1])
                last.then_inc(b_k_hi, 1)
                for tt in range(2):
                    last = nc.scalar.copy(diagonal(vz[HI], s, tt), values_of(grp, tt))
                last.then_inc(b_v_hi, 1)

            def exponentials(i):
                s = i % 2
                act.wait_ge(b_min, b * HEADS1 + i + 3)
                for qt, cols in ((0, slice(0, P)), (1, slice(P, 3 * P))):
                    last = nc.scalar.activation(s1[:, s, cols], s1[:, s, cols], ACT.Exp,
                                                bias=neg_max[:, s, qt:qt + 1], scale=-1.0,
                                                accum_out=row_sum[:, s, qt:qt + 1])
                last.then_inc(b_exp, 1)

            def turned_hi(i):
                act.wait_ge(b_turned, b * HEADS1 + i + 1)
                nc.scalar.copy(pt1[HI][:, i % 2, P:4 * P], bank[PT][:, 0:3 * P]).then_inc(b_pt_hi, 1)

            def result_hi(grp):
                act.wait_ge(b_pv, b * GR1 + grp + 1)
                nc.scalar.copy(oT1[HI][:, grp, :], bank[OB][:, 0:SEQ]).then_inc(b_o_hi, 1)

            for tt in range(2):
                ln_hi_part(act, b * 2 + (LN1 + tt), OUTB[tt], xb_tile(tt))
            prepare_hi(0)
            for j in range(STEPS):
                if 2 <= j < HEADS1 + 2:
                    turned_hi(j - 2)
                if j < HEADS1:
                    exponentials(j)
                if ends_at(j) is not None:
                    result_hi(ends_at(j))
                if prep_at(j):
                    prepare_hi(prep_at(j))

        def xb_tile(tt):
            return [xb[i][:, :, tt * P:(tt + 1) * P] for i in (HI, LO)]

        def b_vector(dve):
            for s, n in ((b_proj_free, 2), (b_min, 2), (b_pt_lo, 1), (b_o_lo, 1)):
                dve.sem_inc(s, n)
            dve.wait_ge(b_zero, 2)
            dve.wait_ge(x_written, X4)
            dve.wait_ge(bqkv_loaded, 16)
            dve.wait_ge(row_loaded, 16 * 4)
            with dve.Fori(0, BATCH) as b:
                b_vector_batch(dve, b)
            dve.wait_ge(b_added, 2 * TILES)
            dve.sem_inc(x_written, 1)

        def per_head(ap):
            return ap.rearrange("p (h d) -> p h d", d=D1)

        def angles(kind, tt):
            c = T_R1 + (kind * 2 + tt) * D1
            return table[:, c:c + D1].unsqueeze(1).to_broadcast([P, HEADS1, D1])

        def b_vector_batch(dve, b):
            def biased(tt, j):
                i = 3 * tt + j
                dve.wait_ge(b_proj, b * FILLS1 + i + 1)
                cols = slice(j * DIM, (j + 1) * DIM)
                nc.vector.tensor_tensor(qkv[:, tt, cols], bank[i % 2][:, :], bqkv[:, cols],
                                        ALU.add).then_inc(b_proj_free, 1)

            def cosine(tt, j):
                r = 2 * tt + j
                cols = slice(j * DIM, (j + 1) * DIM)
                dve.wait_ge(b_proj_free, b * FILLS1 + 3 * tt + j + 3)
                nc.vector.tensor_tensor(per_head(work[:, 2 + r % 2, :]), per_head(qkv[:, tt, cols]),
                                        angles(2 * j, tt), ALU.mult).then_inc(b_cos, 1)

            def rotate(tt, j):
                r = 2 * tt + j
                cols = slice(j * DIM, (j + 1) * DIM)
                dve.wait_ge(b_sin, b * 4 + r + 1)
                dve.wait_ge(b_cos, b * 4 + r + 1)
                nc.vector.tensor_tensor(qkv[:, tt, cols], work[:, 2 + r % 2, :], work[:, r % 2, :],
                                        ALU.add).then_inc(b_rope, 1)

            def prepare_lo(grp):
                s = grp % 2
                src = bank[(6 + grp) % 2]
                dve.wait_ge(b_k_hi, b * GR1 + grp + 1)
                nc.vector.tensor_tensor(k1[LO][:, s, :], src[:, SEQ:2 * SEQ], k1[HI][:, s, :].bitcast(F32),
                                        ALU.subtract)
                for eo in range(2):
                    last = nc.vector.scalar_tensor_tensor(
                        qE[LO][:, s, eo, :], src[:, 0:SEQ], table[:, T_EO + eo:T_EO + eo + 1],
                        qE[HI][:, s, eo, :].bitcast(F32), ALU.mult, ALU.subtract)
                last.then_inc(b_proj_free, 1)

            def minima(i):
                s = i % 2
                dve.wait_ge(b_scores, b * HEADS1 + i + 1)
                dve.sem_inc(passed, 1)
                nc.vector.tensor_tensor_reduce(s1[:, s, 0:P], bank[2 + s][:, 0:P], table[:, T_M1:T_M1 + P],
                                               1.0, 3e38, ALU.add, ALU.min, neg_max[:, s, 0:1])
                nc.vector.tensor_tensor_reduce(s1[:, s, P:3 * P], bank[2 + s][:, 2 * P:4 * P],
                                               table[:, T_M1 + P:T_M1 + 3 * P],
                                               1.0, 3e38, ALU.add, ALU.min,
                                               neg_max[:, s, 1:2]).then_inc(b_min, 1)

            def inverses(i):
                dve.wait_ge(b_exp, b * HEADS1 + i + 1)
                nc.vector.reciprocal(inv_sum[:, i % 2, :], row_sum[:, i % 2, :]).then_inc(b_inv, 1)

            def turned_lo(i):
                dve.wait_ge(b_pt_hi, b * HEADS1 + i + 1)
                nc.vector.tensor_tensor(pt1[LO][:, i % 2, P:4 * P], bank[PT][:, 0:3 * P],
                                        pt1[HI][:, i % 2, P:4 * P].bitcast(F32),
                                        ALU.subtract).then_inc(b_pt_lo, 1)

            def result_lo(grp):
                dve.wait_ge(b_o_hi, b * GR1 + grp + 1)
                nc.vector.tensor_tensor(oT1[LO][:, grp, :], bank[OB][:, 0:SEQ],
                                        oT1[HI][:, grp, :].bitcast(F32),
                                        ALU.subtract).then_inc(b_o_lo, 1)

            def tile(tt):
                return x[:, bass.ds(b * 2 + tt, 1), :].rearrange("p a n -> p (a n)")

            for tt in range(2):
                ln_normalise(dve, b * 2 + (LN1 + tt), tt, tile(tt))
                ln_lo_part(dve, b * 2 + (LN1 + tt), OUTB[tt], xb_tile(tt))
            for tt in range(2):
                biased(tt, 0)
                cosine(tt, 0)
                biased(tt, 1)
                cosine(tt, 1)
                biased(tt, 2)
                rotate(tt, 0)
                rotate(tt, 1)
            prepare_lo(0)
            for j in range(STEPS):
                if 1 <= j < HEADS1 + 1:
                    inverses(j - 1)
                if 2 <= j < HEADS1 + 2:
                    turned_lo(j - 2)
                if j < HEADS1:
                    minima(j)
                if ends_at(j) is not None:
                    result_lo(ends_at(j))
                if prep_at(j):
                    prepare_lo(prep_at(j))
            for tt in range(2):
                nc.vector.tensor_tensor(tile(tt), tile(tt), row[:, :], ALU.add).then_inc(b_added, 1)
            for tt in range(2):
                dve.wait_ge(b_added, b * 4 + tt + 1)
                dve.wait_ge(b_out, b * 2 + tt + 1)
                nc.vector.tensor_tensor(tile(tt), tile(tt), bank[OUTB[tt]][:, :],
                                        ALU.add).then_inc(b_added, 1)

        def b_gpsimd(pool):
            pool.wait_ge(x_written, X4)
            for i in (HI, LO):
                nc.gpsimd.memset(vz[i][:, :, :, :, :].bitcast(F32), 0.0)
                nc.gpsimd.memset(pt1[i][:, :, 0:P].bitcast(F32), 0.0).then_inc(b_zero, 1)
            with pool.Fori(0, BATCH) as b:
                b_gpsimd_batch(pool, b)

        def b_gpsimd_batch(pool, b):
            def sine(tt, j):
                r = 2 * tt + j
                pool.wait_ge(b_proj_free, b * FILLS1 + 3 * tt + j + 3)
                if r >= 2:
                    pool.wait_ge(b_rope, b * 4 + r - 1)
                c = j * DIM
                halves = lambda ap: ap.rearrange("p (h a d) -> p h a d", a=2, d=D1 // 2)
                t = T_R1 + ((2 * j + 1) * 2 + tt) * D1
                src, dst = halves(qkv[:, tt, c:c + DIM]), halves(work[:, r % 2, :])
                for a in range(2):
                    sin = table[:, t + a * (D1 // 2):t + (a + 1) * (D1 // 2)]
                    last = nc.gpsimd.tensor_tensor(dst[:, :, a, :], src[:, :, 1 - a, :],
                                                   sin.unsqueeze(1).to_broadcast([P, HEADS1, D1 // 2]),
                                                   ALU.mult)
                last.then_inc(b_sin, 1)

            def values_lo(grp):
                pool.wait_ge(b_v_hi, b * GR1 + grp + 1)
                for tt in range(2):
                    last = nc.gpsimd.tensor_tensor(diagonal(vz[LO], grp % 2, tt), values_of(grp, tt),
                                                   diagonal(vz[HI], grp % 2, tt).bitcast(F32),
                                                   ALU.subtract)
                last.then_inc(b_v_lo, 1)

            def normalise(i):
                s = i % 2
                pool.wait_ge(b_inv, b * HEADS1 + i + 1)
                nc.gpsimd.tensor_tensor(s1[:, s, 0:P], s1[:, s, 0:P],
                                        inv_sum[:, s, 0:1].to_broadcast([P, P]), ALU.mult)
                nc.gpsimd.tensor_tensor(s1[:, s, P:3 * P], s1[:, s, P:3 * P],
                                        inv_sum[:, s, 1:2].to_broadcast([P, 2 * P]),
                                        ALU.mult).then_inc(b_norm, 1)

            for tt in range(2):
                ln_power(pool, b * 2 + (LN1 + tt), tt)
            for tt in range(2):
                for j in range(2):
                    sine(tt, j)
            values_lo(0)
            for j in range(STEPS):
                if 1 <= j < HEADS1 + 1:
                    normalise(j - 1)
                if prep_at(j):
                    values_lo(prep_at(j))

        block = ctx.enter_context(nc.Block())

        @block.sync
        def _(sp):
            def flat(n):
                return w_in[n, :, :]

            xr = x_in.rearrange("(t p) d -> t p d", p=P)
            sp.dma_start(x[:, 0, :], xr[0]).then_inc(x_loaded[0], 16)
            sp.dma_start(table[:, :], table_in).then_inc(table_loaded, 16)
            sp.dma_start(biases[:, :], bias_in).then_inc(table_loaded, 16)
            for t in range(1, 4):
                sp.dma_start(x[:, t, :], xr[t]).then_inc(x_loaded[t], 16)
            for j in range(F0_CHUNKS):
                st_f0a.load(sp, j, flat(W_F0A + j))
                if j == 3:
                    for t in range(4, TILES):
                        sp.dma_start(x[:, t, :], xr[t]).then_inc(x_loaded[t], 16)
                    sp.dma_start(row[:, :], rows_in[0]).then_inc(row_loaded, 16)
            st_lq.load(sp, 0, flat(W_LQ))
            for j in range(len(BEFORE)):
                st_a0.load(sp, j, flat(W_A0 + j))
            with sp.Fori(0, KVH - 1) as g:
                for j in range(G_CHUNKS):
                    src = w_in[bass.ds(g * G_CHUNKS + (W_A0 + len(BEFORE) + j), 1), :, :]
                    st_loop.load(sp, j, src.rearrange("a p n -> (a p) n"), g)
            for j in range(len(TAIL)):
                st_tail.load(sp, j, flat(W_F1 - len(TAIL) + j))
            sp.wait_ge(x_written, X1)
            sp.dma_start(row[:, :], rows_in[0]).then_inc(row_loaded, 16)
            for j in range(F1_CHUNKS):
                st_f1a.load(sp, j, flat(W_F1 + j))
            sp.wait_ge(x_written, X3)
            sp.dma_start(row[:, :], rows_in[1]).then_inc(row_loaded, 16)
            for j in range(A1_CHUNKS):
                st_a1.load(sp, j, flat(W_A1 + j))
            sp.wait_ge(x_written, X4)
            sp.dma_start(row[:, :], rows_in[2]).then_inc(row_loaded, 16)
            sp.dma_start(bqkv[:, :], rows_in[3:6].rearrange("a p n -> p a n")).then_inc(bqkv_loaded, 16)
            for j in range(F1_CHUNKS):
                st_f1b.load(sp, j, flat(W_F1 + j))
            sp.wait_ge(x_written, X5)
            sp.dma_start(row[:, :], rows_in[1]).then_inc(row_loaded, 16)
            outr = out.rearrange("(t p) d -> t p d", p=P)
            for t in range(TILES):
                sp.wait_ge(x_written, X5 + 2 * (t + 1))
                sp.dma_start(outr[t], x[:, t, :]).then_inc(stored, 16)
            sp.wait_ge(stored, 16 * TILES)

        @block.tensor
        def _(pe):
            pe.wait_ge(table_loaded, 32)
            ffn0a.tensor(pe)
            a0_tensor(pe)
            ffn0b.tensor(pe)
            ffn1a.tensor(pe)
            b_tensor(pe)
            ffn1b.tensor(pe)

        @block.scalar
        def _(act):
            act.wait_ge(table_loaded, 32)
            ffn0a.scalar(act)
            a0_scalar(act)
            ffn0b.scalar(act)
            ffn1a.scalar(act)
            b_scalar(act)
            ffn1b.scalar(act)

        @block.vector
        def _(dve):
            dve.wait_ge(table_loaded, 32)
            ffn0a.vector(dve)
            a0_vector(dve)
            ffn0b.vector(dve)
            ffn1a.vector(dve)
            b_vector(dve)
            ffn1b.vector(dve)

        @block.gpsimd
        def _(pool):
            pool.wait_ge(table_loaded, 32)
            ffn0a.gpsimd(pool)
            a0_gpsimd(pool)
            ffn0b.gpsimd(pool)
            ffn1a.gpsimd(pool)
            b_gpsimd(pool)
            ffn1b.gpsimd(pool)


def chunks_of(a):
    n = -(-a.shape[1] // CH) * CH
    full = np.zeros((P, n), a.dtype)
    full[:, :a.shape[1]] = a
    return full.reshape(P, n // CH, CH).transpose(1, 0, 2)


def by_rows(w):
    k = w.shape[0] // P
    return w.reshape(k, P, w.shape[1]).transpose(1, 0, 2).reshape(P, k * w.shape[1])


def lay_out_weights(a):
    f0 = chunks_of(np.concatenate([by_rows(a["L0_ffn_w12"].T), by_rows(a["L0_ffn_w3"].T)], 1))
    wq, wk, wv = a["L0_attn_w_q"], a["L0_attn_w_k"], a["L0_attn_w_v"]
    wlk, wlv, wo, wlo = a["L0_attn_w_lk"], a["L0_attn_w_lv"], a["L0_attn_w_o"], a["L0_attn_w_lo"]
    groups = []
    for g in range(KVH):
        kv = slice(g * HD, (g + 1) * HD)
        hs = slice(g * GH * HD, (g + 1) * GH * HD)
        heads = [slice((g * GH + h) * HD, (g * GH + h + 1) * HD) for h in range(GH)]
        groups.append(chunks_of(np.concatenate(
            [by_rows(wk[:, kv])] + [by_rows(wq[:, h]) for h in heads] + [wlk[:, hs]]
            + [by_rows(np.concatenate([wlv[:, hs], wv[:, kv]], 1))]
            + [by_rows(wo[hs])] + [by_rows(wlo[hs])], 1)))
    a0 = [groups[0][BEFORE]]
    for g in range(KVH - 1):
        a0 += [groups[g][TURN[:OWN]], groups[g + 1][TURN[OWN:]]]
    a0 += [groups[-1][TAIL[:OWN]], f0[TAIL[OWN:]]]
    v1, u2 = a["L1_ffn_V1"], a["L1_ffn_U2"]
    halves = []
    for up in range(2):
        part = np.zeros((P, M1 * P), v1.dtype)
        part[:, :INTER] = v1[:, up * INTER:(up + 1) * INTER]
        halves.append(part)
    u2p = np.zeros((M1 * P, u2.shape[1]), u2.dtype)
    u2p[:INTER] = u2
    f1 = chunks_of(np.concatenate([by_rows(a["L1_ffn_U1"])] + halves + [by_rows(u2p), a["L1_ffn_V2"]], 1))
    a1 = chunks_of(np.concatenate([by_rows(a["L1_attn_qkv_w"]), by_rows(a["L1_attn_out_w"])], 1))
    lq = chunks_of(by_rows(a["L0_attn_w_lq"]))
    return np.ascontiguousarray(np.concatenate([f0, lq] + a0 + [f1, a1], 0))


def lay_out_biases(a):
    b = np.zeros((P, B_ALL), np.float32)
    b[:, B_12:B_12 + 2 * M0] = a["L0_ffn_b12"].reshape(2 * M0, P).T
    for up in range(2):
        part = np.zeros(M1 * P, np.float32)
        part[:INTER] = a["L1_ffn_b1"][up * INTER:(up + 1) * INTER]
        b[:, B_1 + up * M1:B_1 + (up + 1) * M1] = part.reshape(M1, P).T
    rows = np.concatenate([a["L0_ffn_b3"], a["L1_ffn_b2"], a["L1_attn_out_b"], a["L1_attn_qkv_b"]])
    rows = np.broadcast_to(rows.reshape(6, 1, DIM), (6, P, DIM))
    return b, np.ascontiguousarray(rows)


def kernel(**inputs):
    import concourse.bacc as bacc
    from concourse.bass_utils import run_bass_kernel_spmd

    a = {k: np.ascontiguousarray(v) for k, v in inputs.items()}
    weights = lay_out_weights(a)
    biases, rows = lay_out_biases(a)
    arrays = {"x": a["L0_attn_hidden_states"].reshape(TOKENS, DIM), "weights": weights,
              "constants": constants(), "bias_columns": biases, "bias_rows": rows}
    nc = bacc.Bacc("TRN2", target_bir_lowering=False, num_devices=1)
    args = [nc.dram_tensor(f"in_{n}", v.shape, F32, kind="ExternalInput").ap() for n, v in arrays.items()]
    args.append(nc.dram_tensor("out", (TOKENS, DIM), F32, kind="ExternalOutput").ap())
    program(nc, *args)
    r = run_bass_kernel_spmd(nc, [{f"in_{n}": v for n, v in arrays.items()}], core_ids=[0])
    return r.results[0]["out"].reshape(BATCH, SEQ, DIM)
```

```python
from contextlib import ExitStack

import numpy as np

import concourse.bass as bass
from concourse import mybir

F32 = mybir.dt.float32
F32R = mybir.dt.float32r
ALU = mybir.AluOpType
ACT = mybir.ActivationFunctionType

P = 128
BATCH, SEQ, DIM = 4, 256, 512
TOKENS = BATCH * SEQ
TILES = TOKENS // P
KC = DIM // P
CH = 512
HI, LO = 0, 1
PASSES = ((HI, HI), (HI, LO), (LO, HI))
EPS = 1e-5

HEADS0, KVH, HD = 32, 8, 128
GH = HEADS0 // KVH
G_CHUNKS = 19
C_K, C_Q, C_LK, C_LVV, C_WO, C_WLO = 0, 1, 5, 6, 11, 15
SPLIT_AT = {2: [17, 14], 3: [18], 11: [1], 12: [0, 2], 13: [3, 6], 14: [4, 7], 15: [8, 9],
            16: [10, 11, 15, 12], 17: [16, 13]}
SPLIT_LATE = {13: [5]}
SPLIT_FROM = 11
TURN = [c for s in sorted(SPLIT_AT) for c in SPLIT_AT[s] + SPLIT_LATE.get(s, [])]
OWN = sum(len(c) for s, c in SPLIT_AT.items() if s < SPLIT_FROM)
BEFORE = TURN[OWN:]
WEIGHTS_FOR = {2 + h: [C_WO + h, C_WLO + h] for h in range(GH)}
WEIGHTS_FOR.update({14: [C_K, C_Q, C_LK], 15: [C_Q + 1], 16: [C_Q + 2], 17: [C_Q + 3]})
LVW = GH * HD + HD
HALF = LVW // 2

M0 = 4
INTER = 1376
M1 = -(-INTER // P)
F0_CHUNKS = (KC * 2 * M0 * P + M0 * DIM) // CH
F1_COLS = KC * P + 2 * M1 * P + M1 * P + DIM
F1_CHUNKS = -(-F1_COLS // CH)

FIRST = [0, 2, 4, 6, 1, 3, 5, 7] + list(range(8, F0_CHUNKS))

HEADS1, D1 = 32, 16
GR1, HG1 = 4, 8
A1_CHUNKS = (KC * 3 * DIM + KC * DIM) // CH

W_F0A = 0
W_LQ = W_F0A + F0_CHUNKS
W_A0 = W_LQ + 1
W_F0B = W_A0 + KVH * G_CHUNKS
W_F1 = W_F0B + F0_CHUNKS
W_A1 = W_F1 + F1_CHUNKS
W_ALL = W_A1 + A1_CHUNKS
TAIL = TURN[:OWN] + [c for c in TURN[OWN:] if c < F0_CHUNKS]

T_ID = 0
T_MH = T_ID + P
T_HEAD = T_MH + 2
T_FIRST = T_HEAD + HG1
T_M0 = T_FIRST
T_M1 = T_M0 + 3 * P
T_COS = T_M1 + 3 * P
T_SIN = T_COS + 2 * SEQ
T_R1 = T_SIN + 2 * SEQ
T_ALL = T_R1 + 4 * 2 * D1

B_12 = 0
B_1 = B_12 + 2 * M0
B_ALL = B_1 + 2 * M1
RAW = 4


def constants():
    t = np.zeros((P, T_ALL), np.float32)
    t[:, T_ID:T_ID + P] = np.eye(P, dtype=np.float32)
    future = (np.arange(P)[None, :] > np.arange(P)[:, None]).astype(np.float32)
    for at, value in ((T_M0, 1e30), (T_M1, 66504.0)):
        t[:, at:at + P] = future * np.float32(value)
        t[:, at + 2 * P:at + 3 * P] = future * np.float32(value)
    inv = (1.0 / np.float32(10000.0) ** (np.arange(0, HD, 2, dtype=np.float32) / np.float32(HD))).astype(np.float32)
    ang = np.outer(np.arange(SEQ, dtype=np.float32), inv).astype(np.float32)
    cos = np.concatenate([np.cos(ang), np.cos(ang)], 1).T
    sin = np.concatenate([-np.sin(ang), np.sin(ang)], 1).T
    scale = np.float32(-1.0 / np.sqrt(HD))
    t[:, T_COS:T_COS + SEQ] = cos * scale
    t[:, T_COS + SEQ:T_COS + 2 * SEQ] = cos
    t[:, T_SIN:T_SIN + SEQ] = sin * scale
    t[:, T_SIN + SEQ:T_SIN + 2 * SEQ] = sin
    half = D1 // 2
    inv = (1.0 / np.float32(10000.0) ** (np.arange(0, half, dtype=np.float32) / np.float32(half))).astype(np.float32)
    ang = (np.arange(SEQ, dtype=np.float32)[:, None] * inv[None, :]).astype(np.float32)
    c1 = np.concatenate([np.cos(ang), np.cos(ang)], 1).reshape(2, P, D1).transpose(1, 0, 2)
    s1 = np.concatenate([-np.sin(ang), np.sin(ang)], 1).reshape(2, P, D1).transpose(1, 0, 2)
    t[:, T_R1:T_R1 + 8 * D1] = np.stack([c1 * np.float32(-0.25), s1 * np.float32(-0.25), c1, s1], 1).reshape(P, 8 * D1)
    t[:, T_HEAD:T_HEAD + HG1] = np.arange(P)[:, None] // D1 == np.arange(HG1)[None, :]
    t[:, T_MH:T_MH + 2] = -0.5
    return t


def program(nc, x_in, w_in, table_in, bias_in, rows_in, out):
    ctx = ExitStack()
    with ctx:
        def sem(name):
            return ctx.enter_context(nc.semaphore(name))

        def sb(scope, name, shape, dt=F32):
            return scope.enter_context(nc.sbuf_tensor(name, shape, dt))

        x = sb(ctx, "x", [P, TILES, DIM])
        table = sb(ctx, "table", [P, T_ALL])
        biases = sb(ctx, "biases", [P, B_ALL])
        row = sb(ctx, "row", [P, DIM])
        raw = sb(ctx, "raw", [P, RAW, CH])
        work = sb(ctx, "work", [P, 4, CH])
        stats = sb(ctx, "stats", [P, 2, 6])
        mean_var = sb(ctx, "mean_var", [P, 2, 2])
        var_eps = sb(ctx, "var_eps", [P, 2])
        rstd = sb(ctx, "rstd", [P, 2])
        neg_max = sb(ctx, "neg_max", [P, 4, 2])
        row_sum = sb(ctx, "row_sum", [P, 4, 2])
        inv_sum = sb(ctx, "inv_sum", [P, 4, 2])
        W = [sb(ctx, f"W{i}", [P, G_CHUNKS * CH], F32R) for i in (HI, LO)]
        xnA = [sb(ctx, f"xnA{i}", [P, KC, CH], F32R) for i in (HI, LO)]
        pz = [W[i][:, A1_CHUNKS * CH:(A1_CHUNKS + 2) * CH].rearrange("p (s n) -> p s n", s=2)
              for i in (HI, LO)]
        with ExitStack() as a:
            xnB = [sb(a, f"xnB{i}", [P, KC, CH], F32R) for i in (HI, LO)]
            with ExitStack() as s:
                WF0 = [sb(s, f"WF0_{i}", [P, F0_CHUNKS * CH], F32R) for i in (HI, LO)]
                h0 = [sb(s, f"h0_{i}", [P, 2, CH], F32R) for i in (HI, LO)]
            with ExitStack() as s:
                qk = [sb(s, f"qk{i}", [P, 6, SEQ], F32R) for i in (HI, LO)]
                lvv = sb(s, "lvv", [P, 2, LVW])
                pt0 = sb(s, "pt0", [P, 2, 3 * P])
                oT0 = [sb(s, f"oT0_{i}", [P, 4, SEQ], F32R) for i in (HI, LO)]
                lqT = [sb(s, f"lqT{i}", [P, TOKENS], F32R) for i in (HI, LO)]
                s0 = sb(s, "s0", [P, 4, 3 * P])
                normed = sb(s, "normed", [P, 4, DIM])
            with ExitStack() as s:
                WF1 = [sb(s, f"WF1_{i}", [P, F1_CHUNKS * CH], F32R) for i in (HI, LO)]
                h1 = [sb(s, f"h1_{i}", [P, 2, CH], F32R) for i in (HI, LO)]
        with ExitStack() as a:
            qkT = sb(a, "qkT", [P, 2, 2 * SEQ])
            qz = sb(a, "qz", [P, 2, HG1, SEQ])
            vz = sb(a, "vz", [P, 2, 2, HG1, P])
            pt1 = sb(a, "pt1", [P, 2, 3 * P])
            oT1 = [sb(a, f"oT1_{i}", [P, GR1, SEQ], F32R) for i in (HI, LO)]
            qkv = sb(a, "qkv", [P, 2, 3 * DIM])
            s1 = sb(a, "s1", [P, 4, 3 * P])
            bqkv = sb(a, "bqkv", [P, 3 * DIM])

        bank = [ctx.enter_context(nc.psum_tensor(f"bank{i}", [P, CH], F32)) for i in range(8)]
        ident = table[:, T_ID:T_ID + P]

        x_loaded = [sem(f"x_loaded{t}") for t in range(TILES)]
        table_loaded = sem("table_loaded")
        table_rest = sem("table_rest")
        row_loaded = sem("row_loaded")
        bqkv_loaded = sem("bqkv_loaded")
        stored = sem("stored")
        x_written = sem("x_written")
        passed = sem("passed")

        raw_loaded = [sem(f"raw_loaded{i}") for i in range(RAW)]
        w_hi = sem("w_hi")
        w_split = sem("w_split")

        class Stream:

            used = [0] * RAW
            last = [None] * RAW
            done = 0

            def __init__(self, n, turns=1):
                self.n, self.turns, self.base, self.at = n, turns, Stream.done, []
                per = [len(range(s, n, RAW)) for s in range(RAW)]
                for j in range(n):
                    s = j % RAW
                    before = Stream.used[s] + j // RAW
                    if j >= RAW:
                        prev = Stream.done + j - RAW
                    elif turns > 1:
                        prev = Stream.done - n + max(range(s, n, RAW))
                        assert Stream.last[s] is not None and Stream.last[s] <= Stream.done
                        prev = max(prev, Stream.last[s])
                    else:
                        prev = Stream.last[s]
                    self.at.append((s, before, per[s], prev))
                for s in range(RAW):
                    if per[s]:
                        Stream.last[s] = Stream.done + n * (turns - 1) + max(range(s, n, RAW))
                    Stream.used[s] += per[s] * turns
                Stream.done += n * turns

            def load(self, sp, j, source, g=None):
                s, before, per, prev = self.at[j]
                turn = 0 if g is None else g
                if prev is not None:
                    sp.wait_ge(w_split, prev + 1 + turn * self.n)
                sp.dma_start(raw[:, s, :], source).then_inc(raw_loaded[s], 16)

            def split_hi(self, act, j, dst, g=None):
                s, before, per, _ = self.at[j]
                turn = 0 if g is None else g
                act.wait_ge(raw_loaded[s], 16 * (before + 1) + turn * (16 * per))
                nc.scalar.copy(dst[HI], raw[:, s, :]).then_inc(w_hi, 1)

            def split_lo(self, dve, j, dst, g=None):
                s = self.at[j][0]
                turn = 0 if g is None else g
                dve.wait_ge(w_hi, self.base + j + 1 + turn * self.n)
                nc.vector.tensor_tensor(dst[LO], raw[:, s, :], dst[HI].bitcast(F32),
                                        ALU.subtract).then_inc(w_split, 1)

            def split_lo_pool(self, pool, j, dst):
                pool.wait_ge(w_hi, self.base + j + 1)
                pool.wait_ge(w_split, self.base + j)
                nc.gpsimd.tensor_tensor(dst[LO], raw[:, self.at[j][0], :], dst[HI].bitcast(F32),
                                        ALU.subtract).then_inc(w_split, 1)

            def ready(self, eng, j, g=None):
                turn = 0 if g is None else g
                eng.wait_ge(w_split, self.base + j + 1 + turn * self.n)

        def chunk(w, c):
            return [w[i][:, c * CH:(c + 1) * CH] for i in (HI, LO)]

        st_f0a = Stream(F0_CHUNKS)
        st_lq = Stream(1)
        st_a0 = Stream(len(BEFORE))
        st_loop = Stream(G_CHUNKS, KVH - 1)
        st_tail = Stream(len(TAIL))
        st_f1a = Stream(F1_CHUNKS)
        st_a1 = Stream(A1_CHUNKS)
        st_f1b = Stream(F1_CHUNKS)

        ln_stat = sem("ln_stat")
        ln_var = sem("ln_var")
        ln_rstd = sem("ln_rstd")
        ln_xn = sem("ln_xn")
        ln_turned = sem("ln_turned")
        ln_hi = sem("ln_hi")
        ln_done = sem("ln_done")

        def at_least(eng, s, value):
            if not isinstance(value, int) or value > 0:
                eng.wait_ge(s, value)

        def ln_moments(dve, n, slot, xt):
            nc.vector.bn_stats(stats[:, slot, :], xt).then_inc(ln_stat, 1)
            dve.wait_ge(ln_stat, n * 2 + 1)
            dve.sem_inc(passed, 1)
            nc.vector.bn_aggr(mean_var[:, slot, :], stats[:, slot, :]).then_inc(ln_stat, 1)
            dve.wait_ge(ln_stat, n * 2 + 2)
            nc.vector.tensor_scalar(var_eps[:, slot:slot + 1], mean_var[:, slot, 1:2], EPS, None,
                                    ALU.add).then_inc(ln_var, 1)

        def ln_apply(dve, n, slot, xt, to=None):
            dve.wait_ge(ln_rstd, n + 1)
            if to is None:
                at_least(dve, ln_turned, n - 1)
            nc.vector.tensor_scalar(work[:, slot, :] if to is None else to, xt, mean_var[:, slot, 0:1],
                                    rstd[:, slot:slot + 1], ALU.subtract, ALU.mult).then_inc(ln_xn, 1)

        def ln_power(pool, n, slot):
            pool.wait_ge(ln_var, n + 1)
            nc.gpsimd.tensor_tensor(rstd[:, slot:slot + 1], var_eps[:, slot:slot + 1],
                                    table[:, T_MH:T_MH + 1], ALU.pow).then_inc(ln_rstd, 1)

        def ln_turn(pe, n, slot, b, buffer=work, banks=1):
            pe.wait_ge(ln_xn, n + 1)
            at_least(pe, ln_done, n + 1 - banks)
            for c in range(KC):
                last = nc.tensor.transpose(bank[b][:, c * P:(c + 1) * P],
                                           buffer[:, slot, c * P:(c + 1) * P], ident)
            last.then_inc(ln_turned, 1)

        def turned(b):
            return bank[b][:, :].rearrange("p (c n) -> p c n", c=KC)

        def ln_hi_part(act, n, b, dst):
            act.wait_ge(ln_turned, n + 1)
            nc.scalar.copy(dst[HI], turned(b)).then_inc(ln_hi, 1)

        def ln_lo_part(dve, n, b, dst):
            dve.wait_ge(ln_hi, n + 1)
            nc.vector.tensor_tensor(dst[LO], turned(b), dst[HI].bitcast(F32),
                                    ALU.subtract).then_inc(ln_done, 1)

        def xn(i, c, tokens):
            half, at = (xnA, xnB)[tokens.start // CH], tokens.start // CH * CH
            return half[i][:, c, tokens.start - at:tokens.stop - at]

        def xn_tile(t):
            half, at = (xnA, xnB)[t * P // CH], t * P % CH
            return [half[i][:, :, at:at + P] for i in (HI, LO)]

        def product(out_ap, lhs, rhs, start=True, stop=True):
            for k, (i, j) in enumerate(PASSES):
                last = nc.tensor.matmul(out_ap, lhs(i), rhs(j), start=start and k == 0,
                                        stop=stop and k == 2)
            return last

        f_ready = sem("f_ready")
        f_silu = sem("f_silu")
        f_mul = sem("f_mul")
        f_hi = sem("f_hi")
        f_lo = sem("f_lo")
        f_used = sem("f_used")
        f_out = sem("f_out")
        pz_ready = sem("pz_ready")
        pz_hi = sem("pz_hi")
        pz_lo = sem("pz_lo")
        RING, LNB, ZB = (0, 1, 2), 3, 4

        class FFN:

            m_all, o_all, u_all, z_all = 0, 0, 0, 0

            def __init__(self, layer, w, h, ln0, next_tiles, x_before, row_n, first, own=(), beside=(),
                         needs=None):
                self.layer, self.w, self.h = layer, w, h
                self.M = M0 if layer == 0 else M1
                self.m0, self.o0, self.u0, self.z0 = FFN.m_all, FFN.o_all, FFN.u_all, FFN.z_all
                FFN.m_all += 2 * self.M
                FFN.o_all += TILES
                FFN.u_all += 2 * (self.M - 1)
                FFN.z_all += 4 if layer else 0
                self.lag = 2 if layer else 1
                self.out_banks = (4, 5, 6, 7) if layer == 0 else (5, 6, 7)
                self.ln0, self.ln_next, self.row_n, self.first = ln0, ln0 + TILES, row_n, first
                self.next_tiles = next_tiles
                self.x_before = x_before
                self.needs = needs
                self.own = own
                self.beside = beside

            def gate_up(self, m, up, c):
                if self.layer == 0:
                    at = c * 2 * M0 * P + (up * M0 + m) * P
                else:
                    at = KC * P + (up * M1 + m) * P
                return lambda i: self.w[i][:, at:at + P]

            def down(self, m):
                if self.layer == 0:
                    at = KC * 2 * M0 * P + m * DIM
                    return lambda i: self.w[i][:, at:at + DIM]
                at = KC * P + 2 * M1 * P + m * P
                return lambda i: self.w[i][:, at:at + P]

            def bias(self, m, up):
                at = (B_12 + up * M0 + m) if self.layer == 0 else (B_1 + up * M1 + m)
                return biases[:, at:at + 1]

            def added(self, t):
                return self.x_before + t // 4 * 8 + 4 + t % 4 + 1

            def bank_of(self, o):
                return self.out_banks[(o - self.o0) % len(self.out_banks)]

            def at(self, i):
                k = min(i // self.M, 1)
                return k, i - k * self.M

            def low_rank(self, i):
                if not self.layer:
                    return []
                return {0: [(self.z0, 0, ZB)],
                        self.M - 1: [(self.z0 + 1, 1, self.out_banks[0])],
                        self.M + self.lag: [(self.z0 + 2, 0, ZB)]}.get(i, [])

            def tiles_out(self, i):
                if self.layer:
                    t = i - self.M - self.lag
                    return [t] if 0 <= t < 4 else []
                return [0, 1, 2, 3] if i == self.M else []

            def ln_tiles(self, k, m):
                if self.layer:
                    t, odd = (m - 4 * k) // 2, m % 2
                else:
                    t, odd = m - k, 0
                if t < 0 or odd or t >= (self.next_tiles if k else 4):
                    return []
                return [(self.ln0 + 4 + t, 4 + t)] if k == 0 else [(self.ln_next + t, t)]

            def splits(self, i):
                per = -(-len(self.beside) // (2 * self.M))
                return self.beside[i * per:(i + 1) * per]

            def consumed(self, eng, i):
                k, m = self.at(i)
                if m < self.M - 1:
                    eng.wait_ge(f_used, self.u0 + k * (self.M - 1) + m + 1)
                elif self.layer:
                    eng.wait_ge(pz_ready, self.z0 + 2 + k + 1)
                else:
                    eng.wait_ge(f_out, self.o0 + 4 * k + 4)

            def tensor(self, pe):
                M = self.M
                if self.first:
                    for t in range(4):
                        ln_turn(pe, self.ln0 + t, t % 2, LNB + t % 2, banks=2)
                if self.layer:
                    pe.wait_ge(x_written, self.x_before)
                pe.wait_ge(ln_done, self.ln0 + 4)
                if self.needs:
                    self.needs[0].ready(pe, self.needs[1])
                if self.layer:
                    at_least(pe, pz_lo, self.z0)
                    self.tensor_low_rank(pe, 0, bank[ZB])
                for i in range(2 * M + self.lag):
                    k, m = self.at(i)
                    if not self.layer and i == M:
                        pe.wait_ge(ln_done, self.ln0 + 8)
                    if i < 2 * M:
                        if self.layer and m == 0:
                            pe.wait_ge(pz_lo, self.z0 + k + 1)
                        self.tensor_gate_up(pe, k, m)
                    if i >= self.lag:
                        self.tensor_down(pe, *divmod(i - self.lag, M))
                    if self.layer and i == M - 2:
                        pe.wait_ge(ln_done, self.ln0 + 8)
                        self.tensor_low_rank(pe, 1, bank[self.out_banks[0]])
                    if self.layer:
                        for t in self.tiles_out(i):
                            self.tensor_out(pe, 0, t)
                    for n, t in self.ln_tiles(k, m - 2 * self.layer):
                        ln_turn(pe, n, t % 2, LNB)
                if self.layer:
                    for t in range(4):
                        self.tensor_out(pe, 1, t)

            def tensor_low_rank(self, pe, k, to):
                for c in range(KC):
                    last = product(to[:, :], lambda i: self.w[i][:, c * P:(c + 1) * P],
                                   lambda i: xn(i, c, slice(k * CH, (k + 1) * CH)), c == 0, c == KC - 1)
                last.then_inc(pz_ready, 1)

            def tensor_out(self, pe, k, t):
                o = 4 * k + t
                if t == 0:
                    pe.wait_ge(pz_lo, self.z0 + 2 + k + 1)
                if o >= 3:
                    pe.wait_ge(x_written, self.added(o - 3))
                at = F1_COLS - DIM
                product(bank[self.bank_of(self.o0 + o)][:, :],
                        lambda i: pz[i][:, k, t * P:(t + 1) * P],
                        lambda i: self.w[i][:, at:at + DIM]).then_inc(f_out, 1)

            def tensor_gate_up(self, pe, k, m):
                q = self.m0 + k * self.M + m
                for up in (0, 1):
                    if self.own and k == 0 and m == 0:
                        st_f0a.ready(pe, 4 * up + 3)
                    f = 2 * q + up
                    prev = f - len(RING)
                    if prev >= 0 and prev % 2:
                        pe.wait_ge(f_mul, prev // 2 + 1)
                    elif prev >= 0:
                        pe.wait_ge(f_silu, prev // 2 + 1)
                    dst = bank[RING[f % len(RING)]][:, :]
                    if self.layer == 0:
                        for c in range(KC):
                            last = product(dst, self.gate_up(m, up, c),
                                           lambda i: xn(i, c, slice(k * CH, (k + 1) * CH)),
                                           c == 0, c == KC - 1)
                    else:
                        last = product(dst, self.gate_up(m, up, 0), lambda i: pz[i][:, k, :])
                    last.then_inc(f_ready, 1)

            def tensor_down(self, pe, k, m):
                q = self.m0 + k * self.M + m
                pe.wait_ge(f_lo, q + 1)
                first, end = m == 0, m == self.M - 1
                if self.layer == 0:
                    if first and k == 0 and self.own:
                        st_f0a.ready(pe, F0_CHUNKS - 1)
                    if first and k == 0:
                        at_least(pe, x_written, self.x_before)
                    for t in range(4):
                        if first and k == 1:
                            pe.wait_ge(x_written, self.added(t))
                        last = product(bank[self.out_banks[t]][:, :],
                                       lambda i: self.h[i][:, q % 2, t * P:(t + 1) * P], self.down(m),
                                       first, end)
                        if end:
                            last.then_inc(f_out, 1)
                else:
                    if first and k == 1:
                        pe.wait_ge(pz_lo, self.z0 + 3)
                    last = product(bank[ZB][:, :], self.down(m), lambda i: self.h[i][:, q % 2, :],
                                   first, end)
                    if end:
                        last.then_inc(pz_ready, 1)
                if not end:
                    last.then_inc(f_used, 1)

            def scalar(self, act):
                M = self.M
                if self.first:
                    for st, j, dst in self.own[:RAW]:
                        st.split_hi(act, j, dst)
                    for t in range(4):
                        ln_hi_part(act, self.ln0 + t, LNB + t % 2, xn_tile(t))
                    for st, j, dst in self.own[RAW:]:
                        st.split_hi(act, j, dst)
                for i in range(2 * M + 1):
                    (k, m), q = self.at(i), self.m0 + i
                    if i > 0:
                        act.wait_ge(f_mul, q)
                        if i > 2:
                            self.consumed(act, i - 3)
                        nc.scalar.copy(self.h[HI][:, (q - 1) % 2, :],
                                       work[:, 2 + (q - 1) % 2, :]).then_inc(f_hi, 1)
                    for z in self.low_rank(i):
                        self.low_rank_hi(act, *z)
                    if i < 2 * M:
                        act.wait_ge(f_ready, 2 * q + 1)
                        at_least(act, f_lo, q - 1)
                        nc.scalar.activation(work[:, 2 + q % 2, :], bank[RING[(2 * q) % 3]][:, :],
                                             ACT.Silu, bias=self.bias(m, 0)).then_inc(f_silu, 1)
                    for n, t in self.ln_tiles(k, m - 3 * self.layer):
                        if k == 1:
                            act.wait_ge(f_ready, 2 * (self.m0 + M))
                        ln_hi_part(act, n, LNB, xn_tile(t))
                    for st, j, dst in self.splits(i):
                        st.split_hi(act, j, dst)
                if self.layer:
                    self.low_rank_hi(act, self.z0 + 3, 1, ZB)

            def low_rank_hi(self, act, z, slot, b):
                act.wait_ge(pz_ready, z + 1)
                nc.scalar.copy(pz[HI][:, slot, :], bank[b][:, :]).then_inc(pz_hi, 1)

            def vector(self, dve):
                M = self.M

                def normalise(n, t, parts):
                    if self.x_before == 0 and n < TILES:
                        dve.wait_ge(x_loaded[t], 16)
                    elif n < self.ln0 + TILES:
                        dve.wait_ge(x_written, self.x_before)
                    else:
                        dve.wait_ge(x_written, self.added(t))
                    for part in parts:
                        part(dve, n, t % 2, x[:, t, :])

                def add(t):
                    dve.wait_ge(x_written, self.x_before + t // 4 * 8 + 4)
                    dve.wait_ge(f_out, self.o0 + t + 1)
                    nc.vector.scalar_tensor_tensor(x[:, t, :], bank[self.bank_of(self.o0 + t)][:, :],
                                                   0.5, x[:, t, :], ALU.mult,
                                                   ALU.add).then_inc(x_written, 1)

                if self.first:
                    for t in range(6):
                        if t < 4:
                            normalise(self.ln0 + t, t, (ln_moments,))
                        if 0 < t < 5:
                            normalise(self.ln0 + t - 1, t - 1, (ln_apply,))
                        if t > 1:
                            ln_lo_part(dve, self.ln0 + t - 2, LNB + t % 2, xn_tile(t - 2))
                for i in range(2 * M + 1):
                    (k, m), q = self.at(i), self.m0 + i
                    if i > 0:
                        slot = (q - 1) % 2
                        dve.wait_ge(f_hi, q)
                        nc.vector.tensor_tensor(self.h[LO][:, slot, :], work[:, 2 + slot, :],
                                                self.h[HI][:, slot, :].bitcast(F32),
                                                ALU.subtract).then_inc(f_lo, 1)
                    for z in self.low_rank(i):
                        self.low_rank_lo(dve, *z)
                    for n, t in [] if self.layer else self.ln_tiles(k, m):
                        normalise(n, t, (ln_moments, ln_apply))
                    if i < 2 * M:
                        dve.wait_ge(f_ready, 2 * q + 2)
                        dve.wait_ge(f_silu, q + 1)
                        w = work[:, 2 + q % 2, :]
                        nc.vector.scalar_tensor_tensor(w, bank[RING[(2 * q + 1) % 3]][:, :],
                                                       self.bias(m, 1), w, ALU.add,
                                                       ALU.mult).then_inc(f_mul, 1)
                    for t in self.tiles_out(i):
                        add(t)
                    if self.layer:
                        for n, t in self.ln_tiles(k, m):
                            normalise(n, t, (ln_moments,))
                        for n, t in self.ln_tiles(k, m - 1):
                            normalise(n, t, (ln_apply,))
                    if M - 4 <= m < M:
                        t = 4 * k + m - (M - 4)
                        dve.wait_ge(row_loaded, 16 * (self.row_n + 1))
                        dve.wait_ge(ln_xn, self.ln0 + t + 1)
                        nc.vector.scalar_tensor_tensor(x[:, t, :], row[:, :], 0.5, x[:, t, :],
                                                       ALU.mult, ALU.add).then_inc(x_written, 1)
                    for n, t in self.ln_tiles(k, m - 3 * self.layer):
                        ln_lo_part(dve, n, LNB, xn_tile(t))
                if self.layer:
                    self.low_rank_lo(dve, self.z0 + 3, 1, ZB)
                for t in range(4, TILES):
                    add(t)

            def low_rank_lo(self, dve, z, slot, b):
                dve.wait_ge(pz_hi, z + 1)
                nc.vector.tensor_tensor(pz[LO][:, slot, :], bank[b][:, :], pz[HI][:, slot, :].bitcast(F32),
                                        ALU.subtract).then_inc(pz_lo, 1)

            def gpsimd(self, pool):
                if self.first:
                    for t in range(4):
                        ln_power(pool, self.ln0 + t, t % 2)
                    for st, j, dst in self.own:
                        st.split_lo_pool(pool, j, dst)
                for i in range(2 * self.M + 1):
                    for n, t in self.ln_tiles(*self.at(i)):
                        ln_power(pool, n, t % 2)
                    for st, j, dst in self.splits(i):
                        st.split_lo_pool(pool, j, dst)

        def lot(stream, w, columns):
            return [(stream, j, chunk(w, c)) for j, c in enumerate(columns)]

        X1 = 2 * TILES
        X2 = X1 + 1
        X3, X4 = X2 + 2 * TILES, X2 + 4 * TILES
        X5 = X4 + 1
        ffn0a = FFN(0, WF0, h0, 0, 4, 0, 0, True, lot(st_f0a, WF0, FIRST),
                    lot(st_lq, W, [C_WO + 3]) + lot(st_a0, W, BEFORE))
        ffn0b = FFN(0, W, h0, 16, 4, X2, 1, False, (), lot(st_f1a, WF1, range(F1_CHUNKS)),
                    (st_tail, len(TAIL) - 1))
        ffn1a = FFN(1, WF1, h1, 24, 2, X3, 2, False, (), lot(st_a1, W, range(A1_CHUNKS)),
                    (st_f1a, F1_CHUNKS - 1))
        ffn1b = FFN(1, W, h1, 40, 0, X5, 4, False, (), (), (st_f1b, F1_CHUNKS - 1))

        a_proj = sem("a_proj")
        a_proj_free = sem("a_proj_free")
        a_swapped = sem("a_swapped")
        a_sin = sem("a_sin")
        a_rope = sem("a_rope")
        a_rope_hi = sem("a_rope_hi")
        a_rope_lo = sem("a_rope_lo")
        a_scores = sem("a_scores")
        a_min = sem("a_min")
        a_exp = sem("a_exp")
        a_inv = sem("a_inv")
        a_norm = sem("a_norm")
        a_turned = sem("a_turned")
        a_pt = sem("a_pt")
        a_pv = sem("a_pv")
        a_o_hi = sem("a_o_hi")
        a_o_lo = sem("a_o_lo")
        a_out = sem("a_out")
        a_added = sem("a_added")
        a_lq = sem("a_lq")
        a_lq_hi = sem("a_lq_hi")
        a_lq_lo = sem("a_lq_lo")
        PT, OB, OUTB = 4, 5, (6, 7)
        LQB = (2, OUTB[1])
        STEPS0 = BATCH * GH
        FILLS, ROPES = 9, 5
        AHEAD = 3

        class Step:

            def __init__(self, g, s):
                self.g, self.s = g, s
                self.batch, self.h = divmod(s, GH)
                self.first = isinstance(g, int) and g == 0 and s < 1
                self.second = isinstance(g, int) and g == 0 and s < 2
                self.last_group = isinstance(g, int) and g == KVH - 1
                self.heads = not (self.last_group and s >= STEPS0)
                self.queries = not (self.last_group and s >= STEPS0 - 2)
                self.key = self.queries and self.h == GH - 2
                self.tokens = slice(self.batch % BATCH * SEQ, (self.batch % BATCH + 1) * SEQ)
                self.added = 1 + 2 * self.batch + g * (2 * BATCH)

            def near(self, d):
                return Step(self.g, self.s + d)

            def number(self):
                return self.g * STEPS0 + self.s

            def inst(self, k):
                return self.g * (2 * STEPS0) + (2 * self.s + k), (2 * self.s + k) % 4

            def fill(self, what):
                i = 6 if what == "k" else (0, 5, 7, 8)[self.h] if what == "q" else 1 + what
                n = FILLS * self.batch + i + AHEAD
                return self.g * (BATCH * FILLS) + n, n % 2

            def rope(self, what):
                i = 2 if what == "k" else (0, 1, 3, 4)[self.h]
                n = ROPES * self.batch + i + AHEAD
                return self.g * (BATCH * ROPES) + n, n % 2

            def columns(self, what):
                return slice(SEQ, 2 * SEQ) if what == "k" else slice(0, 2 * SEQ)

            def target(self, what):
                if what == "k":
                    at = 4 + self.near(2).batch % 2
                    return [qk[i][:, at, :] for i in (HI, LO)]
                at = 2 * (self.h % 2)
                return [qk[i][:, at:at + 2, :].rearrange("p a n -> p (a n)") for i in (HI, LO)]

        def a0_run(eng, step, other_half):
            step(Step(0, 0))
            other_half()
            step(Step(0, 1))
            with eng.Fori(0, KVH - 1) as g:
                for s in range(2, STEPS0 + 2):
                    step(Step(g, s))
            for s in range(2, STEPS0 + 2):
                step(Step(KVH - 1, s))

        def step_splits(st, late):
            s = st.s
            if s < 2:
                return []
            stream, turn = (st_tail, TAIL) if st.last_group else (st_loop, TURN)
            chunks = (SPLIT_LATE if late else SPLIT_AT).get(s, [])
            return [(stream, turn.index(c), chunk(W, c)) for c in chunks if c in turn]

        def weights(pe, st, chunks):
            if st.s < 2 or not chunks or (st.last_group and st.s >= SPLIT_FROM):
                return
            at = max(TURN.index(c) + 1 - (G_CHUNKS if st.s < SPLIT_FROM and c in TURN[OWN:] else 0)
                     for c in chunks)
            stream = st_tail if st.last_group else st_loop
            pe.wait_ge(w_split, stream.base + at + (0 if st.last_group else st.g * G_CHUNKS))

        def a0_tensor(pe):
            def latent(i):
                for c in range(KC):
                    at = (C_WO + 3) * CH + c * P
                    last = product(bank[LQB[i]][:, :], lambda p: W[p][:, at:at + P],
                                   lambda p: xn(p, c, slice(i * CH, (i + 1) * CH)), c == 0, c == KC - 1)
                last.then_inc(a_lq, 1)

            def turn_tiles(tiles):
                for t in tiles:
                    ln_turn(pe, 8 + t, t - 4, OUTB[t % 2], normed, 2)

            def other_half():
                turn_tiles((6, 7))
                pe.wait_ge(ln_done, 16)
                latent(1)
                pe.wait_ge(a_lq_lo, 2)

            pe.wait_ge(ln_done, 12)
            pe.wait_ge(f_mul, 2 * M0)
            st_lq.ready(pe, 0)
            latent(0)
            pe.wait_ge(a_lq_lo, 1)
            st_a0.ready(pe, len(BEFORE) - 1)
            a0_keys(pe, Step(0, -2))
            a0_queries(pe, Step(0, -2))
            turn_tiles((4, 5))
            a0_queries(pe, Step(0, -1))
            a0_run(pe, lambda st: a0_tensor_step(pe, st), other_half)

        def a0_claim(pe, st, what):
            n, s = st.fill(what)
            pe.wait_ge(a_proj_free, n + 1)
            return bank[s]

        def a0_keys(pe, st):
            dst, to = a0_claim(pe, st, "k"), st.near(2)
            for c in range(KC):
                w = C_K * CH + c * P
                last = product(dst[:, SEQ:2 * SEQ], lambda p: W[p][:, w:w + P],
                               lambda p: xn(p, c, to.tokens), c == 0, c == KC - 1)
            last.then_inc(a_proj, 1)

        def a0_queries(pe, st):
            dst, to = a0_claim(pe, st, "q"), st.near(2)
            for c in range(KC):
                w = (C_Q + to.h) * CH + c * P
                product(dst[:, 0:SEQ], lambda p: W[p][:, w:w + P],
                        lambda p: xn(p, c, to.tokens), c == 0, c == KC - 1)
            w = C_LK * CH + to.h * P
            product(dst[:, SEQ:2 * SEQ], lambda p: W[p][:, w:w + P],
                    lambda p: lqT[p][:, to.tokens]).then_inc(a_proj, 1)

        def a0_values(pe, st):
            for i in range(4):
                tt, half = divmod(i, 2)
                dst = a0_claim(pe, st, i)
                t = st.tokens.start + tt * P
                for c in range(KC):
                    w = C_LVV * CH + c * LVW + half * HALF
                    last = product(dst[:, 0:HALF], lambda p: xn(p, c, slice(t, t + P)),
                                   lambda p: W[p][:, w:w + HALF], c == 0, c == KC - 1)
                last.then_inc(a_proj, 1)

        def score_columns(k, qt):
            n = (qt + 1) * P
            return bank[2 + qt][:, (1 - k) * n:(2 - k) * n]

        def a0_tensor_step(pe, st):
            def scores():
                pe.wait_ge(a_rope_lo, st.near(-2).rope("q")[0] + 3)
                pe.wait_ge(a_min, st.inst(1)[0] + 1)
                q, k = 2 * (st.h % 2), 4 + st.batch % 2
                pair = slice(q + 1, k + 1, k - q - 1)
                for qt in range(2):
                    n = (qt + 1) * P
                    dst = bank[2 + qt][:, 0:2 * n].rearrange("p (a n) -> p a n", a=2)
                    last = product(dst, lambda p: qk[p][:, q, qt * P:(qt + 1) * P],
                                   lambda p: qk[p][:, pair, 0:n])
                last.then_inc(a_scores, 1)

            def turn(k):
                n, s = st.near(-1).inst(k)
                pe.wait_ge(a_norm, n + 1)
                pe.wait_ge(a_pt, n + 1)
                for blk in range(3):
                    last = nc.tensor.transpose(bank[PT][:, blk * P:(blk + 1) * P],
                                               s0[:, s, blk * P:(blk + 1) * P], ident)
                last.then_inc(a_turned, 1)

            def weigh(k):
                before = st.near(-1)
                n, _ = before.inst(k)
                col = before.h * P if k else GH * P
                if before.h == 0 and k == 0:
                    pe.wait_ge(a_proj_free, before.fill(3)[0] + 3)
                pe.wait_ge(a_pt, n + 2)
                pe.wait_ge(a_o_lo, n + 1)
                nc.tensor.matmul(bank[OB][:, 0:SEQ], lvv[:, 0, col:col + P], pt0[:, k, 0:2 * P],
                                 start=True, stop=False)
                nc.tensor.matmul(bank[OB][:, P:SEQ], lvv[:, 1, col:col + P], pt0[:, k, 2 * P:3 * P],
                                 start=False, stop=True).then_inc(a_pv, 1)

            def output(k):
                done = st.near(-2)
                n, s = done.inst(k)
                first, end = done.h == 0 and k == 0, done.h == GH - 1 and k == 1
                if first:
                    pe.wait_ge(a_added, done.added)
                pe.wait_ge(a_o_lo, n + 2)
                w = ((C_WLO if k else C_WO) + done.h) * CH
                for tt in range(2):
                    last = product(bank[OUTB[tt]][:, :], lambda p: oT0[p][:, s, tt * P:(tt + 1) * P],
                                   lambda p: W[p][:, w:w + CH], first, end)
                    if end:
                        last.then_inc(a_out, 1)

            lag1, lag2 = lagging(st), not st.second
            if lag1:
                turn(0)
            if st.heads:
                scores()
            if st.s in WEIGHTS_FOR:
                weights(pe, st, WEIGHTS_FOR[st.s])
            if st.key:
                a0_keys(pe, st)
            if lag1:
                weigh(0)
                turn(1)
            if st.queries:
                a0_queries(pe, st)
            if lag2:
                output(0)
            if lag1:
                weigh(1)
            if lag2:
                output(1)
            if st.h == 0 and st.heads:
                if st.s == STEPS0:
                    weights(pe, st, range(C_LVV, C_WO))
                a0_values(pe, st)
            t = next_norm(st)
            if t is not None:
                if t == 0:
                    pe.wait_ge(a_proj_free, st.near(-1).fill("q")[0] + 3)
                ln_turn(pe, 16 + t, t % 2, t % 2, banks=2)

        def next_norm(st):
            return st.s - (STEPS0 - 2) if st.last_group and st.s >= STEPS0 - 2 else None

        def lagging(st):
            return not st.first and not (st.last_group and st.s == STEPS0 + 1)

        def a0_scalar(act):
            def latent_hi(i):
                act.wait_ge(a_lq, i + 1)
                nc.scalar.copy(lqT[HI][:, i * CH:(i + 1) * CH], bank[LQB[i]][:, :]).then_inc(a_lq_hi, 1)

            def tiles_hi(tiles):
                for t in tiles:
                    ln_hi_part(act, 8 + t, OUTB[t % 2], xn_tile(t))

            def other_half():
                tiles_hi((6, 7))
                latent_hi(1)

            act.wait_ge(x_written, X1)
            latent_hi(0)
            a0_swap(act, Step(0, -2), "k")
            a0_swap(act, Step(0, -2), "q")
            tiles_hi((4, 5))
            a0_rope_hi(act, Step(0, -2), "k")
            a0_rope_hi(act, Step(0, -2), "q")
            a0_swap(act, Step(0, -1), "q")
            a0_run(act, lambda st: a0_scalar_step(act, st), other_half)

        def a0_swap(act, st, what):
            n, s = st.rope(what)
            f, fs = st.fill(what)
            cols, half = st.columns(what), P // 2
            act.wait_ge(a_proj, f + 1)
            act.wait_ge(a_rope_lo, n + 1)
            nc.scalar.copy(work[0:half, s, cols], bank[fs][half:P, cols])
            nc.scalar.copy(work[half:P, s, cols], bank[fs][0:half, cols]).then_inc(a_swapped, 1)

        def a0_rope_hi(act, st, what):
            n, s = st.rope(what)
            act.wait_ge(a_rope, n + 1)
            nc.scalar.copy(st.target(what)[HI], work[:, 2 + s, st.columns(what)]).then_inc(a_rope_hi, 1)

        def a0_scalar_step(act, st):
            before = st.near(-1)

            def exponentials(k):
                n, s = st.inst(k)
                act.wait_ge(a_min, n + 3)
                for qt, cols in ((0, slice(0, P)), (1, slice(P, 3 * P))):
                    last = nc.scalar.activation(s0[:, s, cols], s0[:, s, cols], ACT.Exp,
                                                bias=neg_max[:, s, qt:qt + 1], scale=-1.0,
                                                accum_out=row_sum[:, s, qt:qt + 1])
                last.then_inc(a_exp, 1)

            def turned_out(k):
                act.wait_ge(a_turned, before.inst(k)[0] + 1)
                nc.scalar.copy(pt0[:, k, :], bank[PT][:, 0:3 * P]).then_inc(a_pt, 1)

            def result_hi(k):
                n, s = before.inst(k)
                act.wait_ge(a_pv, n + 1)
                nc.scalar.copy(oT0[HI][:, s, :], bank[OB][:, 0:SEQ]).then_inc(a_o_hi, 1)

            turn_of = None if st.last_group else st.g
            if lagging(st):
                turned_out(0)
            if before.queries:
                a0_rope_hi(act, before, "q")
            if st.heads:
                exponentials(0)
            if st.key:
                a0_swap(act, st, "k")
            if st.heads:
                exponentials(1)
            if lagging(st):
                result_hi(0)
                turned_out(1)
            for stream, j, dst in step_splits(st, False):
                stream.split_hi(act, j, dst, turn_of)
            if st.key:
                a0_rope_hi(act, st, "k")
            if st.queries:
                a0_swap(act, st, "q")
            if lagging(st):
                result_hi(1)
            for stream, j, dst in step_splits(st, True):
                stream.split_hi(act, j, dst, turn_of)
            t = next_norm(st)
            if t is not None:
                ln_hi_part(act, 16 + t, t % 2, xn_tile(t))

        def a0_vector(dve):
            for s, n in ((a_proj_free, 2), (a_rope_lo, 2), (a_min, 2), (a_pt, 1), (a_o_lo, 1),
                         (a_added, 1)):
                dve.sem_inc(s, n)
            def latent_lo(i):
                dve.wait_ge(a_lq_hi, i + 1)
                cols = slice(i * CH, (i + 1) * CH)
                nc.vector.tensor_tensor(lqT[LO][:, cols], bank[LQB[i]][:, :], lqT[HI][:, cols].bitcast(F32),
                                        ALU.subtract).then_inc(a_lq_lo, 1)

            def normalise(tiles):
                for t in tiles:
                    ln_moments(dve, 8 + t, t % 2, x[:, t, :])
                for t in tiles:
                    ln_apply(dve, 8 + t, t % 2, x[:, t, :], normed[:, t - 4, :])

            def tiles_lo(tiles):
                for t in tiles:
                    ln_lo_part(dve, 8 + t, OUTB[t % 2], xn_tile(t))

            def other_half():
                tiles_lo((6, 7))
                latent_lo(1)

            dve.wait_ge(x_written, X1)
            dve.wait_ge(table_rest, 16)
            latent_lo(0)
            normalise((4, 5))
            a0_cosine(dve, Step(0, -2), "k")
            a0_cosine(dve, Step(0, -2), "q")
            a0_rotate(dve, Step(0, -2), "k")
            a0_rotate(dve, Step(0, -2), "q")
            normalise((6, 7))
            tiles_lo((4, 5))
            a0_cosine(dve, Step(0, -1), "q")
            a0_run(dve, lambda st: a0_vector_step(dve, st), other_half)
            dve.wait_ge(a_added, 1 + KVH * TILES)
            dve.sem_inc(x_written, 1)

        def a0_cosine(dve, st, what):
            n, s = st.rope(what)
            _, fs = st.fill(what)
            cols = st.columns(what)
            dve.wait_ge(a_swapped, n + 1)
            dve.wait_ge(a_rope_lo, n + 1)
            nc.vector.tensor_tensor(work[:, 2 + s, cols], bank[fs][:, cols],
                                    table[:, T_COS + cols.start:T_COS + cols.stop],
                                    ALU.mult).then_inc(a_proj_free, 1)

        def a0_rotate(dve, st, what):
            n, s = st.rope(what)
            cols = st.columns(what)
            dve.wait_ge(a_sin, n + 1)
            dve.wait_ge(a_proj_free, st.fill(what)[0] + 3)
            nc.vector.tensor_tensor(work[:, 2 + s, cols], work[:, 2 + s, cols], work[:, s, cols],
                                    ALU.add).then_inc(a_rope, 1)

        def a0_vector_step(dve, st):
            before = st.near(-1)

            def minima(k):
                _, s = st.inst(k)
                if k == 0:
                    dve.wait_ge(a_scores, st.number() + 1)
                    dve.sem_inc(passed, 1)
                nc.vector.tensor_tensor_reduce(s0[:, s, 0:P], score_columns(k, 0), table[:, T_M0:T_M0 + P],
                                               1.0, 3e38, ALU.add, ALU.min, neg_max[:, s, 0:1])
                nc.vector.tensor_tensor_reduce(s0[:, s, P:3 * P], score_columns(k, 1),
                                               table[:, T_M0 + P:T_M0 + 3 * P],
                                               1.0, 3e38, ALU.add, ALU.min,
                                               neg_max[:, s, 1:2]).then_inc(a_min, 1)

            def inverses(k):
                n, s = st.inst(k)
                dve.wait_ge(a_exp, n + 1)
                nc.vector.reciprocal(inv_sum[:, s, :], row_sum[:, s, :]).then_inc(a_inv, 1)

            def result_lo(k):
                n, s = before.inst(k)
                dve.wait_ge(a_o_hi, n + 1)
                nc.vector.tensor_tensor(oT0[LO][:, s, :], bank[OB][:, 0:SEQ], oT0[HI][:, s, :].bitcast(F32),
                                        ALU.subtract).then_inc(a_o_lo, 1)

            turn_of = None if st.last_group else st.g
            if before.queries:
                a0_rotate(dve, before, "q")
            if st.heads:
                minima(0)
                minima(1)
            if st.key:
                a0_cosine(dve, st, "k")
            if st.heads:
                inverses(0)
                inverses(1)
            t = next_norm(st)
            if t is not None:
                dve.wait_ge(a_added, 1 + (KVH - 1) * TILES + t + 1)
                ln_moments(dve, 16 + t, t % 2, x[:, t, :])
            if st.key:
                a0_rotate(dve, st, "k")
            if lagging(st):
                result_lo(0)
            for stream, j, dst in step_splits(st, False):
                stream.split_lo(dve, j, dst, turn_of)
            if st.queries:
                a0_cosine(dve, st, "q")
            if lagging(st):
                result_lo(1)
            if st.h == 1 and not st.second:
                done = st.near(-2)
                for tt in range(2):
                    xt = x[:, 2 * (done.batch % BATCH) + tt, :]
                    dve.wait_ge(a_out, done.added + tt)
                    nc.vector.tensor_tensor(xt, xt, bank[OUTB[tt]][:, :], ALU.add).then_inc(a_added, 1)
            if st.h == 0 and st.heads:
                for i in range(4):
                    tt, half = divmod(i, 2)
                    f, fs = st.fill(i)
                    dve.wait_ge(a_proj, f + 1)
                    nc.vector.tensor_copy(lvv[:, tt, half * HALF:(half + 1) * HALF],
                                          bank[fs][:, 0:HALF]).then_inc(a_proj_free, 1)
            for stream, j, dst in step_splits(st, True):
                stream.split_lo(dve, j, dst, turn_of)
            if t is not None:
                if t == 0:
                    dve.wait_ge(a_rope_lo, st.near(-1).rope("q")[0] + 3)
                ln_apply(dve, 16 + t, t % 2, x[:, t, :])
                ln_lo_part(dve, 16 + t, t % 2, xn_tile(t))

        def a0_gpsimd(pool):
            for t in (4, 5):
                ln_power(pool, 8 + t, t % 2)
            pool.wait_ge(table_rest, 16)
            a0_sine(pool, Step(0, -2), "k")
            a0_sine(pool, Step(0, -2), "q")
            for t in (6, 7):
                ln_power(pool, 8 + t, t % 2)
            a0_rope_lo(pool, Step(0, -2), "k")
            a0_rope_lo(pool, Step(0, -2), "q")
            a0_sine(pool, Step(0, -1), "q")
            a0_run(pool, lambda st: a0_gpsimd_step(pool, st), lambda: None)

        def a0_sine(pool, st, what):
            n, s = st.rope(what)
            cols = st.columns(what)
            pool.wait_ge(a_swapped, n + 1)
            nc.gpsimd.tensor_tensor(work[:, s, cols], work[:, s, cols],
                                    table[:, T_SIN + cols.start:T_SIN + cols.stop],
                                    ALU.mult).then_inc(a_sin, 1)

        def a0_rope_lo(pool, st, what):
            n, s = st.rope(what)
            pool.wait_ge(a_rope_hi, n + 1)
            hi, lo = st.target(what)
            nc.gpsimd.tensor_tensor(lo, work[:, 2 + s, st.columns(what)], hi.bitcast(F32),
                                    ALU.subtract).then_inc(a_rope_lo, 1)

        def a0_gpsimd_step(pool, st):
            if st.near(-1).queries:
                a0_rope_lo(pool, st.near(-1), "q")
            if st.key:
                a0_sine(pool, st, "k")
            for k in range(2 if st.heads else 0):
                n, s = st.inst(k)
                pool.wait_ge(a_inv, n + 1)
                nc.gpsimd.tensor_tensor(s0[:, s, 0:P], s0[:, s, 0:P],
                                        inv_sum[:, s, 0:1].to_broadcast([P, P]), ALU.mult)
                nc.gpsimd.tensor_tensor(s0[:, s, P:3 * P], s0[:, s, P:3 * P],
                                        inv_sum[:, s, 1:2].to_broadcast([P, 2 * P]),
                                        ALU.mult).then_inc(a_norm, 1)
            if st.key:
                a0_rope_lo(pool, st, "k")
            if st.queries:
                a0_sine(pool, st, "q")
            if next_norm(st) is not None:
                ln_power(pool, 16 + next_norm(st), next_norm(st) % 2)

        b_proj = sem("b_proj")
        b_proj_free = sem("b_proj_free")
        b_sin = sem("b_sin")
        b_cos = sem("b_cos")
        b_rope = sem("b_rope")
        b_q = sem("b_q")
        b_v = sem("b_v")
        b_scores = sem("b_scores")
        b_min = sem("b_min")
        b_exp = sem("b_exp")
        b_inv = sem("b_inv")
        b_norm = sem("b_norm")
        b_turned = sem("b_turned")
        b_pt = sem("b_pt")
        b_pv = sem("b_pv")
        b_o_hi = sem("b_o_hi")
        b_o_lo = sem("b_o_lo")
        b_out = sem("b_out")
        b_added = sem("b_added")
        b_zero = sem("b_zero")
        LN1 = 32
        TURN_LAG, WEIGH_LAG = 3, 4
        OVER = WEIGH_LAG + 1
        PROJ = [(0, 0), (1, 0), (0, 1), (1, 1), (2, 0), (2, 1)]
        PROJ_AT = {19 + 2 * i: p for i, p in enumerate(PROJ)}
        FILLS1 = GR1 + len(PROJ)
        LN_AT, LAST_LN_AT = {5: 0, 12: 1}, {5: 0, 11: 1, 17: 2, 24: 3}
        LAST_SPLIT_AT = {OVER + i * 28 // F1_CHUNKS: i for i in range(F1_CHUNKS)}
        NEXT_AT = 28
        OUTPUTS_AT = {34: [0, 1], 35: [2], 36: [3]}

        def prep_at(j):
            return j // HG1 + 1 if j % HG1 == 0 and j // HG1 % GR1 < GR1 - 1 else None

        def ended_before(j):
            i = j - 1 - WEIGH_LAG
            return i // HG1 if i > 0 and i % HG1 == HG1 - 1 else None

        def fill_of(b, what):
            if isinstance(what, int):
                i = what // GR1 * FILLS1 + what % GR1 - 1
            else:
                i = GR1 - 1 + FILL_ORDER.index(what)
            n = FILLS1 - 3 + i
            return b * FILLS1 + n, n % 2

        NEXT = "next"
        FILL_ORDER = PROJ[:5] + [NEXT] + PROJ[5:]

        def b_run(eng, step, ahead):
            ahead(-1)
            for j in range(OVER):
                step(0, j, True)
            with eng.Fori(0, BATCH - 1) as b:
                for j in range(OVER, HEADS1 + OVER):
                    step(b, j, True)
            for j in range(OVER, HEADS1 + OVER):
                step(BATCH - 1, j, False)

        def there(i, more):
            return 0 <= i and (i < HEADS1 or more)

        def ln_no(b, tt):
            return b * 2 + (LN1 + 2 + tt)

        def b_tensor(pe):
            pe.wait_ge(f_mul, ffn1b.m0)
            st_a1.ready(pe, A1_CHUNKS - 1)
            b_run(pe, lambda b, j, more: b_tensor_step(pe, b, j, more),
                  lambda b: b_tensor_ahead(pe, b))

        def b_claim(pe, b, what):
            n, s = fill_of(b, what)
            pe.wait_ge(b_proj_free, n + 1)
            return bank[s]

        def tile_at(j, more):
            return (LN_AT if more else LAST_LN_AT).get(j)

        def b_tensor_norm(pe, b, tt):
            pe.wait_ge(b_added, b * 4 + 1)
            ln_turn(pe, ln_no(b, tt), tt % 2, OUTB[tt % 2])

        def b_tensor_project(pe, b, what):
            j, tt = what
            if what == PROJ[0]:
                pe.wait_ge(ln_done, ln_no(b, 1) + 1)
            dst = b_claim(pe, b, what)
            for c in range(KC):
                w = c * 3 * DIM + j * DIM
                last = product(dst[:, :], lambda p: xn(p, c, slice(tt * P, (tt + 1) * P)),
                               lambda p: W[p][:, w:w + DIM], c == 0, c == KC - 1)
            last.then_inc(b_proj, 1)

        def b_tensor_prepare(pe, b, what):
            grp = 0 if what == NEXT else what
            if what == NEXT:
                pe.wait_ge(b_rope, b * 4 + 8)
            dst = b_claim(pe, b, what)
            for j in range(2):
                for tt in range(2):
                    c = j * DIM + grp % GR1 * P
                    last = nc.tensor.transpose(dst[:, j * SEQ + tt * P:j * SEQ + (tt + 1) * P],
                                               qkv[:, tt, c:c + P], ident)
            last.then_inc(b_proj, 1)

        def b_tensor_ahead(pe, b):
            for what in FILL_ORDER:
                if what == NEXT:
                    b_tensor_prepare(pe, b, NEXT)
                else:
                    b_tensor_project(pe, b, what)

        def b_tensor_step(pe, b, j, more):
            def scores(i):
                grp, hh = divmod(i, HG1)
                s = grp % 2
                if hh == 0:
                    n = fill_of(b + grp // GR1 - 1, NEXT) if grp % GR1 == 0 else fill_of(b, grp)
                    pe.wait_ge(b_proj_free, n[0] + 3)
                    pe.wait_ge(b_q, b * GR1 + grp + 1)
                pe.wait_ge(b_min, b * HEADS1 + i + 1)
                for qt, n in enumerate((P, 2 * P)):
                    last = nc.tensor.matmul(bank[2 + i % 2][:, qt * P:qt * P + n],
                                            qz[:, s, hh, qt * P:(qt + 1) * P],
                                            qkT[:, s, SEQ:SEQ + n], start=True, stop=True)
                last.then_inc(b_scores, 1)

            def turn(i):
                pe.wait_ge(b_norm, b * HEADS1 + i + 1)
                pe.wait_ge(b_pt, b * HEADS1 + i + 1)
                for blk in range(3):
                    last = nc.tensor.transpose(bank[PT][:, blk * P:(blk + 1) * P],
                                               s1[:, i % 4, blk * P:(blk + 1) * P], ident)
                last.then_inc(b_turned, 1)

            def weigh(i):
                grp, hh = divmod(i, HG1)
                if hh == 0:
                    pe.wait_ge(b_v, b * GR1 + grp + 1)
                    pe.wait_ge(b_o_lo, b * GR1 + grp + 1)
                pe.wait_ge(b_pt, b * HEADS1 + i + 2)
                nc.tensor.matmul(bank[OB][:, 0:SEQ], vz[:, grp % 2, 0, hh, :], pt1[:, i % 2, 0:2 * P],
                                 start=hh == 0, stop=False)
                last = nc.tensor.matmul(bank[OB][:, P:SEQ], vz[:, grp % 2, 1, hh, :],
                                        pt1[:, i % 2, 2 * P:3 * P], start=False, stop=hh == HG1 - 1)
                if hh == HG1 - 1:
                    last.then_inc(b_pv, 1)

            def outputs(grp):
                if grp == 0:
                    pe.wait_ge(ln_done, ln_no(b, 1 if more else 3) + 1)
                    pe.wait_ge(b_added, b * 4 + 1)
                pe.wait_ge(b_o_lo, b * GR1 + grp + 2)
                w = (KC * 3 + grp) * CH
                for tt in range(2):
                    last = product(bank[OUTB[tt]][:, :], lambda p: oT1[p][:, grp, tt * P:(tt + 1) * P],
                                   lambda p: W[p][:, w:w + CH], grp == 0, grp == GR1 - 1)
                    if grp == GR1 - 1:
                        last.then_inc(b_out, 1)

            if there(j - TURN_LAG, more):
                turn(j - TURN_LAG)
            if there(j, more):
                scores(j)
            if there(j - WEIGH_LAG, more):
                weigh(j - WEIGH_LAG)
            if prep_at(j) and there(j, more):
                b_tensor_prepare(pe, b, prep_at(j))
            if tile_at(j - 2, more) is not None:
                b_tensor_norm(pe, b, tile_at(j - 2, more))
            if more and j in PROJ_AT:
                b_tensor_project(pe, b, PROJ_AT[j])
            if more and j == NEXT_AT:
                b_tensor_prepare(pe, b, NEXT)
            for grp in OUTPUTS_AT.get(j, []):
                outputs(grp)

        def b_scalar(act):
            act.wait_ge(x_written, X4)
            b_run(act, lambda b, j, more: b_scalar_step(act, b, j, more),
                  lambda b: b_scalar_ahead(act, b))

        def diagonal(s, tt):
            flat = vz[:, s, tt, :, :].rearrange("p h (a d) -> p (h a) d", d=D1)
            return flat[:, 0::HG1 + 1, :]

        def b_scalar_queries(act, b, what, heads):
            grp = 0 if what == NEXT else what
            if heads[0] == 0:
                act.wait_ge(b_proj_free, fill_of(b, what)[0] + 3)
            for hh in heads:
                last = nc.scalar.activation(qz[:, grp % 2, hh, :], qkT[:, grp % 2, 0:SEQ], ACT.Copy,
                                            scale=table[:, T_HEAD + hh:T_HEAD + hh + 1])
            if heads[-1] == HG1 - 1:
                last.then_inc(b_q, 1)

        def b_scalar_values(act, b, what):
            grp = 0 if what == NEXT else what
            if what == NEXT:
                act.wait_ge(b_proj_free, fill_of(b, PROJ[-1])[0] + 3)
            for tt in range(2):
                c = 2 * DIM + grp % GR1 * P
                last = nc.scalar.copy(diagonal(grp % 2, tt),
                                      qkv[:, tt, c:c + P].rearrange("p (h d) -> p h d", d=D1))
            last.then_inc(b_v, 1)

        def b_scalar_ahead(act, b):
            b_scalar_queries(act, b, NEXT, range(HG1))
            act.wait_ge(b_zero, 2)
            b_scalar_values(act, b, NEXT)

        def b_scalar_step(act, b, j, more):
            def exponentials(i):
                s = i % 4
                act.wait_ge(b_min, b * HEADS1 + i + 3)
                for qt, cols in ((0, slice(0, P)), (1, slice(P, 3 * P))):
                    last = nc.scalar.activation(s1[:, s, cols], s1[:, s, cols], ACT.Exp,
                                                bias=neg_max[:, s, qt:qt + 1], scale=-1.0,
                                                accum_out=row_sum[:, s, qt:qt + 1])
                last.then_inc(b_exp, 1)

            def result_hi(grp):
                act.wait_ge(b_pv, b * GR1 + grp + 1)
                nc.scalar.copy(oT1[HI][:, grp, :], bank[OB][:, 0:SEQ]).then_inc(b_o_hi, 1)

            if j % HG1 and there(j, more) and prep_at(j - j % HG1):
                b_scalar_queries(act, b, prep_at(j - j % HG1), (0, 1) if j % HG1 == 1 else (j % HG1,))
            if ended_before(j) is not None:
                result_hi(ended_before(j))
            if j >= 4 and there(j, more) and prep_at(j - 4):
                b_scalar_values(act, b, prep_at(j - 4))
            if there(j, more):
                exponentials(j)
            if tile_at(j - 3, more) is not None:
                tt = tile_at(j - 3, more)
                ln_hi_part(act, ln_no(b, tt), OUTB[tt % 2], xn_tile(tt))
            if not more and j in LAST_SPLIT_AT:
                i = LAST_SPLIT_AT[j]
                st_f1b.split_hi(act, i, chunk(W, i))
            if more and 0 <= j - NEXT_AT - 1 < 3:
                i = j - NEXT_AT - 1
                b_scalar_queries(act, b, NEXT, range(3 * i, min(3 * i + 3, HG1)))
            if more and j == NEXT_AT + 3:
                b_scalar_values(act, b, NEXT)

        def tile_of(b, tt):
            if isinstance(b, int):
                return x[:, 2 * b + tt, :]
            return x[:, bass.ds(b * 2 + tt, 1), :].rearrange("p a n -> p (a n)")

        def b_vector(dve):
            for s, n in ((b_proj_free, 2), (b_min, 2), (b_pt, 1), (b_o_lo, 1), (b_added, 1)):
                dve.sem_inc(s, n)
            dve.wait_ge(x_written, X4)
            dve.wait_ge(bqkv_loaded, 16)
            dve.wait_ge(row_loaded, 16 * 4)
            b_run(dve, lambda b, j, more: b_vector_step(dve, b, j, more),
                  lambda b: b_vector_ahead(dve, b))
            dve.wait_ge(b_added, 1 + 2 * TILES)
            dve.sem_inc(x_written, 1)

        def per_head(ap):
            return ap.rearrange("p (h d) -> p h d", d=D1)

        def angles(kind, tt):
            c = T_R1 + (kind * 2 + tt) * D1
            return table[:, c:c + D1].unsqueeze(1).to_broadcast([P, HEADS1, D1])

        def b_vector_norm(dve, b, tt, part):
            if part is ln_apply:
                at_least(dve, b_rope, b * 4 + 4)
            elif isinstance(b, int):
                dve.wait_ge(b_added, tt // 2 * 4 + 5)
            part(dve, ln_no(b, tt), tt % 2, x[:, tt, :] if isinstance(b, int) else tile_of(b + 1, tt))

        def b_vector_biased(dve, b, what):
            (j, tt), (n, s) = what, fill_of(b, what)
            dve.wait_ge(b_proj, n + 1)
            if what == PROJ[0]:
                at_least(dve, b_v, b * GR1 + 4)
            cols = slice(j * DIM, (j + 1) * DIM)
            nc.vector.tensor_tensor(qkv[:, tt, cols], bank[s][:, :], bqkv[:, cols],
                                    ALU.add).then_inc(b_proj_free, 1)
            if j < 2:
                r = PROJ.index(what)
                dve.wait_ge(b_proj_free, n + 3)
                at_least(dve, b_rope, b * 4 + (r - 1 + 4))
                nc.vector.tensor_tensor(per_head(work[:, 2 + r % 2, :]), per_head(qkv[:, tt, cols]),
                                        angles(2 * j, tt), ALU.mult).then_inc(b_cos, 1)

        def b_vector_rotate(dve, b, what):
            (j, tt), r = what, PROJ.index(what)
            cols = slice(j * DIM, (j + 1) * DIM)
            dve.wait_ge(b_sin, b * 4 + (r + 5))
            dve.wait_ge(b_cos, b * 4 + (r + 5))
            nc.vector.tensor_tensor(qkv[:, tt, cols], work[:, 2 + r % 2, :], work[:, r % 2, :],
                                    ALU.add).then_inc(b_rope, 1)

        def b_vector_prepare(dve, b, what):
            n, s = fill_of(b, what)
            dve.wait_ge(b_proj, n + 1)
            nc.vector.tensor_copy(qkT[:, (0 if what == NEXT else what) % 2, :],
                                  bank[s][:, :]).then_inc(b_proj_free, 1)

        def b_vector_ahead(dve, b):
            for i, what in enumerate(FILL_ORDER):
                if what == NEXT:
                    b_vector_prepare(dve, b, NEXT)
                else:
                    b_vector_biased(dve, b, what)
                if 0 < i <= 4:
                    b_vector_rotate(dve, b, PROJ[i - 1])

        def b_vector_step(dve, b, j, more):
            def minima(i):
                s = i % 4
                dve.wait_ge(b_scores, b * HEADS1 + i + 1)
                dve.sem_inc(passed, 1)
                nc.vector.tensor_tensor_reduce(s1[:, s, 0:P], bank[2 + i % 2][:, 0:P],
                                               table[:, T_M1:T_M1 + P],
                                               1.0, 3e38, ALU.add, ALU.min, neg_max[:, s, 0:1])
                nc.vector.tensor_tensor_reduce(s1[:, s, P:3 * P], bank[2 + i % 2][:, P:3 * P],
                                               table[:, T_M1 + P:T_M1 + 3 * P],
                                               1.0, 3e38, ALU.add, ALU.min,
                                               neg_max[:, s, 1:2]).then_inc(b_min, 1)

            def inverses(i):
                dve.wait_ge(b_exp, b * HEADS1 + i + 1)
                nc.vector.reciprocal(inv_sum[:, i % 4, :], row_sum[:, i % 4, :]).then_inc(b_inv, 1)

            def turned_out(i):
                dve.wait_ge(b_turned, b * HEADS1 + i + 1)
                nc.vector.tensor_copy(pt1[:, i % 2, :], bank[PT][:, 0:3 * P]).then_inc(b_pt, 1)

            def result_lo(grp):
                dve.wait_ge(b_o_hi, b * GR1 + grp + 1)
                nc.vector.tensor_tensor(oT1[LO][:, grp, :], bank[OB][:, 0:SEQ],
                                        oT1[HI][:, grp, :].bitcast(F32),
                                        ALU.subtract).then_inc(b_o_lo, 1)

            if there(j - TURN_LAG, more):
                turned_out(j - TURN_LAG)
            if ended_before(j) is not None:
                result_lo(ended_before(j))
            if there(j, more):
                minima(j)
            if there(j - 1, more):
                inverses(j - 1)
            if prep_at(j) and there(j, more):
                b_vector_prepare(dve, b, prep_at(j))
            if tile_at(j, more) is not None:
                b_vector_norm(dve, b, tile_at(j, more), ln_moments)
            if tile_at(j - 1, more) is not None:
                b_vector_norm(dve, b, tile_at(j - 1, more), ln_apply)
            if tile_at(j - 4, more) is not None:
                tt = tile_at(j - 4, more)
                ln_lo_part(dve, ln_no(b, tt), OUTB[tt % 2], xn_tile(tt))
            if more and j - 1 in PROJ_AT:
                b_vector_biased(dve, b, PROJ_AT[j - 1])
            if more and j - 2 in PROJ_AT and PROJ_AT[j - 2][0] < 2:
                b_vector_rotate(dve, b, PROJ_AT[j - 2])
            if more and j == NEXT_AT + 1:
                b_vector_prepare(dve, b, NEXT)
            if j in (8, 9):
                tile = tile_of(b, j - 8)
                nc.vector.tensor_tensor(tile, tile, row[:, :], ALU.add).then_inc(b_added, 1)
            if j == HEADS1 + OVER - 1:
                for tt in range(2):
                    dve.wait_ge(b_added, b * 4 + tt + 2)
                    dve.wait_ge(b_out, b * 2 + tt + 1)
                    nc.vector.tensor_tensor(tile_of(b, tt), tile_of(b, tt), bank[OUTB[tt]][:, :],
                                            ALU.add).then_inc(b_added, 1)

        def b_gpsimd(pool):
            pool.wait_ge(x_written, X4)
            nc.gpsimd.memset(vz[:, 0, :, :, :], 0.0).then_inc(b_zero, 1)
            nc.gpsimd.memset(vz[:, 1, :, :, :], 0.0).then_inc(b_zero, 1)
            b_run(pool, lambda b, j, more: b_gpsimd_step(pool, b, j, more),
                  lambda b: b_gpsimd_ahead(pool, b))

        def b_sine(pool, b, what):
            (j, tt), r = what, PROJ.index(what)
            pool.wait_ge(b_proj_free, fill_of(b, what)[0] + 3)
            at_least(pool, b_rope, b * 4 + (r - 1 + 4))
            c = j * DIM
            halves = lambda ap: ap.rearrange("p (h a d) -> p h a d", a=2, d=D1 // 2)
            t = T_R1 + ((2 * j + 1) * 2 + tt) * D1
            src, dst = halves(qkv[:, tt, c:c + DIM]), halves(work[:, r % 2, :])
            for a in range(2):
                sin = table[:, t + a * (D1 // 2):t + (a + 1) * (D1 // 2)]
                last = nc.gpsimd.tensor_tensor(dst[:, :, a, :], src[:, :, 1 - a, :],
                                               sin.unsqueeze(1).to_broadcast([P, HEADS1, D1 // 2]),
                                               ALU.mult)
            last.then_inc(b_sin, 1)

        def b_gpsimd_ahead(pool, b):
            for what in PROJ[:4]:
                b_sine(pool, b, what)

        def b_gpsimd_step(pool, b, j, more):
            def normalise(i):
                s = i % 4
                pool.wait_ge(b_inv, b * HEADS1 + i + 1)
                nc.gpsimd.tensor_tensor(s1[:, s, 0:P], s1[:, s, 0:P],
                                        inv_sum[:, s, 0:1].to_broadcast([P, P]), ALU.mult)
                nc.gpsimd.tensor_tensor(s1[:, s, P:3 * P], s1[:, s, P:3 * P],
                                        inv_sum[:, s, 1:2].to_broadcast([P, 2 * P]),
                                        ALU.mult).then_inc(b_norm, 1)

            if there(j - 1, more):
                normalise(j - 1)
            if not more and j in LAST_SPLIT_AT:
                i = LAST_SPLIT_AT[j]
                st_f1b.split_lo_pool(pool, i, chunk(W, i))
            if tile_at(j, more) is not None:
                ln_power(pool, ln_no(b, tile_at(j, more)), tile_at(j, more) % 2)
            if more and j - 1 in PROJ_AT and PROJ_AT[j - 1][0] < 2:
                b_sine(pool, b, PROJ_AT[j - 1])

        block = ctx.enter_context(nc.Block())

        @block.sync
        def _(sp):
            def flat(n):
                return w_in[n, :, :]

            xr = x_in.rearrange("(t p) d -> t p d", p=P)
            sp.dma_start(x[:, 0, :], xr[0]).then_inc(x_loaded[0], 16)
            sp.dma_start(table[:, 0:T_FIRST], table_in[:, 0:T_FIRST]).then_inc(table_loaded, 16)
            sp.dma_start(biases[:, :], bias_in).then_inc(table_loaded, 16)
            for t in range(1, 4):
                sp.dma_start(x[:, t, :], xr[t]).then_inc(x_loaded[t], 16)
            for j in range(F0_CHUNKS):
                st_f0a.load(sp, j, flat(W_F0A + FIRST[j]))
                if j == 3:
                    for t in range(4, TILES):
                        sp.dma_start(x[:, t, :], xr[t]).then_inc(x_loaded[t], 16)
                    sp.dma_start(row[:, :], rows_in[0]).then_inc(row_loaded, 16)
            sp.dma_start(table[:, T_FIRST:], table_in[:, T_FIRST:]).then_inc(table_rest, 16)
            st_lq.load(sp, 0, flat(W_LQ))
            for j in range(len(BEFORE)):
                st_a0.load(sp, j, flat(W_A0 + j))
            with sp.Fori(0, KVH - 1) as g:
                for j in range(G_CHUNKS):
                    src = w_in[bass.ds(g * G_CHUNKS + (W_A0 + len(BEFORE) + j), 1), :, :]
                    st_loop.load(sp, j, src.rearrange("a p n -> (a p) n"), g)
            for j in range(len(TAIL)):
                st_tail.load(sp, j, flat(W_F1 - len(TAIL) + j))
            sp.wait_ge(x_written, X1)
            sp.dma_start(row[:, :], rows_in[0]).then_inc(row_loaded, 16)
            for j in range(F1_CHUNKS):
                st_f1a.load(sp, j, flat(W_F1 + j))
            sp.wait_ge(x_written, X3)
            sp.dma_start(row[:, :], rows_in[1]).then_inc(row_loaded, 16)
            for j in range(A1_CHUNKS):
                st_a1.load(sp, j, flat(W_A1 + j))
            sp.wait_ge(x_written, X4)
            sp.dma_start(row[:, :], rows_in[2]).then_inc(row_loaded, 16)
            sp.dma_start(bqkv[:, :], rows_in[3:6].rearrange("a p n -> p a n")).then_inc(bqkv_loaded, 16)
            for j in range(F1_CHUNKS):
                st_f1b.load(sp, j, flat(W_F1 + j))
            sp.wait_ge(x_written, X5)
            sp.dma_start(row[:, :], rows_in[1]).then_inc(row_loaded, 16)
            outr = out.rearrange("(t p) d -> t p d", p=P)
            for t in range(TILES):
                sp.wait_ge(x_written, ffn1b.added(t))
                sp.dma_start(outr[t], x[:, t, :]).then_inc(stored, 16)
            sp.wait_ge(stored, 16 * TILES)

        @block.tensor
        def _(pe):
            pe.wait_ge(table_loaded, 32)
            ffn0a.tensor(pe)
            a0_tensor(pe)
            ffn0b.tensor(pe)
            ffn1a.tensor(pe)
            b_tensor(pe)
            ffn1b.tensor(pe)

        @block.scalar
        def _(act):
            act.wait_ge(table_loaded, 32)
            ffn0a.scalar(act)
            a0_scalar(act)
            ffn0b.scalar(act)
            ffn1a.scalar(act)
            b_scalar(act)
            ffn1b.scalar(act)

        @block.vector
        def _(dve):
            dve.wait_ge(table_loaded, 32)
            ffn0a.vector(dve)
            a0_vector(dve)
            ffn0b.vector(dve)
            ffn1a.vector(dve)
            b_vector(dve)
            ffn1b.vector(dve)

        @block.gpsimd
        def _(pool):
            pool.wait_ge(table_loaded, 32)
            ffn0a.gpsimd(pool)
            a0_gpsimd(pool)
            ffn0b.gpsimd(pool)
            ffn1a.gpsimd(pool)
            b_gpsimd(pool)
            ffn1b.gpsimd(pool)


def chunks_of(a):
    n = -(-a.shape[1] // CH) * CH
    full = np.zeros((P, n), a.dtype)
    full[:, :a.shape[1]] = a
    return full.reshape(P, n // CH, CH).transpose(1, 0, 2)


def by_rows(w):
    k = w.shape[0] // P
    return w.reshape(k, P, w.shape[1]).transpose(1, 0, 2).reshape(P, k * w.shape[1])


def lay_out_weights(a):
    f0 = chunks_of(np.concatenate([by_rows(a["L0_ffn_w12"].T), by_rows(a["L0_ffn_w3"].T)], 1))
    wq, wk, wv = a["L0_attn_w_q"], a["L0_attn_w_k"], a["L0_attn_w_v"]
    wlk, wlv, wo, wlo = a["L0_attn_w_lk"], a["L0_attn_w_lv"], a["L0_attn_w_o"], a["L0_attn_w_lo"]
    groups = []
    for g in range(KVH):
        kv = slice(g * HD, (g + 1) * HD)
        hs = slice(g * GH * HD, (g + 1) * GH * HD)
        heads = [slice((g * GH + h) * HD, (g * GH + h + 1) * HD) for h in range(GH)]
        groups.append(chunks_of(np.concatenate(
            [by_rows(wk[:, kv])] + [by_rows(wq[:, h]) for h in heads] + [wlk[:, hs]]
            + [by_rows(np.concatenate([wlv[:, hs], wv[:, kv]], 1))]
            + [by_rows(wo[hs])] + [by_rows(wlo[hs])], 1)))
    a0 = [groups[0][BEFORE]]
    for g in range(KVH - 1):
        a0 += [groups[g][TURN[:OWN]], groups[g + 1][TURN[OWN:]]]
    a0 += [groups[-1][TAIL[:OWN]], f0[TAIL[OWN:]]]
    v1, u2 = a["L1_ffn_V1"], a["L1_ffn_U2"]
    halves = []
    for up in range(2):
        part = np.zeros((P, M1 * P), v1.dtype)
        part[:, :INTER] = v1[:, up * INTER:(up + 1) * INTER]
        halves.append(part)
    u2p = np.zeros((M1 * P, u2.shape[1]), u2.dtype)
    u2p[:INTER] = u2
    f1 = chunks_of(np.concatenate([by_rows(a["L1_ffn_U1"])] + halves + [by_rows(u2p), a["L1_ffn_V2"]], 1))
    a1 = chunks_of(np.concatenate([by_rows(a["L1_attn_qkv_w"]), by_rows(a["L1_attn_out_w"])], 1))
    lq = chunks_of(by_rows(a["L0_attn_w_lq"]))
    return np.ascontiguousarray(np.concatenate([f0, lq] + a0 + [f1, a1], 0))


def lay_out_biases(a):
    b = np.zeros((P, B_ALL), np.float32)
    b[:, B_12:B_12 + 2 * M0] = a["L0_ffn_b12"].reshape(2 * M0, P).T
    for up in range(2):
        part = np.zeros(M1 * P, np.float32)
        part[:INTER] = a["L1_ffn_b1"][up * INTER:(up + 1) * INTER]
        b[:, B_1 + up * M1:B_1 + (up + 1) * M1] = part.reshape(M1, P).T
    rows = np.concatenate([a["L0_ffn_b3"], a["L1_ffn_b2"], a["L1_attn_out_b"], a["L1_attn_qkv_b"]])
    rows = np.broadcast_to(rows.reshape(6, 1, DIM), (6, P, DIM))
    return b, np.ascontiguousarray(rows)


def kernel(**inputs):
    import concourse.bacc as bacc
    from concourse.bass_utils import run_bass_kernel_spmd

    a = {k: np.ascontiguousarray(v) for k, v in inputs.items()}
    weights = lay_out_weights(a)
    biases, rows = lay_out_biases(a)
    arrays = {"x": a["L0_attn_hidden_states"].reshape(TOKENS, DIM), "weights": weights,
              "constants": constants(), "bias_columns": biases, "bias_rows": rows}
    nc = bacc.Bacc("TRN2", target_bir_lowering=False, num_devices=1)
    args = [nc.dram_tensor(f"in_{n}", v.shape, F32, kind="ExternalInput").ap() for n, v in arrays.items()]
    args.append(nc.dram_tensor("out", (TOKENS, DIM), F32, kind="ExternalOutput").ap())
    program(nc, *args)
    r = run_bass_kernel_spmd(nc, [{f"in_{n}": v for n, v in arrays.items()}], core_ids=[0])
    return r.results[0]["out"].reshape(BATCH, SEQ, DIM)
```
